# Optimizing a Trainium2 kernel written in Bass

```python
import numpy as np
import jax
import jax.numpy as jnp

def _softmax(x, axis=-1):
    return jax.nn.softmax(x, axis=axis)

def _gelu(x):
    return jax.nn.gelu(x, approximate=True)

def _silu(x):
    return jax.nn.silu(x)

def _sigmoid(x):
    return jax.nn.sigmoid(x)

def _layernorm(x, axis=-1, eps=1e-05):
    m = jnp.mean(x, axis=axis, keepdims=True)
    v = jnp.var(x, axis=axis, keepdims=True)
    return (x - m) / jnp.sqrt(v + eps)

def _scatter_add(tgt, idx, src, axis=0):
    return tgt.at[idx].add(src)

def _segment_sum(src, seg, n):
    return jax.ops.segment_sum(src, seg, n)
kernel_name = 'mk_seq_postln_d1_jaxref_r4_d56516'

def setup_inputs(seed: int=0):
    np.random.seed(seed)
    _w = jnp.asarray

    def _L0_attn_setup():
        import jax, jax.numpy as jnp
        import numpy as np
        N_HEAD = 16
        LATENT = 32

        def _rotate_half(x):
            xe = x[..., ::2]
            xo = x[..., 1::2]
            return jnp.stack((-xo, xe), axis=-1).reshape(x.shape)

        def _rope_tables(T, latent_dim, dtype):
            inv_freq = 1.0 / 10000.0 ** (jnp.arange(0, latent_dim, 2, dtype=jnp.float32) / latent_dim)
            t = jnp.arange(T, dtype=jnp.float32)
            freqs = jnp.outer(t, inv_freq)
            cos = jnp.repeat(jnp.cos(freqs), 2, axis=-1)[:, :latent_dim]
            sin = jnp.repeat(jnp.sin(freqs), 2, axis=-1)[:, :latent_dim]
            return (cos.astype(dtype), sin.astype(dtype))
        key = jax.random.key(seed)
        ks = jax.random.split(key, 14)
        C = 256
        hd = C // N_HEAD
        L = LATENT
        s = 0.02
        return {'x': jax.random.normal(ks[0], (4, 512, C), jnp.float32), 'c_attn_w': jax.random.normal(ks[1], (3 * C, C), jnp.float32) * s, 'c_attn_b': jnp.zeros((3 * C,), jnp.float32), 'q2l_w': jax.random.normal(ks[2], (L, hd), jnp.float32) * s, 'q2l_b': jnp.zeros((L,), jnp.float32), 'kv2l_w': jax.random.normal(ks[3], (L, hd), jnp.float32) * s, 'kv2l_b': jnp.zeros((L,), jnp.float32), 'l2o_w': jax.random.normal(ks[4], (hd, L), jnp.float32) * s, 'l2o_b': jnp.zeros((hd,), jnp.float32), 'wqk_w': jax.random.normal(ks[5], (L, L), jnp.float32) * s, 'wqk_b': jnp.zeros((L,), jnp.float32), 'cproj_w': jax.random.normal(ks[6], (C, C), jnp.float32) * s, 'cproj_b': jnp.zeros((C,), jnp.float32)}
    _L0_attn_in = _L0_attn_setup()

    def _L0_ffn_setup():
        import jax, jax.numpy as jnp
        import numpy as np
        B, T, C, E, K, CAP, H = (8, 512, 256, 8, 2, 1024, 1024)
        key = jax.random.key(seed)
        ks = jax.random.split(key, 6)
        s = 0.02
        return {'x': jax.random.normal(ks[0], (B, T, C), jnp.float32), 'rw1': s * jax.random.normal(ks[1], (C, H), jnp.float32), 'rb1': jnp.zeros((H,), jnp.float32), 'rw2': s * jax.random.normal(ks[2], (H, E), jnp.float32), 'rb2': jnp.zeros((E,), jnp.float32), 'ew1': s * jax.random.normal(ks[3], (E, C, H), jnp.float32), 'eb1': jnp.zeros((E, H), jnp.float32), 'ew2': s * jax.random.normal(ks[4], (E, H, C), jnp.float32), 'eb2': jnp.zeros((E, C), jnp.float32)}
    _L0_ffn_in = _L0_ffn_setup()
    _d = {'L0_attn_x': _L0_attn_in['x'], 'L0_attn_c_attn_w': _L0_attn_in['c_attn_w'], 'L0_attn_c_attn_b': _L0_attn_in['c_attn_b'], 'L0_attn_q2l_w': _L0_attn_in['q2l_w'], 'L0_attn_q2l_b': _L0_attn_in['q2l_b'], 'L0_attn_kv2l_w': _L0_attn_in['kv2l_w'], 'L0_attn_kv2l_b': _L0_attn_in['kv2l_b'], 'L0_attn_l2o_w': _L0_attn_in['l2o_w'], 'L0_attn_l2o_b': _L0_attn_in['l2o_b'], 'L0_attn_wqk_w': _L0_attn_in['wqk_w'], 'L0_attn_wqk_b': _L0_attn_in['wqk_b'], 'L0_attn_cproj_w': _L0_attn_in['cproj_w'], 'L0_attn_cproj_b': _L0_attn_in['cproj_b'], 'L0_ffn_rw1': _L0_ffn_in['rw1'], 'L0_ffn_rb1': _L0_ffn_in['rb1'], 'L0_ffn_rw2': _L0_ffn_in['rw2'], 'L0_ffn_rb2': _L0_ffn_in['rb2'], 'L0_ffn_ew1': _L0_ffn_in['ew1'], 'L0_ffn_eb1': _L0_ffn_in['eb1'], 'L0_ffn_ew2': _L0_ffn_in['ew2'], 'L0_ffn_eb2': _L0_ffn_in['eb2']}
    _x0 = _d['L0_attn_x']
    _d['L0_attn_x'] = jax.random.normal(jax.random.fold_in(jax.random.key(seed), 1), (4, 2048, 256), dtype=_x0.dtype)
    del _x0
    return _d

def reference(L0_attn_x, L0_attn_c_attn_w, L0_attn_c_attn_b, L0_attn_q2l_w, L0_attn_q2l_b, L0_attn_kv2l_w, L0_attn_kv2l_b, L0_attn_l2o_w, L0_attn_l2o_b, L0_attn_wqk_w, L0_attn_wqk_b, L0_attn_cproj_w, L0_attn_cproj_b, L0_ffn_rw1, L0_ffn_rb1, L0_ffn_rw2, L0_ffn_rb2, L0_ffn_ew1, L0_ffn_eb1, L0_ffn_ew2, L0_ffn_eb2):

    def _L0_attn_ref(x, c_attn_w, c_attn_b, q2l_w, q2l_b, kv2l_w, kv2l_b, l2o_w, l2o_b, wqk_w, wqk_b, cproj_w, cproj_b):
        import jax, jax.numpy as jnp
        import numpy as np
        N_HEAD = 16
        LATENT = 32

        def _rotate_half(x):
            xe = x[..., ::2]
            xo = x[..., 1::2]
            return jnp.stack((-xo, xe), axis=-1).reshape(x.shape)

        def _rope_tables(T, latent_dim, dtype):
            inv_freq = 1.0 / 10000.0 ** (jnp.arange(0, latent_dim, 2, dtype=jnp.float32) / latent_dim)
            t = jnp.arange(T, dtype=jnp.float32)
            freqs = jnp.outer(t, inv_freq)
            cos = jnp.repeat(jnp.cos(freqs), 2, axis=-1)[:, :latent_dim]
            sin = jnp.repeat(jnp.sin(freqs), 2, axis=-1)[:, :latent_dim]
            return (cos.astype(dtype), sin.astype(dtype))
        B, T, C = x.shape
        H = N_HEAD
        hd = C // H
        L = q2l_w.shape[0]
        qkv = x @ c_attn_w.T + c_attn_b
        q, k, v = jnp.split(qkv, 3, axis=2)

        def heads(t):
            return t.reshape(B, T, H, hd).transpose(0, 2, 1, 3)
        q, k, v = (heads(q), heads(k), heads(v))
        q_lat = q @ q2l_w.T + q2l_b
        k_lat = k @ kv2l_w.T + kv2l_b
        v_lat = v @ kv2l_w.T + kv2l_b
        cos, sin = _rope_tables(T, L, x.dtype)
        cos = cos[None, None]
        sin = sin[None, None]
        q_lat = q_lat * cos + _rotate_half(q_lat) * sin
        k_lat = k_lat * cos + _rotate_half(k_lat) * sin
        q_for_k = q_lat @ wqk_w.T + wqk_b
        att = jnp.einsum('bhql,bhkl->bhqk', q_for_k, k_lat) * L ** (-0.5)
        causal = jnp.tril(jnp.ones((T, T), dtype=bool))
        att = jnp.where(causal[None, None], att, -jnp.inf)
        att = jax.nn.softmax(att, axis=-1)
        y_lat = jnp.einsum('bhqk,bhkl->bhql', att, v_lat)
        y = y_lat @ l2o_w.T + l2o_b
        y = y.transpose(0, 2, 1, 3).reshape(B, T, C)
        return y @ cproj_w.T + cproj_b

    def _L0_ffn_ref(x, rw1, rb1, rw2, rb2, ew1, eb1, ew2, eb2):
        import jax, jax.numpy as jnp
        import numpy as np
        B, T, C, E, K, CAP, H = (8, 512, 256, 8, 2, 1024, 1024)
        Bx, Tx, Cx = x.shape
        N = Bx * Tx
        logits = jax.nn.relu(x @ rw1 + rb1) @ rw2 + rb2
        vals, ids = jax.lax.top_k(logits, K)
        probs = jax.nn.softmax(vals, axis=-1)
        ids_f = ids.reshape(N * K)
        probs_f = probs.reshape(N * K)
        xr = jnp.repeat(x.reshape(N, Cx), K, axis=0)
        m = jax.nn.one_hot(ids_f, E, dtype=jnp.int32)
        pos = jnp.cumsum(m, axis=0) - 1
        pos_tok = jnp.take_along_axis(pos, ids_f[:, None], axis=1)[:, 0]
        keep = (pos_tok < CAP).astype(x.dtype)
        pos_c = jnp.clip(pos_tok, 0, CAP - 1)
        disp = jnp.zeros((E, CAP, Cx), x.dtype).at[ids_f, pos_c].add(xr * keep[:, None])
        h = jax.nn.relu(jnp.einsum('enc,ech->enh', disp, ew1) + eb1[:, None, :])
        eo = jnp.einsum('enh,ehc->enc', h, ew2) + eb2[:, None, :]
        y = eo[ids_f, pos_c] * (probs_f * keep)[:, None]
        return y.reshape(Bx, Tx, K, Cx).sum(axis=2)
    x = L0_attn_x
    x = _layernorm(x + _L0_attn_ref(x, L0_attn_c_attn_w, L0_attn_c_attn_b, L0_attn_q2l_w, L0_attn_q2l_b, L0_attn_kv2l_w, L0_attn_kv2l_b, L0_attn_l2o_w, L0_attn_l2o_b, L0_attn_wqk_w, L0_attn_wqk_b, L0_attn_cproj_w, L0_attn_cproj_b), axis=-1)
    x = _layernorm(x + _L0_ffn_ref(x, L0_ffn_rw1, L0_ffn_rb1, L0_ffn_rw2, L0_ffn_rb2, L0_ffn_ew1, L0_ffn_eb1, L0_ffn_ew2, L0_ffn_eb2), axis=-1)
    return x

_drawn_inputs = setup_inputs


def setup_inputs(seed=0):
    import zlib

    import numpy as np

    out = dict(_drawn_inputs(seed))
    spreads = {'L0_attn_c_attn_b': (0.0, 0.8),
     'L0_attn_q2l_b': (0.0, 0.8),
     'L0_attn_kv2l_b': (0.0, 0.8),
     'L0_attn_l2o_b': (0.0, 0.1),
     'L0_attn_wqk_b': (0.0, 0.8),
     'L0_attn_cproj_b': (0.0, 0.1),
     'L0_ffn_rb1': (0.0, 0.1),
     'L0_ffn_rb2': (0.0, 0.1),
     'L0_ffn_eb1': (0.0, 0.431),
     'L0_ffn_eb2': (0.0, 0.1)}
    factors = {'L0_attn_c_attn_w': 8.0,
     'L0_attn_q2l_w': 8.0,
     'L0_attn_kv2l_w': 8.0,
     'L0_attn_l2o_w': 8.0,
     'L0_attn_wqk_w': 8.0}
    for name, (base, spread) in spreads.items():
        noise = np.random.default_rng([zlib.crc32(name.encode()), seed]).standard_normal(out[name].shape)
        drawn = base * np.exp(spread * noise) if base else spread * noise
        out[name] = jnp.asarray(drawn.astype(out[name].dtype))
    for name, factor in factors.items():
        out[name] = (out[name] * factor).astype(out[name].dtype)
    return out
```

```python
from contextlib import ExitStack

import numpy as np
import concourse.bass as bass
from concourse import mybir

F32 = mybir.dt.float32
F32R = mybir.dt.float32r
BF16 = mybir.dt.bfloat16
U32 = mybir.dt.uint32
ALU = mybir.AluOpType
ACT = mybir.ActivationFunctionType
AX = mybir.AxisListType

P = 128
B, T, C = 4, 2048, 256
N = B * T
H, HD, L = 16, 16, 32
HG = P // L
G = H // HG
CH = 512
NC = T // CH
TT = CH // P
KC = C // P
SLOTS = B * G
SCALE = float(L) ** -0.5
E, CAP, HID = 8, 1024, 1024
MC = HID // P
NEG = -1.0e30
FREE = 1


class Scope:

    def __init__(self, nc, ctx, stage):
        self.nc, self.ctx, self.stage = nc, ctx, stage

    def sb(self, name, shape, dt=F32):
        return self.ctx.enter_context(self.nc.sbuf_tensor(f"{self.stage}_{name}", shape, dt))

    def ps(self, name, shape, dt=F32):
        return self.ctx.enter_context(self.nc.psum_tensor(f"{self.stage}_{name}_bank", shape, dt))

    def sem(self, name):
        return self.ctx.enter_context(self.nc.semaphore(f"{self.stage}_{name}"))


def project_heads(nc, a, d):
    NU = 2 * G
    ITS = B * NC // 2
    with ExitStack() as ctx:
        s = Scope(nc, ctx, "proj")
        sb, ps, sem = s.sb, s.ps, s.sem
        cq = sb("cq", [64, G, C])
        ck = sb("ck", [64, G, C])
        wv = sb("wv", [P, KC, C])
        fold_q = sb("fold_q", [64, P])
        fold_k = sb("fold_k", [64, P])
        b_cq = sb("b_cq", [64, G])
        b_ck = sb("b_ck", [64, G])
        b_small = sb("b_small", [P, 3])
        b_v = sb("b_v", [P, C])
        wqk = sb("wqk", [P, P])
        rot = sb("rot", [P, 2, P])
        cos = sb("cos", [P, T])
        sin = sb("sin", [P, T])
        wq_lat = sb("wq_lat", [P, KC, G, P])
        wk_lat = sb("wk_lat", [P, KC, G, P])
        wqk_rot = sb("wqk_rot", [P, P])
        b_q = sb("b_q", [P, G])
        b_k = sb("b_k", [P, G])
        b_qk = sb("b_qk", [P, 1])
        zeros = sb("zeros", [P, CH])
        xt = sb("xt", [P, 2, KC, CH])
        q_cos = sb("q_cos", [P, 2, CH])
        q_sin = sb("q_sin", [P, 2, CH])
        k_cos = sb("k_cos", [P, 2, CH])
        k_sin = sb("k_sin", [P, 2, CH])
        q_full = sb("q_full", [P, 2, CH])
        k_full = sb("k_full", [P, 2, CH])
        parts = sb("parts", [P, 2, 4, CH], F32R)
        v_tok = sb("v_tok", [P, 2, TT, H, L])
        lat = [[ps(f"lat{i}{x}", [P, CH]) for x in "qk"] for i in range(2)]
        fin_q = ps("fin_q", [P, CH])
        fin_k = ps("fin_k", [P, CH])
        v_ps = [ps(f"v{i}", [P, 2, C]) for i in range(2)]

        consts_in = sem("consts_in")
        filled = sem("filled")
        folded = sem("folded")
        weights_ready = sem("weights_ready")
        zeros_out = sem("zeros_out")
        xt_in = [sem(f"xt_in{i}") for i in range(2)]
        lat_ready = sem("lat_ready")
        roped = sem("roped")
        fin_q_ready = sem("fin_q_ready")
        fin_k_ready = sem("fin_k_ready")
        q_done = sem("q_done")
        k_full_done = sem("k_full_done")
        k_high_done = sem("k_high_done")
        parts_done = sem("parts_done")
        parts_out = [sem(f"parts_out{i}") for i in range(2)]
        v_ready = sem("v_ready")
        v_copied = sem("v_copied")
        v_out = [sem(f"v_out{i}") for i in range(2)]
        for free in (q_done, k_full_done, v_copied, *parts_out, parts_done, k_high_done, fin_q_ready, fin_k_ready, *v_out):
            nc.sync.sem_inc(free, FREE)
        block = ctx.enter_context(nc.Block())

        loads = [
            (cq[:], a["c_attn_w"][0:C].rearrange("(g r) c -> r g c", r=64)),
            (ck[:], a["c_attn_w"][C:2 * C].rearrange("(g r) c -> r g c", r=64)),
            (wv[:], a["wv_t"].rearrange("(k p) n -> p k n", p=P)),
            (fold_q[:], a["fold_q"]), (fold_k[:], a["fold_k"]),
            (b_cq[:], a["b_cq"]), (b_ck[:], a["b_ck"]), (b_small[:], a["b_small"]), (b_v[:], a["b_v"]),
            (wqk[:], a["wqk_t"]), (rot[:], a["rot"].rearrange("m p n -> p m n")),
            (cos[:], a["cos"]), (sin[:], a["sin"]),
        ]
        xt_src = a["x_t"].rearrange("(k p) (i n) -> i p k n", p=P, n=CH)

        @block.gpsimd
        def _(pool):
            for sub in range(2):
                pool.dma_start(xt[:, sub], xt_src[sub]).then_inc(xt_in[sub], 16)
            with pool.Fori(0, ITS - 1) as i:
                for sub in range(2):
                    nxt = pool.snap(i * 2 + (2 + sub))
                    pool.wait_ge(v_ready, i * 4 + 2 * (sub + 1))
                    pool.dma_start(xt[:, sub], xt_src[nxt]).then_inc(xt_in[sub], 16)

        @block.sync
        def _(sp):
            for dst, src in loads:
                sp.dma_start(dst, src).then_inc(consts_in, 16)
            sp.wait_ge(filled, 1)
            for c in range(NC):
                for f in range(4):
                    sp.dma_start(d["qk"][SLOTS, c, f], zeros[:]).then_inc(zeros_out, 16)
                sp.dma_start(d["v"][SLOTS, c].rearrange("p t n -> p (t n)"), zeros[:]).then_inc(zeros_out, 16)
            with sp.Fori(0, B) as b:
                with sp.Fori(0, NC // 2) as cp:
                    it = sp.snap(b * (NC // 2) + cp)
                    slot = [sp.snap(b * G + g) for g in range(G)]
                    chunk = [sp.snap(cp * 2 + sub) for sub in range(2)]
                    for sub in range(2):
                        for g in range(G):
                            u = sub * G + g
                            sp.wait_ge(parts_done, it * NU + (u + 1 + FREE))
                            sp.dma_start(d["qk"][slot[g], chunk[sub]].rearrange("f p n -> p f n"),
                                         parts[:, u % 2].bitcast(F32)).then_inc(parts_out[u % 2], 16)
                        sp.wait_ge(v_copied, it * 4 + (2 * (sub + 1) + FREE))
                        for g in range(G):
                            sp.dma_start(d["v"][slot[g], chunk[sub]],
                                         v_tok[:, sub, :, g * HG:(g + 1) * HG, :].rearrange("p t j l -> p t (j l)"),
                                         ).then_inc(v_out[sub], 16)
            sp.wait_ge(zeros_out, 16 * 5 * NC)
            for i in range(2):
                sp.wait_ge(parts_out[i], 16 * ITS * NU // 2 + FREE)
                sp.wait_ge(v_out[i], 16 * G * ITS + FREE)

        @block.tensor
        def _(pe):
            pe.wait_ge(consts_in, 16 * len(loads))
            for k in range(KC):
                for x, (c_w, fold) in enumerate(((cq, fold_q), (ck, fold_k))):
                    for g in range(G):
                        last = nc.tensor.matmul(lat[x][k][:, g * P:(g + 1) * P], c_w[:, g, k * P:(k + 1) * P],
                                                fold[:], start=True, stop=True)
            last.then_inc(folded, 1)
            nc.tensor.matmul(fin_q[:, 0:G], fold_q[:], b_cq[:], start=True, stop=True)
            nc.tensor.matmul(fin_q[:, G:2 * G], fold_k[:], b_ck[:], start=True, stop=True)
            nc.tensor.matmul(fin_k[:, 0:P], rot[:, 0], wqk[:], start=True, stop=True).then_inc(folded, 1)
            pe.wait_ge(weights_ready, 8)

            def finish(it, u):
                par = u % 2
                pe.wait_ge(roped, it * (2 * NU) + (2 * u + 1))
                pe.wait_ge(q_done, it * NU + (u + FREE))
                nc.tensor.matmul(fin_q[:], wqk[:], q_cos[:, par], start=True, stop=False)
                nc.tensor.matmul(fin_q[:], wqk_rot[:], q_sin[:, par], start=False, stop=True).then_inc(fin_q_ready, 1)
                pe.wait_ge(roped, it * (2 * NU) + (2 * u + 2))
                pe.wait_ge(k_full_done, it * NU + (u + FREE))
                nc.tensor.matmul(fin_k[:], rot[:, 1], k_sin[:, par], start=True, stop=True).then_inc(fin_k_ready, 1)

            with pe.Fori(0, ITS) as it:
                for u in range(NU):
                    sub, g, par = u // G, u % G, u % 2
                    if g == 0:
                        pe.wait_ge(xt_in[sub], it * 16 + 16)
                    if u >= 2:
                        pe.wait_ge(roped, it * (2 * NU) + 2 * (u - 1))
                    for x, w in enumerate((wq_lat, wk_lat)):
                        for k in range(KC):
                            last = nc.tensor.matmul(lat[par][x][:], w[:, k, g, :], xt[:, sub, k, :],
                                                    start=(k == 0), stop=(k == KC - 1))
                        last.then_inc(lat_ready, 1)
                    if u > 0:
                        finish(it, u - 1)
                    if g == G - 1:
                        for pair in range(2):
                            vi = 2 * sub + pair
                            pe.wait_ge(v_copied, it * 4 + (max(vi - 1, 0) + FREE))
                            for t in range(2):
                                for k in range(KC):
                                    last = nc.tensor.matmul(
                                        v_ps[pair][:, t, :], xt[:, sub, k, (2 * pair + t) * P:(2 * pair + t + 1) * P],
                                        wv[:, k, :], start=(k == 0), stop=(k == KC - 1))
                            last.then_inc(v_ready, 1)
                finish(it, NU - 1)

        @block.scalar
        def _(act):
            act.wait_ge(consts_in, 16 * len(loads))
            nc.scalar.mul(b_qk[:], b_small[:, 2:3], SCALE).then_inc(weights_ready, 1)
            act.wait_ge(weights_ready, 8)
            with act.Fori(0, ITS) as it:
                for u in range(NU):
                    par = u % 2
                    act.wait_ge(fin_q_ready, it * NU + (u + 1 + FREE))
                    act.wait_ge(parts_out[par], it * (8 * NU) + (16 * (u // 2) + FREE))
                    act.wait_ge(parts_done, it * NU + (max(u - 1, 0) + FREE))
                    nc.scalar.activation(q_full[:, par], fin_q[:], ACT.Identity, bias=b_qk[:], scale=SCALE)
                    nc.scalar.activation(parts[:, par, 0], fin_q[:], ACT.Identity, bias=b_qk[:],
                                         scale=SCALE).then_inc(q_done, 1)
                    act.wait_ge(k_full_done, it * NU + (u + 1 + FREE))
                    nc.scalar.activation(parts[:, par, 2], k_full[:, par], ACT.Copy).then_inc(k_high_done, 1)

        @block.vector
        def _(dve):
            nc.vector.memset(zeros[:], 0.0).then_inc(filled, 1)
            nc.vector.memset(v_tok[:], 0.0).then_inc(filled, 1)
            dve.wait_ge(filled, 2)
            nc.vector.memset(v_tok[:, :, :, :, HD:HD + 1], 1.0).then_inc(filled, 1)
            dve.wait_ge(folded, 1)
            for k in range(KC):
                for x, w in enumerate((wq_lat, wk_lat)):
                    nc.vector.tensor_copy(w[:, k].rearrange("p g n -> p (g n)"), lat[x][k][:]).then_inc(weights_ready, 1)
            dve.wait_ge(folded, 2)
            nc.vector.tensor_copy(wqk_rot[:], fin_k[:, 0:P]).then_inc(weights_ready, 1)
            dve.wait_ge(consts_in, 16 * len(loads))
            nc.vector.tensor_scalar(b_q[:], fin_q[:, 0:G], b_small[:, 0:1], None, ALU.add).then_inc(weights_ready, 1)
            nc.vector.tensor_scalar(b_k[:], fin_q[:, G:2 * G], b_small[:, 1:2], None, ALU.add).then_inc(weights_ready, 1)
            dve.wait_ge(weights_ready, 8)

            def finish(it, u):
                par = u % 2
                dve.wait_ge(fin_k_ready, it * NU + (u + 1 + FREE))
                dve.wait_ge(k_high_done, it * NU + (max(u - 1, 0) + FREE))
                nc.vector.tensor_tensor(k_full[:, par], fin_k[:], k_cos[:, par], ALU.add).then_inc(k_full_done, 1)
                dve.wait_ge(q_done, it * NU + (u + 1 + FREE))
                nc.vector.tensor_tensor(parts[:, par, 1], q_full[:, par], parts[:, par, 0].bitcast(F32), ALU.subtract)
                dve.wait_ge(k_high_done, it * NU + (u + 1 + FREE))
                nc.vector.tensor_tensor(parts[:, par, 3], k_full[:, par], parts[:, par, 2].bitcast(F32),
                                        ALU.subtract).then_inc(parts_done, 1)

            with dve.Fori(0, B) as b:
                with dve.Fori(0, NC // 2) as cp:
                    it = b * (NC // 2) + cp
                    for u in range(NU):
                        sub, g, par = u // G, u % G, u % 2
                        at = bass.ds(cp * (2 * CH) + sub * CH, CH)
                        for x, (bias, w_cos, w_sin) in enumerate(((b_q, q_cos, q_sin), (b_k, k_cos, k_sin))):
                            dve.wait_ge(lat_ready, it * (2 * NU) + (2 * u + x + 1))
                            dve.wait_ge((fin_q_ready, fin_k_ready)[x], it * NU + (max(u - 1, 0) + FREE))
                            nc.vector.scalar_tensor_tensor(w_cos[:, par], lat[par][x][:], bias[:, g:g + 1],
                                                           cos[:, at], ALU.add, ALU.mult)
                            nc.vector.scalar_tensor_tensor(w_sin[:, par], lat[par][x][:], bias[:, g:g + 1],
                                                           sin[:, at], ALU.add, ALU.mult).then_inc(roped, 1)
                        if u > 0:
                            finish(it, u - 1)
                        if g == G - 1:
                            for pair in range(2):
                                dve.wait_ge(v_ready, it * 4 + (2 * sub + pair + 1))
                                dve.wait_ge(v_out[sub], it * (16 * G) + FREE)
                                for t in range(2):
                                    last = nc.vector.tensor_tensor(
                                        v_tok[:, sub, 2 * pair + t, :, 0:HD],
                                        v_ps[pair][:, t, :].rearrange("p (h e) -> p h e", e=HD),
                                        b_v[:].rearrange("p (h e) -> p h e", e=HD), ALU.add)
                                last.then_inc(v_copied, 1)
                    finish(it, NU - 1)


KS = [(p, c, kt) for p in range(2) for c in range(NC) for kt in range(TT * (c + 1))]
KSG = len(KS) // 2
MU = [(c, j, t, kb) for c in range(NC) for j in range(HG) for t in range(TT) for kb in range(c + 1)]
MUG = len(MU)
PER_STEP = MUG // KSG
LEAD = 5 * HG * TT
CHUNK_END = [TT * (c + 1) * (c + 2) // 2 for c in range(NC)]
MU_END = [HG * TT * (c + 1) * (c + 2) // 2 for c in range(NC)]


def maxima_ending(k):
    done = LEAD + PER_STEP * (k + 1)
    group, rest = divmod(done, MUG)
    if rest == 0:
        return NC * group - 1
    return NC * group + MU_END.index(rest) if rest in MU_END else None


def attend(nc, a, d):
    ITS = SLOTS // 2
    NK = len(KS)
    with ExitStack() as ctx:
        s = Scope(nc, ctx, "att")
        sb, ps, sem = s.sb, s.ps, s.sem
        q_st = sb("q_st", [98, NC, HG, CH], F32R)
        k_st = sb("k_st", [98, 2, NC, HG, CH], F32R)
        v_st = sb("v_st", [P, 2, NC, TT, HG * L])
        probs = sb("probs", [P, 4, HG, CH])
        mask_f = sb("mask_f", [P, P])
        mask = sb("mask", [P, P], BF16)
        ident_b = sb("ident_b", [P, P], BF16)
        ident = sb("ident", [P, P])
        pick = sb("pick", [P, P])
        partial_max = sb("partial_max", [P, 2, HG * TT, NC])
        neg_max = sb("neg_max", [P, 2, HG * TT])
        max_high = sb("max_high", [HG * TT, 2, P], F32R)
        max_low = sb("max_low", [HG * TT, 2, P], F32R)
        y_raw = sb("y_raw", [P, 2, CH])
        recip = sb("recip", [P, CH])
        y = sb("y", [P, 2, CH])
        score_ps = [ps(f"score{i}", [P, 2, CH]) for i in range(2)]
        max_ps = [ps(f"max{i}", [P, CH]) for i in range(2)]
        acc = ps("acc", [P, CH])
        misc = ps("misc", [P, CH])

        consts_in = sem("consts_in")
        ones_set = sem("ones_set")
        loaded = [sem(f"loaded{c}") for c in range(NC)]
        unit_scored = sem("unit_scored")
        unit_reduced = sem("unit_reduced")
        max_combined = sem("max_combined")
        misc_ready = sem("misc_ready")
        max_split = sem("max_split")
        high_done = sem("high_done")
        shift_in = [sem(f"shift_in{i}") for i in range(2)]
        scored = sem("scored")
        exped = sem("exped")
        masked = sem("masked")
        edge_due = sem("edge_due")
        weighted = sem("weighted")
        acc_read = sem("acc_read")
        recip_done = sem("recip_done")
        y_done = sem("y_done")
        y_out = [sem(f"y_out{i}") for i in range(2)]
        for free in (y_done, recip_done, max_split, *y_out):
            nc.sync.sem_inc(free, FREE)
        block = ctx.enter_context(nc.Block())

        loads = [(mask_f[:], a["mask"]), (ident[:], a["ident"]), (pick[:], a["pick"])]
        qk_src = d["qk"].rearrange("s c f (j p) n -> s c f p j n", p=L)
        MISC_BODY = 2 * NC * 2
        MISC_HEAD = 2

        def misc_uses():
            out = []
            for k in range(NK):
                if k and maxima_ending(k - 1) is not None:
                    out.append(("max", maxima_ending(k - 1)))
                n = sums_at(k)
                if n is not None:
                    out.append(("sum", n))
            if maxima_ending(NK - 1) is not None:
                out.append(("max", maxima_ending(NK - 1)))
            out.append(("sum", 2 * NC - 1))
            return out

        def sums_at(k):
            p, r = divmod(k - 2, KSG)
            if r == 0:
                return NC - 1 if p == 1 else None
            return NC * p + CHUNK_END.index(r) if r in CHUNK_END[:-1] else None

        uses = misc_uses()
        assert len(uses) == MISC_BODY, uses

        def first_of_chunk(k):
            return KS[k][2] == 0

        def chunk_step(k):
            return NC * KS[k][0] + KS[k][1]

        def last_step(n):
            return (n // NC) * KSG + CHUNK_END[n % NC]

        def load(sp, slot, par, c):
            for dst, f in ((q_st[0:L, c], 0), (q_st[L:2 * L, c], 0), (q_st[2 * L:3 * L, c], 1),
                           (k_st[0:L, par, c], 2), (k_st[L:2 * L, par, c], 3), (k_st[2 * L:3 * L, par, c], 2)):
                sp.dma_start(dst.bitcast(F32), qk_src[slot, c, f]).then_inc(loaded[c], 16)
            sp.dma_start(v_st[:, par, c], d["v"][slot, c]).then_inc(loaded[c], 16)

        def put_shift(sp, m):
            for row, src in ((3 * L, max_high), (3 * L + 1, max_low)):
                sp.dma_start(q_st[row:row + 1, m % NC].rearrange("p j (t n) -> p (j t) n", n=P).bitcast(F32),
                             src[:, m % 2].bitcast(F32)).then_inc(shift_in[m % 2], 16)

        @block.sync
        def _(sp):
            for dst, src in loads:
                sp.dma_start(dst, src).then_inc(consts_in, 16)
            for c in range(NC):
                load(sp, 0, 0, c)
            for m in range(2):
                sp.wait_ge(max_split, m + 1 + FREE)
                put_shift(sp, m)
            with sp.Fori(0, B) as b, sp.Fori(0, G // 2) as gp:
                it = sp.snap(b * (G // 2) + gp)
                slot = [sp.snap(it * 2 + p) for p in range(3)]
                rows = sp.snap(gp * (2 * HG * HD))
                for k in range(NK + 1):
                    n = chunk_step(k - 1) if k else None
                    if k and (k == NK or first_of_chunk(k)):
                        sp.wait_ge(weighted, it * NK + k)
                        load(sp, slot[n // NC + 1], (n // NC + 1) % 2, n % NC)
                    m = maxima_ending(k - 1) if k else None
                    if m is not None:
                        sp.wait_ge(max_split, it * (2 * NC) + (m + 1 + FREE))
                        put_shift(sp, m)
                    n = 2 * NC - 1 if k == NK else sums_at(k)
                    if n is not None:
                        sp.wait_ge(y_done, it * (2 * NC) + (n + 1 + FREE))
                        for j in range(HG):
                            sp.dma_start(d["y"][b, n % NC, bass.ds(rows + ((n // NC) * HG + j) * HD, HD)],
                                         y[j * L:j * L + HD, n % 2]).then_inc(y_out[n % 2], 16)
            for i in range(2):
                sp.wait_ge(y_out[i], 16 * HG * ITS * NC + FREE)
            for c in range(NC):
                sp.wait_ge(loaded[c], 112 * (SLOTS + 1))
            for i in range(2):
                sp.wait_ge(shift_in[i], 32 * (ITS * NC + 1))

        @block.tensor
        def _(pe):
            def max_unit(base, u, wait_free=True):
                group, r = divmod(u, MUG)
                c, j, t, kb = MU[r]
                par = group % 2
                if r == 0 or MU[r - 1][0] != c:
                    pe.wait_ge(loaded[c], base * (2 * 112) + 112 * (group + 1))
                if wait_free:
                    pe.wait_ge(unit_reduced, base * (2 * MUG) + (u - 1))
                width = CH if kb < c else (t + 1) * P
                out = max_ps[u % 2]
                last = nc.tensor.matmul(out[:, 0:width], q_st[0:3 * L, c, j, t * P:(t + 1) * P],
                                        k_st[0:3 * L, par, kb, j, 0:width], start=True, stop=(kb < c))
                if kb == c:
                    last = nc.tensor.matmul(out[:, width - P:width], ident_b[:], mask[:], start=False, stop=True)
                last.then_inc(unit_scored, 1)

            def misc_free(it, use):
                before = [what for what, _ in uses[:max(use - MISC_HEAD, 0)]]
                if use:
                    pe.wait_ge(max_split, it * (2 * NC) + ((min(use, MISC_HEAD) + before.count("max")) + FREE))
                if use >= MISC_HEAD:
                    pe.wait_ge(recip_done, it * (2 * NC) + (before.count("sum") + FREE))

            def transpose_max(it, m, use):
                pe.wait_ge(max_combined, it * (2 * NC) + (m + 1))
                misc_free(it, use)
                nc.tensor.transpose(misc[0:HG * TT, 0:P], neg_max[:, m % 2], ident[:]).then_inc(misc_ready, 1)

            def spread_sums(it, n, use):
                pe.wait_ge(acc_read, it * (2 * NC) + (n + 1))
                misc_free(it, use)
                nc.tensor.matmul(misc[:], pick[:], y_raw[:, n % 2], start=True, stop=True).then_inc(misc_ready, 1)

            def score(it, k, half):
                p, c, kt = KS[k]
                n = NC * p + c
                h = 2 * k + half
                if kt == 0 and half == 0:
                    pe.wait_ge(shift_in[n % 2], it * (32 * NC) + 32 * (n // 2 + 1))
                if h >= 2:
                    pe.wait_ge(exped, it * (2 * NK) + (h - 1))
                q0 = max(kt - TT * c, 0) * P
                for jj in range(2):
                    j = 2 * half + jj
                    last = nc.tensor.matmul(score_ps[half][:, jj, q0:CH],
                                            k_st[:, p, kt // TT, j, (kt % TT) * P:(kt % TT + 1) * P],
                                            q_st[:, c, j, q0:CH], start=True, stop=True)
                last.then_inc(scored, 1)

            def weigh(it, k):
                p, c, kt = KS[k]
                diag = kt >= TT * c
                pe.wait_ge(exped, it * (2 * NK) + 2 * (k + 1))
                if diag:
                    before = (NC * p + c) * TT + (kt - TT * c)
                    pe.wait_ge(masked, it * (2 * NC * TT) + (before + 1))
                if kt == 0 and k:
                    pe.wait_ge(acc_read, it * (2 * NC) + (NC * p + c))
                q0 = max(kt - TT * c, 0) * P
                for j in range(HG):
                    last = nc.tensor.matmul(acc[j * L:(j + 1) * L, q0:CH], v_st[:, p, kt // TT, kt % TT, j * L:(j + 1) * L],
                                            probs[:, k % 4, j, q0:CH], start=(kt == 0), stop=(kt == TT * (c + 1) - 1),
                                            skip_group_check=True)
                last.then_inc(weighted, 1)

            pe.wait_ge(consts_in, 16 * len(loads))
            pe.wait_ge(ones_set, 3)
            for u in range(LEAD):
                max_unit(0, u, wait_free=(u >= 2))
                if u + 1 in MU_END:
                    m = MU_END.index(u + 1)
                    transpose_max(0, m, m)
            with pe.Fori(0, ITS) as it:
                use = 0
                score(it, 0, 0)
                score(it, 0, 1)
                for k in range(NK):
                    for half in range(2):
                        if k + 1 < NK:
                            score(it, k + 1, half)
                        for i in range(PER_STEP // 2):
                            max_unit(it, LEAD + PER_STEP * k + half * (PER_STEP // 2) + i)
                    if k and maxima_ending(k - 1) is not None:
                        transpose_max(it, maxima_ending(k - 1), MISC_HEAD + use)
                        use += 1
                    weigh(it, k)
                    if sums_at(k) is not None:
                        spread_sums(it, sums_at(k), MISC_HEAD + use)
                        use += 1
                if maxima_ending(NK - 1) is not None:
                    transpose_max(it, maxima_ending(NK - 1), MISC_HEAD + use)
                    use += 1
                spread_sums(it, 2 * NC - 1, MISC_HEAD + use)

        @block.scalar
        def _(act):
            def read_acc(it, n):
                act.wait_ge(weighted, it * NK + last_step(n))
                act.wait_ge(y_done, it * (2 * NC) + (max(n - 1, 0) + FREE))
                nc.scalar.activation(y_raw[:, n % 2], acc[:], ACT.Copy).then_inc(acc_read, 1)

            with act.Fori(0, ITS) as it:
                for k in range(NK):
                    p, c, kt = KS[k]
                    q0 = max(kt - TT * c, 0) * P
                    if k >= 4:
                        act.wait_ge(weighted, it * NK + (k - 3))
                    for half in range(2):
                        act.wait_ge(scored, it * (2 * NK) + (2 * k + half + 1))
                        nc.scalar.activation(probs[:, k % 4, 2 * half:2 * half + 2, q0:CH], score_ps[half][:, :, q0:CH],
                                             ACT.Exp).then_inc(exped, 1)
                    if k and first_of_chunk(k):
                        read_acc(it, chunk_step(k) - 1)
                read_acc(it, 2 * NC - 1)

        @block.gpsimd
        def _(pool):
            zero = pool.to_reg(0.0)
            with pool.Fori(0, ITS) as it:
                for k in range(NK):
                    p, c, kt = KS[k]
                    if kt < TT * c:
                        continue
                    q0 = (kt - TT * c) * P
                    pool.wait_ge(exped, it * (2 * NK) + 2 * (k + 1))
                    pool.sem_inc(edge_due, 1)
                    edge = probs[:, k % 4, :, q0:q0 + P]
                    nc.gpsimd.affine_select(out=edge, in_=edge, pattern=[[0, HG], [1, P]], compare_op=ALU.is_ge,
                                            fill=zero, base=0, channel_multiplier=-1).then_inc(masked, 1)

        @block.vector
        def _(dve):
            nc.vector.memset(k_st[3 * L:3 * L + 2].bitcast(F32), 1.0).then_inc(ones_set, 1)
            dve.wait_ge(consts_in, 16 * len(loads))
            nc.vector.tensor_copy(mask[:], mask_f[:]).then_inc(ones_set, 1)
            nc.vector.tensor_copy(ident_b[:], ident[:]).then_inc(ones_set, 1)

            def reduce_unit(base, u):
                r = u % MUG
                c, j, t, kb = MU[r]
                m = NC * (u // MUG) + c
                width = CH if kb < c else (t + 1) * P
                dve.wait_ge(unit_scored, base * (2 * MUG) + (u + 1))
                nc.vector.tensor_reduce(partial_max[:, m % 2, j * TT + t, kb:kb + 1], max_ps[u % 2][:, 0:width],
                                        AX.X, ALU.max).then_inc(unit_reduced, 1)

            def combine_max(base, m, units):
                dve.wait_ge(unit_reduced, base * (2 * MUG) + units)
                if m >= 2:
                    dve.wait_ge(max_split, base * (2 * NC) + (m - 1 + FREE))
                nc.vector.tensor_reduce(neg_max[:, m % 2], partial_max[:, m % 2, :, 0:m % NC + 1],
                                        AX.X, ALU.max, negate=True).then_inc(max_combined, 1)

            def split_max(base, m, use):
                dve.wait_ge(misc_ready, base * MISC_BODY + (use + 1))
                dve.wait_ge(shift_in[m % 2], base * (32 * NC) + 32 * (m // 2))
                nc.vector.tensor_copy(max_high[:, m % 2], misc[0:HG * TT, 0:P]).then_inc(high_done, 1)
                dve.wait_ge(high_done, base * (2 * NC) + (m + 1))
                nc.vector.tensor_tensor(max_low[:, m % 2], misc[0:HG * TT, 0:P], max_high[:, m % 2].bitcast(F32),
                                        ALU.subtract).then_inc(max_split, 1)

            def divide(base, n, use):
                dve.wait_ge(misc_ready, base * MISC_BODY + (use + 1))
                nc.vector.reciprocal(recip[:], misc[:]).then_inc(recip_done, 1)
                dve.wait_ge(recip_done, base * (2 * NC) + (n + 1 + FREE))
                dve.wait_ge(y_out[n % 2], base * (16 * HG * NC) + (16 * HG * (n // 2) + FREE))
                nc.vector.tensor_tensor(y[:, n % 2], y_raw[:, n % 2], recip[:], ALU.mult).then_inc(y_done, 1)

            for u in range(LEAD):
                reduce_unit(0, u)
                if u + 1 in MU_END:
                    m = MU_END.index(u + 1)
                    combine_max(0, m, u + 1)
                    split_max(0, m, m)
            with dve.Fori(0, ITS) as it:
                use = 0
                for k in range(NK):
                    for i in range(PER_STEP):
                        reduce_unit(it, LEAD + PER_STEP * k + i)
                    if k and maxima_ending(k - 1) is not None:
                        split_max(it, maxima_ending(k - 1), MISC_HEAD + use)
                        use += 1
                    if sums_at(k) is not None:
                        divide(it, sums_at(k), MISC_HEAD + use)
                        use += 1
                    if maxima_ending(k) is not None:
                        combine_max(it, maxima_ending(k), LEAD + PER_STEP * (k + 1))
                if maxima_ending(NK - 1) is not None:
                    split_max(it, maxima_ending(NK - 1), MISC_HEAD + use)
                    use += 1
                divide(it, 2 * NC - 1, MISC_HEAD + use)


EPS = 1e-5
SUBS = 2
DROPPED = 65536


def mix_and_route(nc, a, d, keep_on_chip):
    ITS = B * NC // SUBS
    gather_idx, kept, top_vals = keep_on_chip
    with ExitStack() as ctx:
        s = Scope(nc, ctx, "mix")
        sb, ps, sem = s.sb, s.ps, s.sem
        l2o = sb("l2o", [P, 64])
        kv2l = sb("kv2l", [P, 64])
        kv2l_b = sb("kv2l_b", [P, 1])
        l2o_b = sb("l2o_b", [64, 1])
        cproj = sb("cproj", [64, G, C])
        cproj_b = sb("cproj_b", [P, C])
        rw1 = sb("rw1", [P, KC, HID])
        rb1 = sb("rb1", [P, MC])
        rw2 = sb("rw2", [P, MC, L])
        rb2 = sb("rb2", [P, TT, E])
        ident = sb("ident", [P, P])
        fold8 = sb("fold8", [P, E])
        before_f = sb("before_f", [P, P])
        before = sb("before", [P, P], BF16)
        ones_b = sb("ones_b", [P, P], BF16)
        rev = sb("rev", [P, E])
        head_map = sb("head_map", [64, 64])
        bias_col = sb("bias_col", [64, P])
        ones = sb("ones", [64, P])
        w_out = sb("w_out", [P, KC, C])
        b_out = sb("b_out", [P, C])
        eps = sb("eps", [P, 1])
        zero_rows = sb("zero_rows", [P, 2048])
        yt = sb("yt", [P, SUBS, KC, CH])
        xr = sb("xr", [P, SUBS, TT, C])
        xb = sb("xb", [P, SUBS, TT, C])
        z = sb("z", [P, SUBS, TT, C])
        x1 = sb("x1", [P, SUBS, TT, C])
        stats = sb("stats", [P, SUBS, TT, 6])
        moments = sb("moments", [P, SUBS, TT, 2])
        std = sb("std", [P, SUBS, TT])
        rstd = sb("rstd", [P, SUBS, TT])
        shift = sb("shift", [P, SUBS, TT])
        x1t = sb("x1t", [P, KC, CH])
        hid = sb("hid", [P, SUBS, MC, CH])
        l2 = sb("l2", [P, CH])
        logits = sb("logits", [P, TT, E])
        rest = sb("rest", [P, TT, E])
        top = sb("top", [P, 2, TT])
        cand = sb("cand", [P, 2, TT, E])
        rank = sb("rank", [P, 2, TT])
        hot = sb("hot", [P, 2, TT, E])
        hot_b = sb("hot_b", [P, SUBS, TT, E], BF16)
        seen = sb("seen", [P, E])
        seen_add = sb("seen_add", [P, E])
        seen_b = sb("seen_b", [P, SUBS, E], BF16)
        at_pos = sb("at_pos", [P, 2, TT, E])
        pos = sb("pos", [P, 2 * TT])
        fits = sb("fits", [P, 2 * TT])
        slot = sb("slot", [P, 2 * TT])
        off = sb("off", [P, 2 * TT])
        clipped = sb("clipped", [P, 2 * TT])
        scatter_idx = sb("scatter_idx", [P, SUBS, 2 * TT], U32)
        mix_ps = [ps(f"mix{i}", [P, 2, C]) for i in range(2)]
        xt_ps = [ps(f"xt{i}", [P, CH]) for i in range(2)]
        hid_ps = [ps(f"hid{i}", [P, CH]) for i in range(2)]
        l2_ps = ps("l2", [P, CH])
        small = ps("small", [P, 2, TT, E])

        consts_in = sem("consts_in")
        set_up = sem("set_up")
        folded = sem("folded")
        disp_zeroed = sem("disp_zeroed")
        chunk_in = [sem(f"chunk_in{i}") for i in range(SUBS)]
        biased = sem("biased")
        mixed = sem("mixed")
        z_done = sem("z_done")
        stats_done = sem("stats_done")
        moments_done = sem("moments_done")
        aggr_due = sem("aggr_due")
        std_done = sem("std_done")
        rstd_done = sem("rstd_done")
        norm_ready = sem("norm_ready")
        x1_done = sem("x1_done")
        turned = sem("turned")
        turned_copied = sem("turned_copied")
        hid_ready = sem("hid_ready")
        hid_done = sem("hid_done")
        l2_ready = sem("l2_ready")
        l2_copied = sem("l2_copied")
        logits_ready = sem("logits_ready")
        step = sem("step")
        hot_done = sem("hot_done")
        pos_ready = sem("pos_ready")
        pos_read = sem("pos_read")
        slots_done = sem("slots_done")
        scatter_due = sem("scatter_due")
        scattered = [sem(f"scattered{i}") for i in range(SUBS)]
        rows_free = [sem(f"rows_free{i}") for i in range(SUBS)]
        x1_out = [sem(f"x1_out{i}") for i in range(SUBS)]
        for free in (z_done, turned_copied, l2_copied, pos_read, *rows_free, *x1_out, hid_ready, logits_ready, x1_done):
            nc.sync.sem_inc(free, FREE)
        block = ctx.enter_context(nc.Block())

        loads = [
            (l2o[:], a["l2o"]), (kv2l[:], a["kv2l"]), (kv2l_b[:], a["kv2l_b"]), (l2o_b[:], a["l2o_b"]),
            (cproj[:], a["cproj_t"].rearrange("(g r) n -> r g n", r=64)), (cproj_b[:], a["cproj_b"]),
            (rw1[:], a["rw1"].rearrange("(k p) n -> p k n", p=P)), (rb1[:], a["rb1"]),
            (rw2[:, :, 0:E], a["rw2"].rearrange("(m p) n -> p m n", p=P)), (rb2[:], a["rb2"]), (ident[:], a["ident"]),
            (fold8[:], a["fold8"]), (before_f[:], a["before"]), (rev[:], a["rev"]),
        ]
        SET_UP = 7
        disp_rows = d["disp"].rearrange("(i p r) c -> i p (r c)", p=P, r=8)
        x_src = a["x"].rearrange("(i t p) c -> i p t c", p=P, t=TT)

        @block.sync
        def _(sp):
            def load(ci, sub):
                sp.dma_start(yt[:, sub], d["y"].rearrange("b c (k p) n -> (b c) p k n", p=P)[ci]).then_inc(chunk_in[sub], 16)
                sp.dma_start(xr[:, sub], x_src[ci]).then_inc(chunk_in[sub], 16)

            for sub in range(SUBS):
                load(sub, sub)
            for dst, src in loads:
                sp.dma_start(dst, src).then_inc(consts_in, 16)
            sp.wait_ge(set_up, SET_UP)
            for i in range(E):
                sp.dma_start(disp_rows[i], zero_rows[:]).then_inc(disp_zeroed, 16)

            def body(it, ci, ahead):
                for sub in range(SUBS):
                    if ahead is not None:
                        sp.wait_ge(mixed, it * (2 * SUBS) + 2 * (sub + 1))
                        sp.wait_ge(biased, it * SUBS + (sub + 1))
                        load(ahead[sub], sub)
                for sub in range(SUBS):
                    sp.wait_ge(x1_done, it * (SUBS * TT) + (TT * (sub + 1) + FREE))
                    sp.dma_start(d["x1"][ci[sub]], x1[:, sub].rearrange("p t c -> p (t c)")).then_inc(x1_out[sub], 16)
                for sub in range(SUBS):
                    sp.wait_ge(scattered[sub], it * (16 * 2 * TT) + 16 * 2 * TT)
                    sp.sem_inc(rows_free[sub], 1)

            with sp.Fori(0, ITS - 1) as it:
                body(it, [sp.snap(it * SUBS + i) for i in range(SUBS)], [sp.snap(it * SUBS + (SUBS + i)) for i in range(SUBS)])
            body(ITS - 1, [(ITS - 1) * SUBS + i for i in range(SUBS)], None)
            for i in range(SUBS):
                sp.wait_ge(x1_out[i], 16 * ITS + FREE)

        @block.gpsimd
        def _(pool):
            pool.memset(eps[:], EPS).then_inc(set_up, 1)
            pool.memset(ones[:], 1.0).then_inc(set_up, 1)
            pool.memset(seen[:], 0.0).then_inc(set_up, 1)
            pool.memset(seen_b[:], 0.0).then_inc(set_up, 1)
            pool.memset(zero_rows[:], 0.0).then_inc(set_up, 1)
            pool.memset(ones_b[:], 1.0).then_inc(set_up, 1)
            pool.wait_ge(folded, 7)
            last_slot = pool.to_reg(E * CAP - 1)
            with pool.Fori(0, ITS) as it:
                for sub in range(SUBS):
                    pool.wait_ge(chunk_in[sub], it * 32 + 32)
                    pool.wait_ge(z_done, it * (2 * SUBS) + FREE)
                    nc.gpsimd.tensor_tensor(xb[:, sub], xr[:, sub], b_out[:].unsqueeze(1).broadcast_to([P, TT, C]),
                                            ALU.add).then_inc(biased, 1)
                for sub in range(SUBS):
                    pool.wait_ge(slots_done, it * SUBS + (sub + 1))
                    pool.sem_inc(scatter_due, 1)
                    pool.wait_ge(disp_zeroed, 16 * E)
                    for kt in range(2 * TT):
                        pool.indirect_dma_start(
                            d["disp"], bass.IndirectOffsetOnAxis(ap=scatter_idx[:, sub, kt:kt + 1], axis=0),
                            x1[:, sub, kt % TT, :], None, bounds_check=last_slot, oob_is_err=False,
                        ).then_inc(scattered[sub], 16)
            for i in range(SUBS):
                pool.wait_ge(scattered[i], 16 * 2 * TT * ITS)

        @block.tensor
        def _(pe):
            pe.wait_ge(consts_in, 16 * len(loads))
            pe.wait_ge(set_up, SET_UP)
            nc.tensor.matmul(mix_ps[0][0:64, 0, 0:64], l2o[:], kv2l[:], start=True, stop=True)
            nc.tensor.matmul(mix_ps[0][0:64, 0, 64:65], l2o[:], kv2l_b[:], start=True, stop=True).then_inc(folded, 1)
            pe.wait_ge(folded, 3)
            for g in range(G):
                half = 64 * (g % 2)
                nc.tensor.matmul(mix_ps[1][half:half + 64, g // 2, :], head_map[:], cproj[:, g], start=True, stop=True)
            for g in range(G):
                last = nc.tensor.matmul(xt_ps[0][:, 0:C], bias_col[:], cproj[:, g], start=(g == 0), stop=(g == G - 1))
            last.then_inc(folded, 1)
            pe.wait_ge(folded, 7)

            def mix(it, sub):
                pe.wait_ge(chunk_in[sub], it * 32 + 32)
                for i in range(2):
                    q = 2 * sub + i
                    if q >= 2:
                        pe.wait_ge(z_done, it * (2 * SUBS) + (q - 1 + FREE))
                    for t in range(2):
                        for k in range(KC):
                            last = nc.tensor.matmul(mix_ps[i][:, t, :], yt[:, sub, k, (2 * i + t) * P:(2 * i + t + 1) * P],
                                                    w_out[:, k], start=(k == 0), stop=(k == KC - 1))
                    last.then_inc(mixed, 1)

            def turn(it, sub):
                pe.wait_ge(x1_done, it * (SUBS * TT) + (TT * (sub + 1) + FREE))
                for k in range(KC):
                    pe.wait_ge(turned_copied, it * (KC * SUBS) + (KC * sub + FREE))
                    for t in range(TT):
                        last = nc.tensor.transpose(xt_ps[k][:, t * P:(t + 1) * P], x1[:, sub, t, k * P:(k + 1) * P], ident[:])
                    last.then_inc(turned, 1)

            def router(it, sub):
                pe.wait_ge(turned_copied, it * (KC * SUBS) + (KC * (sub + 1) + FREE))
                for m in range(MC):
                    if m >= 2 or sub:
                        pe.wait_ge(hid_done, it * (SUBS * MC) + (sub * MC + m - 1))
                    for k in range(KC):
                        last = nc.tensor.matmul(hid_ps[m % 2][:], rw1[:, k, m * P:(m + 1) * P], x1t[:, k, :],
                                                start=(k == 0), stop=(k == KC - 1))
                    last.then_inc(hid_ready, 1)

            def router_out(it, sub):
                pe.wait_ge(hid_done, it * (SUBS * MC) + MC * (sub + 1))
                pe.wait_ge(l2_copied, it * SUBS + (sub + FREE))
                for m in range(MC):
                    j = m % HG
                    last = nc.tensor.matmul(l2_ps[j * L:(j + 1) * L, :], rw2[:, m, :], hid[:, sub, m, :],
                                            start=(m < HG), stop=(m >= HG), skip_group_check=True)
                last.then_inc(l2_ready, 1)
                pe.wait_ge(l2_copied, it * SUBS + (sub + 1 + FREE))
                pe.wait_ge(pos_read, it * SUBS + (sub + FREE))
                for t in range(TT):
                    last = nc.tensor.matmul(small[:, 0, t, :], l2[:, t * P:(t + 1) * P], fold8[:], start=True, stop=True)
                last.then_inc(logits_ready, 1)

            def positions(it, sub):
                pe.wait_ge(hot_done, it * SUBS + (sub + 1))
                for t in range(TT):
                    nc.tensor.matmul(small[:, 1, t, :], before[:], hot_b[:, sub, t, :], start=True, stop=False)
                    for t0 in range(t):
                        nc.tensor.matmul(small[:, 1, t, :], ones_b[:], hot_b[:, sub, t0, :], start=False, stop=False)
                    last = nc.tensor.matmul(small[:, 1, t, :], ones_b[:], seen_b[:, sub, :], start=False, stop=True)
                last.then_inc(pos_ready, 1)

            with pe.Fori(0, ITS) as it:
                for sub in range(SUBS):
                    mix(it, sub)
                turn(it, 0)
                router(it, 0)
                router_out(it, 0)
                turn(it, 1)
                router(it, 1)
                positions(it, 0)
                router_out(it, 1)
                positions(it, 1)

        @block.scalar
        def _(act):
            act.wait_ge(set_up, SET_UP)

            def norm(it, sub):
                act.wait_ge(moments_done, it * (SUBS * TT) + TT * (sub + 1))
                nc.scalar.activation(std[:, sub], moments[:, sub, :, 1], ACT.Sqrt, bias=eps[:]).then_inc(std_done, 1)
                act.wait_ge(norm_ready, it * SUBS + (sub + 1))
                act.wait_ge(rows_free[sub], it + FREE)
                act.wait_ge(x1_out[sub], it * 16 + FREE)
                for t in range(TT):
                    nc.scalar.activation(x1[:, sub, t], z[:, sub, t], ACT.Identity, bias=shift[:, sub, t:t + 1],
                                         scale=rstd[:, sub, t:t + 1]).then_inc(x1_done, 1)

            def evacuate(it, sub):
                for k in range(KC):
                    act.wait_ge(turned, it * (KC * SUBS) + (KC * sub + k + 1))
                    act.wait_ge(hid_ready, it * (SUBS * MC) + (MC * sub + FREE))
                    nc.scalar.activation(x1t[:, k], xt_ps[k][:], ACT.Copy).then_inc(turned_copied, 1)
                for m in range(MC):
                    act.wait_ge(hid_ready, it * (SUBS * MC) + (MC * sub + m + 1 + FREE))
                    nc.scalar.activation(hid[:, sub, m], hid_ps[m % 2][:], ACT.Relu, bias=rb1[:, m:m + 1]).then_inc(hid_done, 1)
                act.wait_ge(l2_ready, it * SUBS + (sub + 1))
                act.wait_ge(logits_ready, it * SUBS + (sub + FREE))
                nc.scalar.activation(l2[:], l2_ps[:], ACT.Copy).then_inc(l2_copied, 1)

            with act.Fori(0, ITS) as it:
                for sub in range(SUBS):
                    norm(it, sub)
                for sub in range(SUBS):
                    evacuate(it, sub)

        @block.vector
        def _(dve):
            nc.vector.memset(rw2[:, :, E:L], 0.0).then_inc(set_up, 1)
            dve.wait_ge(set_up, SET_UP)
            dve.wait_ge(consts_in, 16 * len(loads))
            dve.wait_ge(folded, 1)
            nc.vector.tensor_copy(head_map[:], mix_ps[0][0:64, 0, 0:64]).then_inc(folded, 1)
            nc.vector.tensor_scalar(bias_col[:], ones[:], mix_ps[0][0:64, 0, 64:65], l2o_b[:], ALU.mult, ALU.add).then_inc(folded, 1)
            dve.wait_ge(folded, 4)
            nc.vector.tensor_copy(w_out[:], mix_ps[1][:]).then_inc(folded, 1)
            nc.vector.tensor_copy(before[:], before_f[:]).then_inc(folded, 1)
            nc.vector.tensor_tensor(b_out[:], xt_ps[0][:, 0:C], cproj_b[:], ALU.add).then_inc(folded, 1)

            def moments_of(it, sub):
                for i in range(2):
                    q = 2 * sub + i
                    dve.wait_ge(mixed, it * (2 * SUBS) + (q + 1))
                    dve.wait_ge(biased, it * SUBS + (sub + 1))
                    dve.wait_ge(x1_done, it * (SUBS * TT) + FREE)
                    nc.vector.tensor_tensor(z[:, sub, 2 * i:2 * i + 2], mix_ps[i][:], xb[:, sub, 2 * i:2 * i + 2],
                                            ALU.add).then_inc(z_done, 1)
                for t in range(TT):
                    if t % 2 == 0:
                        dve.wait_ge(z_done, it * (2 * SUBS) + (2 * sub + t // 2 + 1 + FREE))
                    nc.vector.bn_stats(stats[:, sub, t], z[:, sub, t]).then_inc(stats_done, 1)
                for t in range(TT):
                    dve.wait_ge(stats_done, it * (SUBS * TT) + (TT * sub + t + 1))
                    dve.sem_inc(aggr_due, 1)
                    nc.vector.bn_aggr(moments[:, sub, t], stats[:, sub, t]).then_inc(moments_done, 1)
                dve.wait_ge(std_done, it * SUBS + (sub + 1))
                nc.vector.reciprocal(rstd[:, sub], std[:, sub]).then_inc(rstd_done, 1)
                dve.wait_ge(rstd_done, it * SUBS + (sub + 1))
                nc.vector.scalar_tensor_tensor(shift[:, sub], moments[:, sub, :, 0], -1.0, rstd[:, sub],
                                               ALU.mult, ALU.mult).then_inc(norm_ready, 1)

            STEPS = 22

            def chained(it, sub, first, steps):
                for i, issue in enumerate(steps):
                    issue().then_inc(step, 1)
                    dve.wait_ge(step, it * (SUBS * STEPS) + (sub * STEPS + first + i + 1))
                return len(steps)

            rev_b = rev[:].unsqueeze(1).broadcast_to([P, TT, E])

            def wide(ap):
                return ap.unsqueeze(2).broadcast_to([P, TT, E])

            def choose(it, sub):
                dve.wait_ge(logits_ready, it * SUBS + (sub + 1 + FREE))
                v = nc.vector
                ci = it * SUBS + sub
                n = chained(it, sub, 0, [lambda: v.tensor_tensor(logits[:], small[:, 0], rb2[:], ALU.add)])
                for k, vals in enumerate((logits, rest)):
                    n += chained(it, sub, n, [
                        lambda: v.tensor_reduce(top[:, k], vals[:], AX.X, ALU.max),
                        lambda: v.tensor_tensor(cand[:, k], vals[:], wide(top[:, k]), ALU.is_equal),
                        lambda: v.tensor_tensor(cand[:, k], cand[:, k], rev_b, ALU.mult),
                        lambda: v.tensor_reduce(rank[:, k], cand[:, k], AX.X, ALU.max),
                        lambda: v.tensor_tensor(hot[:, k], wide(rank[:, k]), rev_b, ALU.is_equal),
                    ])
                    if k == 0:
                        n += chained(it, sub, n, [
                            lambda: v.scalar_tensor_tensor(rest[:], hot[:, 0], -3.0e38, logits[:], ALU.mult, ALU.add)])
                n += chained(it, sub, n, [
                    lambda: v.tensor_copy(seen_b[:, sub], seen[:]),
                    lambda: v.tensor_copy(top_vals[:, ci], top[:].rearrange("p k t -> p (k t)"))])
                nc.vector.tensor_tensor(hot_b[:, sub], hot[:, 0], hot[:, 1], ALU.add).then_inc(hot_done, 1)
                dve.wait_ge(hot_done, it * SUBS + (sub + 1))
                n += chained(it, sub, n, [
                    lambda: v.tensor_reduce(seen_add[:], hot_b[:, sub].rearrange("p t e -> p e t"), AX.X, ALU.add),
                    lambda: v.tensor_tensor(seen[:], seen[:], seen_add[:], ALU.add)])
                return n

            def place(it, sub, n):
                v = nc.vector
                ci = it * SUBS + sub
                for k in range(2):
                    dve.wait_ge(pos_ready, it * SUBS + (sub + 1))
                    last = v.tensor_tensor(at_pos[:, k], hot[:, k], small[:, 1], ALU.mult)
                last.then_inc(pos_read, 1)
                dve.wait_ge(pos_read, it * SUBS + (sub + 1 + FREE))
                flat = rank[:].rearrange("p k t -> p (k t)")
                n += chained(it, sub, n, [
                    lambda: v.tensor_reduce(pos[:], at_pos[:].rearrange("p k t e -> p (k t) e"), AX.X, ALU.add),
                    lambda: v.tensor_scalar(fits[:], pos[:], float(CAP), None, ALU.is_lt),
                    lambda: v.tensor_scalar(off[:], fits[:], -float(DROPPED), float(DROPPED + E * CAP), ALU.mult, ALU.add),
                    lambda: v.scalar_tensor_tensor(slot[:], flat, -float(CAP), pos[:], ALU.mult, ALU.add)])
                dve.wait_ge(rows_free[sub], it + FREE)
                n += chained(it, sub, n, [
                    lambda: v.tensor_tensor(scatter_idx[:, sub], slot[:], off[:], ALU.add),
                    lambda: v.tensor_scalar(clipped[:], pos[:], float(CAP - 1), float(E * CAP), ALU.min, ALU.add)])
                v.tensor_copy(kept[:, ci], fits[:])
                v.scalar_tensor_tensor(gather_idx[:, ci], flat, -float(CAP), clipped[:], ALU.mult, ALU.add).then_inc(slots_done, 1)
                return n

            with dve.Fori(0, ITS) as it:
                for sub in range(SUBS):
                    moments_of(it, sub)
                done = [choose(it, 0)]
                done[0] = place(it, 0, done[0])
                done.append(choose(it, 1))
                done[1] = place(it, 1, done[1])
                assert done == [STEPS, STEPS], done


def experts(nc, a, d):
    ITS = E // SUBS
    HALVES = SUBS * CAP // CH
    with ExitStack() as ctx:
        s = Scope(nc, ctx, "exp")
        sb, ps, sem = s.sb, s.ps, s.sem
        ident = sb("ident", [P, P])
        w1 = sb("w1", [P, SUBS, KC, HID])
        w2 = sb("w2", [P, SUBS, MC, C])
        b1 = sb("b1", [P, SUBS, MC])
        b2 = sb("b2", [P, SUBS, C])
        rows = sb("rows", [P, HALVES, TT, C])
        rows_t = sb("rows_t", [P, 2, KC, CH])
        hid = sb("hid", [P, 2, MC, CH])
        eo = sb("eo", [P, 2, TT, C])
        xt_ps = [ps(f"xt{i}", [P, CH]) for i in range(KC)]
        hid_ps = [ps(f"hid{i}", [P, CH]) for i in range(4)]
        eo_ps = [ps(f"eo{i}", [P, 2, C]) for i in range(2)]

        ident_in = sem("ident_in")
        rows_in = [sem(f"rows_in{i}") for i in range(HALVES)]
        w_in = [sem(f"w_in{i}") for i in range(SUBS)]
        turned = sem("turned")
        turned_copied = sem("turned_copied")
        hid_ready = sem("hid_ready")
        hid_done = sem("hid_done")
        eo_ready = sem("eo_ready")
        eo_done = sem("eo_done")
        eo_out = [sem(f"eo_out{i}") for i in range(2)]
        for free in (turned_copied, eo_done, eo_ready, hid_ready, *eo_out):
            nc.sync.sem_inc(free, FREE)
        block = ctx.enter_context(nc.Block())

        rows_src = d["disp"].rearrange("(h t p) c -> h p t c", p=P, t=TT)
        eo_dst = d["eo"].rearrange("(h t p) c -> h p t c", p=P, t=TT)

        @block.sync
        def _(sp):
            def load_rows(h, q):
                sp.dma_start(rows[:, q], rows_src[h]).then_inc(rows_in[q], 16)

            def load_weights(e, sub):
                for dst, src in ((w1[:, sub], a["ew1"][e].rearrange("(k p) n -> p k n", p=P)),
                                 (w2[:, sub], a["ew2"][e].rearrange("(m p) n -> p m n", p=P)),
                                 (b1[:, sub], a["eb1"][e]), (b2[:, sub], a["eb2"][e])):
                    sp.dma_start(dst, src).then_inc(w_in[sub], 16)

            sp.dma_start(ident[:], a["ident"]).then_inc(ident_in, 16)
            for q in range(HALVES):
                if q % 2 == 0:
                    load_weights(q // 2, q // 2)
                load_rows(q, q)

            def body(it, half, ahead, expert_ahead):
                for q in range(HALVES):
                    if ahead is not None:
                        sp.wait_ge(turned, it * (KC * HALVES) + KC * (q + 1))
                        load_rows(ahead[q], q)
                    sp.wait_ge(eo_done, it * (2 * HALVES) + (2 * (q + 1) + FREE))
                    sp.dma_start(eo_dst[half[q]], eo[:, q % 2]).then_inc(eo_out[q % 2], 16)
                    if ahead is not None and q % 2:
                        load_weights(expert_ahead[q // 2], q // 2)

            with sp.Fori(0, ITS - 1) as it:
                body(it, [sp.snap(it * HALVES + q) for q in range(HALVES)],
                     [sp.snap(it * HALVES + (HALVES + q)) for q in range(HALVES)],
                     [sp.snap(it * SUBS + (SUBS + i)) for i in range(SUBS)])
            body(ITS - 1, [(ITS - 1) * HALVES + q for q in range(HALVES)], None, None)
            for i in range(2):
                sp.wait_ge(eo_out[i], 16 * ITS * HALVES // 2 + FREE)

        @block.tensor
        def _(pe):
            pe.wait_ge(ident_in, 16)

            def turn(it, q):
                pe.wait_ge(rows_in[q], it * 16 + 16)
                for k in range(KC):
                    pe.wait_ge(turned_copied, it * (KC * HALVES) + ((KC * q + max(k - 1, 0) if q or k else 0) + FREE))
                    for t in range(TT):
                        last = nc.tensor.transpose(xt_ps[k][:, t * P:(t + 1) * P], rows[:, q, t, k * P:(k + 1) * P], ident[:])
                    last.then_inc(turned, 1)

            def first(it, q):
                sub = q // 2
                pe.wait_ge(w_in[sub], it * 64 + 64)
                pe.wait_ge(turned_copied, it * (KC * HALVES) + (KC * (q + 1) + FREE))
                for m in range(MC):
                    if q or m >= 4:
                        pe.wait_ge(hid_done, it * (MC * HALVES) + (MC * q + m - 3))
                    for k in range(KC):
                        last = nc.tensor.matmul(hid_ps[m % 4][:], w1[:, sub, k, m * P:(m + 1) * P], rows_t[:, q % 2, k],
                                                start=(k == 0), stop=(k == KC - 1))
                    last.then_inc(hid_ready, 1)

            def second(it, q):
                sub = q // 2
                pe.wait_ge(hid_done, it * (MC * HALVES) + MC * (q + 1))
                for i in range(2):
                    pe.wait_ge(eo_done, it * (2 * HALVES) + ((max(2 * q + i - 1, 0)) + FREE))
                    for t in range(2):
                        for m in range(MC):
                            last = nc.tensor.matmul(eo_ps[i][:, t, :], hid[:, q % 2, m, (2 * i + t) * P:(2 * i + t + 1) * P],
                                                    w2[:, sub, m], start=(m == 0), stop=(m == MC - 1))
                    last.then_inc(eo_ready, 1)

            with pe.Fori(0, ITS) as it:
                turn(it, 0)
                for q in range(HALVES):
                    first(it, q)
                    if q + 1 < HALVES:
                        turn(it, q + 1)
                    second(it, q)

        @block.scalar
        def _(act):
            with act.Fori(0, ITS) as it:
                for q in range(HALVES):
                    act.wait_ge(eo_ready, it * (2 * HALVES) + (max(2 * (q - 1), 0) + FREE))
                    for m in range(MC):
                        act.wait_ge(hid_ready, it * (MC * HALVES) + (MC * q + m + 1 + FREE))
                        nc.scalar.activation(hid[:, q % 2, m], hid_ps[m % 4][:], ACT.Relu,
                                             bias=b1[:, q // 2, m:m + 1]).then_inc(hid_done, 1)

        @block.vector
        def _(dve):
            def copy_turned(it, q):
                for k in range(KC):
                    dve.wait_ge(turned, it * (KC * HALVES) + (KC * q + k + 1))
                    dve.wait_ge(hid_ready, it * (MC * HALVES) + (max(MC * (q - 1), 0) + FREE))
                    nc.vector.tensor_copy(rows_t[:, q % 2, k], xt_ps[k][:]).then_inc(turned_copied, 1)

            with dve.Fori(0, ITS) as it:
                copy_turned(it, 0)
                for q in range(HALVES):
                    if q + 1 < HALVES:
                        copy_turned(it, q + 1)
                    dve.wait_ge(eo_out[q % 2], it * (8 * HALVES) + (16 * (q // 2) + FREE))
                    for i in range(2):
                        dve.wait_ge(eo_ready, it * (2 * HALVES) + (2 * q + i + 1 + FREE))
                        nc.vector.tensor_tensor(eo[:, q % 2, 2 * i:2 * i + 2], eo_ps[i][:],
                                                b2[:, q // 2].unsqueeze(1).broadcast_to([P, 2, C]), ALU.add).then_inc(eo_done, 1)


def combine(nc, a, d, keep_on_chip, out):
    NCH = B * NC
    ITS = NCH // SUBS
    gather_idx, kept, top_vals = keep_on_chip
    with ExitStack() as ctx:
        s = Scope(nc, ctx, "fin")
        sb, sem = s.sb, s.sem
        gap = sb("gap", [P, NCH, TT])
        ratio = sb("ratio", [P, NCH, TT])
        total = sb("total", [P, NCH, TT])
        inv = sb("inv", [P, NCH, TT])
        weight = sb("weight", [P, NCH, 2 * TT])
        w_here = sb("w_here", [P, SUBS, 2 * TT])
        eps = sb("eps", [P, 1])
        x1 = sb("x1", [P, SUBS, TT, C])
        eo = sb("eo", [P, SUBS, 2 * TT, C])
        half_z = sb("half_z", [P, SUBS, TT, C])
        z = sb("z", [P, SUBS, TT, C])
        stats = sb("stats", [P, SUBS, TT, 6])
        moments = sb("moments", [P, SUBS, TT, 2])
        std = sb("std", [P, SUBS, TT])
        rstd = sb("rstd", [P, SUBS, TT])
        shift = sb("shift", [P, SUBS, TT])
        result = sb("result", [P, SUBS, TT, C])

        set_up = sem("set_up")
        gap_done = sem("gap_done")
        ratio_done = sem("ratio_done")
        weights = sem("weights")
        x1_in = [sem(f"x1_in{i}") for i in range(SUBS)]
        gathered = [sem(f"gathered{i}") for i in range(SUBS)]
        w_copied = sem("w_copied")
        half_done = sem("half_done")
        z_done = sem("z_done")
        stats_done = sem("stats_done")
        moments_done = sem("moments_done")
        aggr_due = sem("aggr_due")
        std_done = sem("std_done")
        rstd_done = sem("rstd_done")
        norm_ready = sem("norm_ready")
        result_done = sem("result_done")
        stored = [sem(f"stored{i}") for i in range(SUBS)]
        for free in (*stored, result_done):
            nc.sync.sem_inc(free, FREE)
        block = ctx.enter_context(nc.Block())

        out_dst = out.rearrange("b (i t p) c -> (b i) p t c", p=P, t=TT)

        @block.gpsimd
        def _(pool):
            pool.memset(eps[:], EPS).then_inc(set_up, 1)
            for ci in range(NCH):
                if ci >= SUBS:
                    pool.wait_ge(z_done, TT * (ci - 1))
                for kt in range(2 * TT):
                    pool.indirect_dma_start(
                        eo[:, ci % SUBS, kt, :], None, d["eo"],
                        bass.IndirectOffsetOnAxis(ap=gather_idx[:, ci, kt:kt + 1], axis=0),
                    ).then_inc(gathered[ci % SUBS], 16)

        @block.sync
        def _(sp):
            def load(ci, sub):
                sp.dma_start(x1[:, sub].rearrange("p t c -> p (t c)"), d["x1"][ci]).then_inc(x1_in[sub], 16)

            def body(it, ci, ahead):
                for sub in range(SUBS):
                    if ahead is not None:
                        sp.wait_ge(half_done, it * (SUBS * TT) + TT * (sub + 1))
                        load(ahead[sub], sub)
                    sp.wait_ge(result_done, it * (SUBS * TT) + (TT * (sub + 1) + FREE))
                    sp.dma_start(out_dst[ci[sub]], result[:, sub]).then_inc(stored[sub], 16)

            for sub in range(SUBS):
                load(sub, sub)
            with sp.Fori(0, ITS - 1) as it:
                body(it, [sp.snap(it * SUBS + i) for i in range(SUBS)], [sp.snap(it * SUBS + (SUBS + i)) for i in range(SUBS)])
            body(ITS - 1, [(ITS - 1) * SUBS + i for i in range(SUBS)], None)
            for i in range(SUBS):
                sp.wait_ge(stored[i], 16 * ITS + FREE)

        @block.scalar
        def _(act):
            act.wait_ge(gap_done, 1)
            nc.scalar.activation(ratio[:], gap[:], ACT.Exp).then_inc(ratio_done, 1)
            act.wait_ge(set_up, 1)
            with act.Fori(0, ITS) as it:
                for sub in range(SUBS):
                    act.wait_ge(moments_done, it * (SUBS * TT) + TT * (sub + 1))
                    nc.scalar.activation(std[:, sub], moments[:, sub, :, 1], ACT.Sqrt, bias=eps[:]).then_inc(std_done, 1)
                    act.wait_ge(norm_ready, it * SUBS + (sub + 1))
                    act.wait_ge(stored[sub], it * 16 + FREE)
                    for t in range(TT):
                        nc.scalar.activation(result[:, sub, t], z[:, sub, t], ACT.Identity, bias=shift[:, sub, t:t + 1],
                                             scale=rstd[:, sub, t:t + 1]).then_inc(result_done, 1)

        @block.vector
        def _(dve):
            first, second = top_vals[:, :, 0:TT], top_vals[:, :, TT:2 * TT]
            nc.vector.tensor_tensor(gap[:], second, first, ALU.subtract).then_inc(gap_done, 1)
            dve.wait_ge(ratio_done, 1)
            nc.vector.tensor_scalar(total[:], ratio[:], 1.0, None, ALU.add).then_inc(weights, 1)
            dve.wait_ge(weights, 1)
            nc.vector.reciprocal(inv[:], total[:]).then_inc(weights, 1)
            dve.wait_ge(weights, 2)
            nc.vector.tensor_tensor(ratio[:], ratio[:], inv[:], ALU.mult).then_inc(weights, 1)
            nc.vector.tensor_tensor(weight[:, :, 0:TT], inv[:], kept[:, :, 0:TT], ALU.mult).then_inc(weights, 1)
            dve.wait_ge(weights, 4)
            nc.vector.tensor_tensor(weight[:, :, TT:2 * TT], ratio[:], kept[:, :, TT:2 * TT], ALU.mult).then_inc(weights, 1)
            dve.wait_ge(weights, 5)
            with dve.Fori(0, ITS) as it:
                for sub in range(SUBS):
                    nc.vector.tensor_copy(w_here[:, sub], weight[:, it * SUBS + sub]).then_inc(w_copied, 1)
                    dve.wait_ge(w_copied, it * SUBS + (sub + 1))
                    dve.wait_ge(x1_in[sub], it * 16 + 16)
                    dve.wait_ge(gathered[sub], it * (16 * 2 * TT) + 16 * 2 * TT)
                    dve.wait_ge(result_done, it * (SUBS * TT) + FREE)
                    for t in range(TT):
                        nc.vector.scalar_tensor_tensor(half_z[:, sub, t], eo[:, sub, t], w_here[:, sub, t:t + 1], x1[:, sub, t],
                                                       ALU.mult, ALU.add).then_inc(half_done, 1)
                    for t in range(TT):
                        dve.wait_ge(half_done, it * (SUBS * TT) + (TT * sub + t + 1))
                        nc.vector.scalar_tensor_tensor(z[:, sub, t], eo[:, sub, TT + t], w_here[:, sub, TT + t:TT + t + 1],
                                                       half_z[:, sub, t], ALU.mult, ALU.add).then_inc(z_done, 1)
                    for t in range(TT):
                        dve.wait_ge(z_done, it * (SUBS * TT) + (TT * sub + t + 1))
                        nc.vector.bn_stats(stats[:, sub, t], z[:, sub, t]).then_inc(stats_done, 1)
                    for t in range(TT):
                        dve.wait_ge(stats_done, it * (SUBS * TT) + (TT * sub + t + 1))
                        dve.sem_inc(aggr_due, 1)
                        nc.vector.bn_aggr(moments[:, sub, t], stats[:, sub, t]).then_inc(moments_done, 1)
                    dve.wait_ge(std_done, it * SUBS + (sub + 1))
                    nc.vector.reciprocal(rstd[:, sub], std[:, sub]).then_inc(rstd_done, 1)
                    dve.wait_ge(rstd_done, it * SUBS + (sub + 1))
                    nc.vector.scalar_tensor_tensor(shift[:, sub], moments[:, sub, :, 0], -1.0, rstd[:, sub],
                                                   ALU.mult, ALU.mult).then_inc(norm_ready, 1)


def const_arrays():
    f = np.float32
    inv = (f(1.0) / np.power(f(10000.0), np.arange(0, L, 2, dtype=f) / f(L))).astype(f)
    angle = np.outer(np.arange(T, dtype=f), inv).astype(f)
    cos = np.tile(np.repeat(np.cos(angle), 2, axis=1).T, (HG, 1)).astype(f)
    sin = np.tile(np.repeat(np.sin(angle), 2, axis=1).T, (HG, 1)).astype(f)
    rot = np.zeros((2, P, P), f)
    even = np.arange(0, P, 2)
    rot[0, even, even + 1], rot[0, even + 1, even] = -1.0, 1.0
    rot[1, even + 1, even], rot[1, even, even + 1] = -1.0, 1.0
    row = np.arange(P)
    pick = np.zeros((P, P), f)
    pick[L * (row // L) + HD, row] = 1.0
    return {
        "cos": cos, "sin": sin, "rot": rot, "pick": pick, "ident": np.eye(P, dtype=f),
        "rev": np.tile(E - np.arange(E, dtype=f), (P, 1)),
        "before": (row[:, None] < row[None, :]).astype(f),
        "fold8": ((row[:, None] % L) == np.arange(E)[None, :]).astype(f),
        "cap": np.tile(np.where(row[None, :] >= row[:, None], 3.0e38, 0.0).astype(f)[:, None, :], (1, 2, 1)), "mask": np.where(row[None, :] > row[:, None], NEG, 0.0).astype(f),
    }


def laid_out(w):
    def blocks(m, n, dtype=np.float32):
        out = np.zeros((m.shape[0] * n, m.shape[1] * n), dtype)
        for i in range(n):
            out[i * m.shape[0]:(i + 1) * m.shape[0], i * m.shape[1]:(i + 1) * m.shape[1]] = m
        return out

    bias = w["L0_attn_c_attn_b"]
    return {
        "x_t": w["L0_attn_x"].reshape(N, C).T,
        "c_attn_w": w["L0_attn_c_attn_w"],
        "wv_t": w["L0_attn_c_attn_w"][2 * C:].T,
        "fold_q": blocks(w["L0_attn_q2l_w"].T, HG),
        "fold_k": blocks(w["L0_attn_kv2l_w"].T, HG),
        "b_cq": bias[0:C].reshape(G, HG * HD).T,
        "b_ck": bias[C:2 * C].reshape(G, HG * HD).T,
        "b_v": np.tile(bias[2 * C:], (P, 1)),
        "b_small": np.stack([np.tile(w[f"L0_attn_{n}_b"], HG) for n in ("q2l", "kv2l", "wqk")], axis=1),
        "wqk_t": blocks(w["L0_attn_wqk_w"].T, HG),
        "x": w["L0_attn_x"].reshape(N, C),
        "l2o": blocks(w["L0_attn_l2o_w"].T, HG),
        "kv2l": blocks(w["L0_attn_kv2l_w"], HG),
        "kv2l_b": np.tile(w["L0_attn_kv2l_b"], HG)[:, None],
        "l2o_b": np.tile(w["L0_attn_l2o_b"], HG)[:, None],
        "cproj_t": w["L0_attn_cproj_w"].T,
        "cproj_b": np.tile(w["L0_attn_cproj_b"], (P, 1)),
        "rw1": w["L0_ffn_rw1"], "rw2": w["L0_ffn_rw2"],
        "rb1": w["L0_ffn_rb1"].reshape(MC, P).T,
        "rb2": np.tile(w["L0_ffn_rb2"], (P, TT, 1)),
        "ew1": w["L0_ffn_ew1"], "ew2": w["L0_ffn_ew2"],
        "eb1": w["L0_ffn_eb1"].reshape(E, MC, P).transpose(0, 2, 1),
        "eb2": np.tile(w["L0_ffn_eb2"][:, None, :], (1, P, 1)),
    }


def program(nc, a, out):
    def scratch(name, shape, dt=F32):
        return nc.dram_tensor(name, shape, dt, kind="Internal").ap()

    d = {
        "qk": scratch("qk_parts", (SLOTS + 1, NC, 4, P, CH)),
        "v": scratch("v_tokens", (SLOTS + 1, NC, P, TT, HG * L)),
        "y": scratch("y_heads", (B, NC, C, CH)),
    }
    d |= {
        "x1": scratch("x1_rows", (B * NC, P, TT * C)),
        "disp": scratch("dispatched", (E * CAP, C)),
        "eo": scratch("expert_out", (E * CAP, C)),
    }
    with ExitStack() as ctx:
        keep = Scope(nc, ctx, "keep")
        keep_on_chip = (keep.sb("gather_idx", [P, B * NC, 2 * TT], U32), keep.sb("kept", [P, B * NC, 2 * TT]),
                        keep.sb("top_vals", [P, B * NC, 2 * TT]))
        project_heads(nc, a, d)
        attend(nc, a, d)
        mix_and_route(nc, a, d, keep_on_chip)
        experts(nc, a, d)
        combine(nc, a, d, keep_on_chip, out)


def kernel(**inputs):
    import concourse.bacc as bacc
    from concourse.bass_utils import run_bass_kernel_spmd

    nc = bacc.Bacc("TRN2", target_bir_lowering=False, num_devices=1)
    arrays = {**laid_out({k: np.asarray(v) for k, v in inputs.items()}), **const_arrays()}
    arrays = {f"in_{n}": np.ascontiguousarray(v) for n, v in arrays.items()}
    a = {n[3:]: nc.dram_tensor(n, v.shape, mybir.dt.from_np(v.dtype), kind="ExternalInput").ap()
         for n, v in arrays.items()}
    out = nc.dram_tensor("out_0", (B, T, C), F32, kind="ExternalOutput").ap()
    program(nc, a, out)
    r = run_bass_kernel_spmd(nc, [arrays], core_ids=[0])
    return r.results[0]["out_0"]
```

```python
from contextlib import ExitStack

import numpy as np
import concourse.bass as bass
from concourse import mybir

F32 = mybir.dt.float32
F32R = mybir.dt.float32r
BF16 = mybir.dt.bfloat16
U32 = mybir.dt.uint32
ALU = mybir.AluOpType
ACT = mybir.ActivationFunctionType
AX = mybir.AxisListType

P = 128
B, T, C = 4, 2048, 256
N = B * T
H, HD, L = 16, 16, 32
HG = P // L
G = H // HG
CH = 512
NC = T // CH
TT = CH // P
KC = C // P
SLOTS = B * G
SCALE = float(L) ** -0.5
E, CAP, HID = 8, 1024, 1024
MC = HID // P
NEG = -1.0e30
FREE = 1


class Scope:

    def __init__(self, nc, ctx, stage):
        self.nc, self.ctx, self.stage = nc, ctx, stage

    def sb(self, name, shape, dt=F32):
        return self.ctx.enter_context(self.nc.sbuf_tensor(f"{self.stage}_{name}", shape, dt))

    def ps(self, name, shape, dt=F32):
        return self.ctx.enter_context(self.nc.psum_tensor(f"{self.stage}_{name}_bank", shape, dt))

    def sem(self, name):
        return self.ctx.enter_context(self.nc.semaphore(f"{self.stage}_{name}"))


def project_heads(nc, a, d):
    NU = 2 * G
    ITS = B * NC // 2
    with ExitStack() as ctx:
        s = Scope(nc, ctx, "proj")
        sb, ps, sem = s.sb, s.ps, s.sem
        cq = sb("cq", [64, G, C])
        ck = sb("ck", [64, G, C])
        wv = sb("wv", [P, KC, C])
        fold_q = sb("fold_q", [64, P])
        fold_k = sb("fold_k", [64, P])
        b_cq = sb("b_cq", [64, G])
        b_ck = sb("b_ck", [64, G])
        b_small = sb("b_small", [P, 3])
        b_v = sb("b_v", [P, C])
        wqk = sb("wqk", [P, P])
        rot = sb("rot", [P, 2, P])
        cos = sb("cos", [P, T])
        sin = sb("sin", [P, T])
        wq_lat = sb("wq_lat", [P, KC, G, P])
        wk_lat = sb("wk_lat", [P, KC, G, P])
        wqk_rot = sb("wqk_rot", [P, P])
        b_q = sb("b_q", [P, G])
        b_k = sb("b_k", [P, G])
        b_qk = sb("b_qk", [P, 1])
        zeros = sb("zeros", [P, CH])
        xt = sb("xt", [P, 2, KC, CH])
        q_cos = sb("q_cos", [P, 2, CH])
        q_sin = sb("q_sin", [P, 2, CH])
        k_cos = sb("k_cos", [P, 2, CH])
        k_sin = sb("k_sin", [P, 2, CH])
        q_full = sb("q_full", [P, 2, CH])
        k_full = sb("k_full", [P, 2, CH])
        parts = sb("parts", [P, 2, 4, CH], F32R)
        v_tok = sb("v_tok", [P, 2, TT, H, L])
        lat = [[ps(f"lat{i}{x}", [P, CH]) for x in "qk"] for i in range(2)]
        fin_q = ps("fin_q", [P, CH])
        fin_k = ps("fin_k", [P, CH])
        v_ps = [ps(f"v{i}", [P, 2, C]) for i in range(2)]

        consts_in = sem("consts_in")
        filled = sem("filled")
        folded = sem("folded")
        weights_ready = sem("weights_ready")
        zeros_out = sem("zeros_out")
        xt_in = [sem(f"xt_in{i}") for i in range(2)]
        lat_ready = sem("lat_ready")
        roped = sem("roped")
        fin_q_ready = sem("fin_q_ready")
        fin_k_ready = sem("fin_k_ready")
        q_done = sem("q_done")
        k_full_done = sem("k_full_done")
        k_high_done = sem("k_high_done")
        parts_done = sem("parts_done")
        parts_out = [sem(f"parts_out{i}") for i in range(2)]
        v_ready = sem("v_ready")
        v_copied = sem("v_copied")
        v_out = [sem(f"v_out{i}") for i in range(2)]
        for free in (q_done, k_full_done, v_copied, *parts_out, parts_done, k_high_done, fin_q_ready, fin_k_ready, *v_out):
            nc.sync.sem_inc(free, FREE)
        block = ctx.enter_context(nc.Block())

        loads = [
            (cq[:], a["c_attn_w"][0:C].rearrange("(g r) c -> r g c", r=64)),
            (ck[:], a["c_attn_w"][C:2 * C].rearrange("(g r) c -> r g c", r=64)),
            (wv[:], a["wv_t"].rearrange("(k p) n -> p k n", p=P)),
            (fold_q[:], a["fold_q"]), (fold_k[:], a["fold_k"]),
            (b_cq[:], a["b_cq"]), (b_ck[:], a["b_ck"]), (b_small[:], a["b_small"]), (b_v[:], a["b_v"]),
            (wqk[:], a["wqk_t"]), (rot[:], a["rot"].rearrange("m p n -> p m n")),
            (cos[:], a["cos"]), (sin[:], a["sin"]),
        ]
        xt_src = a["x_t"].rearrange("(k p) (i n) -> i p k n", p=P, n=CH)

        @block.gpsimd
        def _(pool):
            for sub in range(2):
                pool.dma_start(xt[:, sub], xt_src[sub]).then_inc(xt_in[sub], 16)
            with pool.Fori(0, ITS - 1) as i:
                for sub in range(2):
                    nxt = pool.snap(i * 2 + (2 + sub))
                    pool.wait_ge(v_ready, i * 4 + 2 * (sub + 1))
                    pool.dma_start(xt[:, sub], xt_src[nxt]).then_inc(xt_in[sub], 16)

        @block.sync
        def _(sp):
            for dst, src in loads:
                sp.dma_start(dst, src).then_inc(consts_in, 16)
            sp.wait_ge(filled, 1)
            for c in range(NC):
                for f in range(4):
                    sp.dma_start(d["qk"][SLOTS, c, f], zeros[:]).then_inc(zeros_out, 16)
                sp.dma_start(d["v"][SLOTS, c].rearrange("p t n -> p (t n)"), zeros[:]).then_inc(zeros_out, 16)
            with sp.Fori(0, B) as b:
                with sp.Fori(0, NC // 2) as cp:
                    it = sp.snap(b * (NC // 2) + cp)
                    slot = [sp.snap(b * G + g) for g in range(G)]
                    chunk = [sp.snap(cp * 2 + sub) for sub in range(2)]
                    for sub in range(2):
                        for g in range(G):
                            u = sub * G + g
                            sp.wait_ge(parts_done, it * NU + (u + 1 + FREE))
                            sp.dma_start(d["qk"][slot[g], chunk[sub]].rearrange("f p n -> p f n"),
                                         parts[:, u % 2].bitcast(F32)).then_inc(parts_out[u % 2], 16)
                        sp.wait_ge(v_copied, it * 4 + (2 * (sub + 1) + FREE))
                        for g in range(G):
                            sp.dma_start(d["v"][slot[g], chunk[sub]],
                                         v_tok[:, sub, :, g * HG:(g + 1) * HG, :].rearrange("p t j l -> p t (j l)"),
                                         ).then_inc(v_out[sub], 16)
            sp.wait_ge(zeros_out, 16 * 5 * NC)
            for i in range(2):
                sp.wait_ge(parts_out[i], 16 * ITS * NU // 2 + FREE)
                sp.wait_ge(v_out[i], 16 * G * ITS + FREE)

        @block.tensor
        def _(pe):
            pe.wait_ge(consts_in, 16 * len(loads))
            for k in range(KC):
                for x, (c_w, fold) in enumerate(((cq, fold_q), (ck, fold_k))):
                    for g in range(G):
                        last = nc.tensor.matmul(lat[x][k][:, g * P:(g + 1) * P], c_w[:, g, k * P:(k + 1) * P],
                                                fold[:], start=True, stop=True)
            last.then_inc(folded, 1)
            nc.tensor.matmul(fin_q[:, 0:G], fold_q[:], b_cq[:], start=True, stop=True)
            nc.tensor.matmul(fin_q[:, G:2 * G], fold_k[:], b_ck[:], start=True, stop=True)
            nc.tensor.matmul(fin_k[:, 0:P], rot[:, 0], wqk[:], start=True, stop=True).then_inc(folded, 1)
            pe.wait_ge(weights_ready, 8)

            def finish(it, u):
                par = u % 2
                pe.wait_ge(roped, it * (2 * NU) + (2 * u + 1))
                pe.wait_ge(q_done, it * NU + (u + FREE))
                nc.tensor.matmul(fin_q[:], wqk[:], q_cos[:, par], start=True, stop=False)
                nc.tensor.matmul(fin_q[:], wqk_rot[:], q_sin[:, par], start=False, stop=True).then_inc(fin_q_ready, 1)
                pe.wait_ge(roped, it * (2 * NU) + (2 * u + 2))
                pe.wait_ge(k_full_done, it * NU + (u + FREE))
                nc.tensor.matmul(fin_k[:], rot[:, 1], k_sin[:, par], start=True, stop=True).then_inc(fin_k_ready, 1)

            with pe.Fori(0, ITS) as it:
                for u in range(NU):
                    sub, g, par = u // G, u % G, u % 2
                    if g == 0:
                        pe.wait_ge(xt_in[sub], it * 16 + 16)
                    if u >= 2:
                        pe.wait_ge(roped, it * (2 * NU) + 2 * (u - 1))
                    for x, w in enumerate((wq_lat, wk_lat)):
                        for k in range(KC):
                            last = nc.tensor.matmul(lat[par][x][:], w[:, k, g, :], xt[:, sub, k, :],
                                                    start=(k == 0), stop=(k == KC - 1))
                        last.then_inc(lat_ready, 1)
                    if u > 0:
                        finish(it, u - 1)
                    if g == G - 1:
                        for pair in range(2):
                            vi = 2 * sub + pair
                            pe.wait_ge(v_copied, it * 4 + (max(vi - 1, 0) + FREE))
                            for t in range(2):
                                for k in range(KC):
                                    last = nc.tensor.matmul(
                                        v_ps[pair][:, t, :], xt[:, sub, k, (2 * pair + t) * P:(2 * pair + t + 1) * P],
                                        wv[:, k, :], start=(k == 0), stop=(k == KC - 1))
                            last.then_inc(v_ready, 1)
                finish(it, NU - 1)

        @block.scalar
        def _(act):
            act.wait_ge(consts_in, 16 * len(loads))
            nc.scalar.mul(b_qk[:], b_small[:, 2:3], SCALE).then_inc(weights_ready, 1)
            act.wait_ge(weights_ready, 8)
            with act.Fori(0, ITS) as it:
                for u in range(NU):
                    par = u % 2
                    act.wait_ge(fin_q_ready, it * NU + (u + 1 + FREE))
                    act.wait_ge(parts_out[par], it * (8 * NU) + (16 * (u // 2) + FREE))
                    act.wait_ge(parts_done, it * NU + (max(u - 1, 0) + FREE))
                    nc.scalar.activation(q_full[:, par], fin_q[:], ACT.Identity, bias=b_qk[:], scale=SCALE)
                    nc.scalar.activation(parts[:, par, 0], fin_q[:], ACT.Identity, bias=b_qk[:],
                                         scale=SCALE).then_inc(q_done, 1)
                    act.wait_ge(k_full_done, it * NU + (u + 1 + FREE))
                    nc.scalar.activation(parts[:, par, 2], k_full[:, par], ACT.Copy).then_inc(k_high_done, 1)

        @block.vector
        def _(dve):
            nc.vector.memset(zeros[:], 0.0).then_inc(filled, 1)
            nc.vector.memset(v_tok[:], 0.0).then_inc(filled, 1)
            dve.wait_ge(filled, 2)
            nc.vector.memset(v_tok[:, :, :, :, HD:HD + 1], 1.0).then_inc(filled, 1)
            dve.wait_ge(folded, 1)
            for k in range(KC):
                for x, w in enumerate((wq_lat, wk_lat)):
                    nc.vector.tensor_copy(w[:, k].rearrange("p g n -> p (g n)"), lat[x][k][:]).then_inc(weights_ready, 1)
            dve.wait_ge(folded, 2)
            nc.vector.tensor_copy(wqk_rot[:], fin_k[:, 0:P]).then_inc(weights_ready, 1)
            dve.wait_ge(consts_in, 16 * len(loads))
            nc.vector.tensor_scalar(b_q[:], fin_q[:, 0:G], b_small[:, 0:1], None, ALU.add).then_inc(weights_ready, 1)
            nc.vector.tensor_scalar(b_k[:], fin_q[:, G:2 * G], b_small[:, 1:2], None, ALU.add).then_inc(weights_ready, 1)
            dve.wait_ge(weights_ready, 8)

            def finish(it, u):
                par = u % 2
                dve.wait_ge(fin_k_ready, it * NU + (u + 1 + FREE))
                dve.wait_ge(k_high_done, it * NU + (max(u - 1, 0) + FREE))
                nc.vector.tensor_tensor(k_full[:, par], fin_k[:], k_cos[:, par], ALU.add).then_inc(k_full_done, 1)
                dve.wait_ge(q_done, it * NU + (u + 1 + FREE))
                nc.vector.tensor_tensor(parts[:, par, 1], q_full[:, par], parts[:, par, 0].bitcast(F32), ALU.subtract)
                dve.wait_ge(k_high_done, it * NU + (u + 1 + FREE))
                nc.vector.tensor_tensor(parts[:, par, 3], k_full[:, par], parts[:, par, 2].bitcast(F32),
                                        ALU.subtract).then_inc(parts_done, 1)

            with dve.Fori(0, B) as b:
                with dve.Fori(0, NC // 2) as cp:
                    it = b * (NC // 2) + cp
                    for u in range(NU):
                        sub, g, par = u // G, u % G, u % 2
                        at = bass.ds(cp * (2 * CH) + sub * CH, CH)
                        for x, (bias, w_cos, w_sin) in enumerate(((b_q, q_cos, q_sin), (b_k, k_cos, k_sin))):
                            dve.wait_ge(lat_ready, it * (2 * NU) + (2 * u + x + 1))
                            dve.wait_ge((fin_q_ready, fin_k_ready)[x], it * NU + (max(u - 1, 0) + FREE))
                            nc.vector.scalar_tensor_tensor(w_cos[:, par], lat[par][x][:], bias[:, g:g + 1],
                                                           cos[:, at], ALU.add, ALU.mult)
                            nc.vector.scalar_tensor_tensor(w_sin[:, par], lat[par][x][:], bias[:, g:g + 1],
                                                           sin[:, at], ALU.add, ALU.mult).then_inc(roped, 1)
                        if u > 0:
                            finish(it, u - 1)
                        if g == G - 1:
                            for pair in range(2):
                                dve.wait_ge(v_ready, it * 4 + (2 * sub + pair + 1))
                                dve.wait_ge(v_out[sub], it * (16 * G) + FREE)
                                for t in range(2):
                                    last = nc.vector.tensor_tensor(
                                        v_tok[:, sub, 2 * pair + t, :, 0:HD],
                                        v_ps[pair][:, t, :].rearrange("p (h e) -> p h e", e=HD),
                                        b_v[:].rearrange("p (h e) -> p h e", e=HD), ALU.add)
                                last.then_inc(v_copied, 1)
                    finish(it, NU - 1)


KS = [(p, c, kt) for p in range(2) for c in range(NC) for kt in range(TT * (c + 1))]
KSG = len(KS) // 2
MU = [(c, j, t, kb) for c in range(NC) for j in range(HG) for t in range(TT) for kb in range(c + 1)]
MUG = len(MU)
PER_STEP = MUG // KSG
LEAD = 5 * HG * TT
CHUNK_END = [TT * (c + 1) * (c + 2) // 2 for c in range(NC)]
MU_END = [HG * TT * (c + 1) * (c + 2) // 2 for c in range(NC)]


def maxima_ending(k):
    done = LEAD + PER_STEP * (k + 1)
    group, rest = divmod(done, MUG)
    if rest == 0:
        return NC * group - 1
    return NC * group + MU_END.index(rest) if rest in MU_END else None


def attend(nc, a, d):
    ITS = SLOTS // 2
    NK = len(KS)
    with ExitStack() as ctx:
        s = Scope(nc, ctx, "att")
        sb, ps, sem = s.sb, s.ps, s.sem
        q_st = sb("q_st", [98, NC, HG, CH], F32R)
        k_st = sb("k_st", [98, 2, NC, HG, CH], F32R)
        v_st = sb("v_st", [P, 2, NC, TT, HG * L])
        probs = sb("probs", [P, 4, HG, CH])
        mask_f = sb("mask_f", [P, P])
        mask = sb("mask", [P, P], BF16)
        ident_b = sb("ident_b", [P, P], BF16)
        ident = sb("ident", [P, P])
        partial_max = sb("partial_max", [P, 2, HG * TT, NC])
        neg_max = sb("neg_max", [P, 2, HG * TT])
        max_high = sb("max_high", [HG * TT, 2, P], F32R)
        max_low = sb("max_low", [HG * TT, 2, P], F32R)
        y_raw = sb("y_raw", [P, 2, CH])
        recip = sb("recip", [P, TT, HG])
        y = sb("y", [P, 2, TT, HG, HD])
        score_ps = [ps(f"score{i}", [P, CH]) for i in range(3)]
        max_ps = [ps(f"max{i}", [P, CH]) for i in range(3)]
        acc = ps("acc", [P, CH])
        misc = ps("misc", [P, CH])

        consts_in = sem("consts_in")
        ones_set = sem("ones_set")
        loaded = [sem(f"loaded{c}") for c in range(NC)]
        unit_scored = sem("unit_scored")
        unit_reduced = sem("unit_reduced")
        max_combined = sem("max_combined")
        misc_ready = sem("misc_ready")
        max_split = sem("max_split")
        high_done = sem("high_done")
        shift_in = [sem(f"shift_in{i}") for i in range(2)]
        scored = sem("scored")
        exped = sem("exped")
        masked = sem("masked")
        edge_due = sem("edge_due")
        weighted = sem("weighted")
        acc_read = sem("acc_read")
        recip_done = sem("recip_done")
        y_done = sem("y_done")
        y_out = [sem(f"y_out{i}") for i in range(2)]
        for free in (y_done, max_split, *y_out):
            nc.sync.sem_inc(free, FREE)
        block = ctx.enter_context(nc.Block())

        loads = [(mask_f[:], a["mask"]), (ident[:], a["ident"])]
        qk_src = d["qk"].rearrange("s c f (j p) n -> s c f p j n", p=L)
        MISC_BODY = 2 * NC * 2
        MISC_HEAD = 2

        def misc_uses():
            out = []
            for k in range(NK):
                if k and maxima_ending(k - 1) is not None:
                    out.append(("max", maxima_ending(k - 1)))
                n = sums_at(k)
                if n is not None:
                    out.append(("sum", n))
            if maxima_ending(NK - 1) is not None:
                out.append(("max", maxima_ending(NK - 1)))
            out.append(("sum", 2 * NC - 1))
            return out

        def sums_at(k):
            p, r = divmod(k - 2, KSG)
            if r == 0:
                return NC - 1 if p == 1 else None
            return NC * p + CHUNK_END.index(r) if r in CHUNK_END[:-1] else None

        def max_bank(u):
            return (u - LEAD) % 3

        uses = misc_uses()
        assert len(uses) == MISC_BODY, uses

        def first_of_chunk(k):
            return KS[k][2] == 0

        def chunk_step(k):
            return NC * KS[k][0] + KS[k][1]

        def last_step(n):
            return (n // NC) * KSG + CHUNK_END[n % NC]

        def load(sp, slot, par, c):
            for dst, f in ((q_st[0:L, c], 0), (q_st[L:2 * L, c], 0), (q_st[2 * L:3 * L, c], 1),
                           (k_st[0:L, par, c], 2), (k_st[L:2 * L, par, c], 3), (k_st[2 * L:3 * L, par, c], 2)):
                sp.dma_start(dst.bitcast(F32), qk_src[slot, c, f]).then_inc(loaded[c], 16)
            sp.dma_start(v_st[:, par, c], d["v"][slot, c]).then_inc(loaded[c], 16)

        def put_shift(sp, m):
            for row, src in ((3 * L, max_high), (3 * L + 1, max_low)):
                sp.dma_start(q_st[row:row + 1, m % NC].rearrange("p j (t n) -> p (j t) n", n=P).bitcast(F32),
                             src[:, m % 2].bitcast(F32)).then_inc(shift_in[m % 2], 16)

        @block.sync
        def _(sp):
            for dst, src in loads:
                sp.dma_start(dst, src).then_inc(consts_in, 16)
            for c in range(NC):
                load(sp, 0, 0, c)
            for m in range(2):
                sp.wait_ge(max_split, m + 1 + FREE)
                put_shift(sp, m)
            with sp.Fori(0, B) as b, sp.Fori(0, G // 2) as gp:
                it = sp.snap(b * (G // 2) + gp)
                slot = [sp.snap(it * 2 + p) for p in range(3)]
                cols = [sp.snap(gp * (2 * HG * HD) + p * (HG * HD)) for p in range(2)]
                for k in range(NK + 1):
                    n = chunk_step(k - 1) if k else None
                    if k and (k == NK or first_of_chunk(k)):
                        sp.wait_ge(weighted, it * NK + k)
                        load(sp, slot[n // NC + 1], (n // NC + 1) % 2, n % NC)
                    m = maxima_ending(k - 1) if k else None
                    if m is not None:
                        sp.wait_ge(max_split, it * (2 * NC) + (m + 1 + FREE))
                        put_shift(sp, m)
                    n = 2 * NC - 1 if k == NK else sums_at(k)
                    if n is not None:
                        sp.wait_ge(y_done, it * (2 * NC) + (n + 1 + FREE))
                        sp.dma_start(d["y"][b, n % NC, :, :, bass.ds(cols[n // NC], HG * HD)],
                                     y[:, n % 2].rearrange("p t j e -> p t (j e)")).then_inc(y_out[n % 2], 16)
            for i in range(2):
                sp.wait_ge(y_out[i], 16 * ITS * NC + FREE)
            for c in range(NC):
                sp.wait_ge(loaded[c], 112 * (SLOTS + 1))
            for i in range(2):
                sp.wait_ge(shift_in[i], 32 * (ITS * NC + 1))

        @block.tensor
        def _(pe):
            def max_unit(base, u, wait_free=True):
                group, r = divmod(u, MUG)
                c, j, t, kb = MU[r]
                par = group % 2
                if r == 0 or MU[r - 1][0] != c:
                    pe.wait_ge(loaded[c], base * (2 * 112) + 112 * (group + 1))
                if wait_free:
                    pe.wait_ge(unit_reduced, base * (2 * MUG) + (u - 1 if (u - LEAD) % (2 * MUG) < 2 else u - 2))
                width = CH if kb < c else (t + 1) * P
                out = max_ps[max_bank(u)]
                last = nc.tensor.matmul(out[:, 0:width], q_st[0:3 * L, c, j, t * P:(t + 1) * P],
                                        k_st[0:3 * L, par, kb, j, 0:width], start=True, stop=(kb < c))
                if kb == c:
                    last = nc.tensor.matmul(out[:, width - P:width], ident_b[:], mask[:], start=False, stop=True)
                last.then_inc(unit_scored, 1)

            def misc_free(it, use):
                before = [what for what, _ in uses[:max(use - MISC_HEAD, 0)]]
                if use:
                    pe.wait_ge(max_split, it * (2 * NC) + ((min(use, MISC_HEAD) + before.count("max")) + FREE))
                if use >= MISC_HEAD:
                    pe.wait_ge(y_done, it * (2 * NC) + (before.count("sum") + FREE))

            def transpose_max(it, m, use):
                pe.wait_ge(max_combined, it * (2 * NC) + (m + 1))
                misc_free(it, use)
                nc.tensor.transpose(misc[0:HG * TT, 0:P], neg_max[:, m % 2], ident[:]).then_inc(misc_ready, 1)

            def turn_sums(it, n, use):
                pe.wait_ge(acc_read, it * (2 * NC) + (n + 1))
                misc_free(it, use)
                for t in range(TT):
                    last = nc.tensor.transpose(misc[:, t * P:(t + 1) * P], y_raw[:, n % 2, t * P:(t + 1) * P], ident[:])
                last.then_inc(misc_ready, 1)

            def exps_through(h):
                return exps_next + (h - HG * NK)

            def score(it, k, j):
                p, c, kt = KS[k]
                n = NC * p + c
                h = HG * k + j
                if kt == 0 and j == 0:
                    pe.wait_ge(shift_in[n % 2], it * (32 * NC) + 32 * (n // 2 + 1))
                if h >= 3:
                    pe.wait_ge(exped, exps_through(h - 2))
                q0 = max(kt - TT * c, 0) * P
                nc.tensor.matmul(score_ps[h % 3][:, q0:CH],
                                 k_st[:, p, kt // TT, j, (kt % TT) * P:(kt % TT + 1) * P],
                                 q_st[:, c, j, q0:CH], start=True, stop=True).then_inc(scored, 1)

            def weigh(it, k):
                p, c, kt = KS[k]
                diag = kt >= TT * c
                pe.wait_ge(exped, exps_through(HG * (k + 1)))
                if diag:
                    before = (NC * p + c) * TT + (kt - TT * c)
                    pe.wait_ge(masked, it * (2 * NC * TT) + (before + 1))
                if kt == 0 and k:
                    pe.wait_ge(acc_read, it * (2 * NC) + (NC * p + c))
                q0 = max(kt - TT * c, 0) * P
                for j in range(HG):
                    last = nc.tensor.matmul(acc[j * L:(j + 1) * L, q0:CH], v_st[:, p, kt // TT, kt % TT, j * L:(j + 1) * L],
                                            probs[:, k % 4, j, q0:CH], start=(kt == 0), stop=(kt == TT * (c + 1) - 1),
                                            skip_group_check=True)
                last.then_inc(weighted, 1)

            pe.wait_ge(consts_in, 16 * len(loads))
            pe.wait_ge(ones_set, 3)
            for u in range(LEAD):
                max_unit(0, u, wait_free=(u >= 2))
                if u + 1 in MU_END:
                    m = MU_END.index(u + 1)
                    transpose_max(0, m, m)
            with pe.Fori(0, ITS) as it:
                use = 0
                exps_next = pe.snap((it + 1) * (HG * NK))
                for j in range(HG):
                    score(it, 0, j)
                for k in range(NK):
                    for j in range(HG):
                        if k + 1 < NK:
                            score(it, k + 1, j)
                        max_unit(it, LEAD + PER_STEP * k + j)
                    if k and maxima_ending(k - 1) is not None:
                        transpose_max(it, maxima_ending(k - 1), MISC_HEAD + use)
                        use += 1
                    weigh(it, k)
                    if sums_at(k) is not None:
                        turn_sums(it, sums_at(k), MISC_HEAD + use)
                        use += 1
                if maxima_ending(NK - 1) is not None:
                    transpose_max(it, maxima_ending(NK - 1), MISC_HEAD + use)
                    use += 1
                turn_sums(it, 2 * NC - 1, MISC_HEAD + use)

        @block.scalar
        def _(act):
            def read_acc(it, n):
                act.wait_ge(weighted, it * NK + last_step(n))
                act.wait_ge(y_done, it * (2 * NC) + (max(n - 1, 0) + FREE))
                nc.scalar.activation(y_raw[:, n % 2], acc[:], ACT.Copy).then_inc(acc_read, 1)

            with act.Fori(0, ITS) as it:
                for k in range(NK):
                    p, c, kt = KS[k]
                    q0 = max(kt - TT * c, 0) * P
                    if k >= 4:
                        act.wait_ge(weighted, it * NK + (k - 3))
                    for j in range(HG):
                        act.wait_ge(scored, it * (HG * NK) + (HG * k + j + 1))
                        nc.scalar.activation(probs[:, k % 4, j, q0:CH], score_ps[(HG * k + j) % 3][:, q0:CH],
                                             ACT.Exp).then_inc(exped, 1)
                    if k and first_of_chunk(k):
                        read_acc(it, chunk_step(k) - 1)
                read_acc(it, 2 * NC - 1)

        @block.gpsimd
        def _(pool):
            zero = pool.to_reg(0.0)
            with pool.Fori(0, ITS) as it:
                for k in range(NK):
                    p, c, kt = KS[k]
                    if kt < TT * c:
                        continue
                    q0 = (kt - TT * c) * P
                    pool.wait_ge(exped, it * (HG * NK) + HG * (k + 1))
                    pool.sem_inc(edge_due, 1)
                    edge = probs[:, k % 4, :, q0:q0 + P]
                    nc.gpsimd.affine_select(out=edge, in_=edge, pattern=[[0, HG], [1, P]], compare_op=ALU.is_ge,
                                            fill=zero, base=0, channel_multiplier=-1).then_inc(masked, 1)

        @block.vector
        def _(dve):
            nc.vector.memset(k_st[3 * L:3 * L + 2].bitcast(F32), 1.0).then_inc(ones_set, 1)
            dve.wait_ge(consts_in, 16 * len(loads))
            nc.vector.tensor_copy(mask[:], mask_f[:]).then_inc(ones_set, 1)
            nc.vector.tensor_copy(ident_b[:], ident[:]).then_inc(ones_set, 1)

            def reduce_unit(base, u):
                r = u % MUG
                c, j, t, kb = MU[r]
                m = NC * (u // MUG) + c
                width = CH if kb < c else (t + 1) * P
                dve.wait_ge(unit_scored, base * (2 * MUG) + (u + 1))
                nc.vector.tensor_reduce(partial_max[:, m % 2, j * TT + t, kb:kb + 1], max_ps[max_bank(u)][:, 0:width],
                                        AX.X, ALU.max).then_inc(unit_reduced, 1)

            def combine_max(base, m, units):
                dve.wait_ge(unit_reduced, base * (2 * MUG) + units)
                if m >= 2:
                    dve.wait_ge(max_split, base * (2 * NC) + (m - 1 + FREE))
                nc.vector.tensor_reduce(neg_max[:, m % 2], partial_max[:, m % 2, :, 0:m % NC + 1],
                                        AX.X, ALU.max, negate=True).then_inc(max_combined, 1)

            def split_max(base, m, use):
                dve.wait_ge(misc_ready, base * MISC_BODY + (use + 1))
                dve.wait_ge(shift_in[m % 2], base * (32 * NC) + 32 * (m // 2))
                nc.vector.tensor_copy(max_high[:, m % 2], misc[0:HG * TT, 0:P]).then_inc(high_done, 1)
                dve.wait_ge(high_done, base * (2 * NC) + (m + 1))
                nc.vector.tensor_tensor(max_low[:, m % 2], misc[0:HG * TT, 0:P], max_high[:, m % 2].bitcast(F32),
                                        ALU.subtract).then_inc(max_split, 1)

            def divide(base, n, use):
                dve.wait_ge(misc_ready, base * MISC_BODY + (use + 1))
                turned = misc[:].rearrange("p (t j l) -> p t j l", t=TT, j=HG)
                nc.vector.reciprocal(recip[:], turned[:, :, :, HD]).then_inc(recip_done, 1)
                dve.wait_ge(recip_done, base * (2 * NC) + (n + 1))
                dve.wait_ge(y_out[n % 2], base * (16 * NC) + (16 * (n // 2) + FREE))
                nc.vector.tensor_tensor(y[:, n % 2], turned[:, :, :, 0:HD],
                                        recip[:].unsqueeze(3).broadcast_to([P, TT, HG, HD]), ALU.mult).then_inc(y_done, 1)

            for u in range(LEAD):
                reduce_unit(0, u)
                if u + 1 in MU_END:
                    m = MU_END.index(u + 1)
                    combine_max(0, m, u + 1)
                    split_max(0, m, m)
            with dve.Fori(0, ITS) as it:
                use = 0
                for k in range(NK):
                    for i in range(PER_STEP):
                        reduce_unit(it, LEAD + PER_STEP * k + i)
                    if k and maxima_ending(k - 1) is not None:
                        split_max(it, maxima_ending(k - 1), MISC_HEAD + use)
                        use += 1
                    if sums_at(k) is not None:
                        divide(it, sums_at(k), MISC_HEAD + use)
                        use += 1
                    if maxima_ending(k) is not None:
                        combine_max(it, maxima_ending(k), LEAD + PER_STEP * (k + 1))
                if maxima_ending(NK - 1) is not None:
                    split_max(it, maxima_ending(NK - 1), MISC_HEAD + use)
                    use += 1
                divide(it, 2 * NC - 1, MISC_HEAD + use)


EPS = 1e-5
SUBS = 2
DROPPED = 65536


def mix_and_route(nc, a, d, keep_on_chip):
    NCH = B * NC
    ROUND = 4
    BODIES = (NCH - 1) // ROUND
    gather_idx, kept, top_vals = keep_on_chip
    with ExitStack() as ctx:
        s = Scope(nc, ctx, "mix")
        sb, ps, sem = s.sb, s.ps, s.sem
        l2o = sb("l2o", [P, 64])
        kv2l = sb("kv2l", [P, 64])
        kv2l_b = sb("kv2l_b", [P, 1])
        l2o_b = sb("l2o_b", [64, 1])
        cproj = sb("cproj", [64, G, C])
        cproj_b = sb("cproj_b", [P, C])
        rw1 = sb("rw1", [P, KC, HID])
        rw1_high = sb("rw1_high", [P, KC, HID], F32R)
        rw1_low = sb("rw1_low", [P, KC, HID], F32R)
        rb1 = sb("rb1", [P, MC])
        rw2 = sb("rw2", [P, MC, L])
        rb2 = sb("rb2", [P, TT, E])
        ident = sb("ident", [P, P])
        fold8 = sb("fold8", [P, E])
        before_f = sb("before_f", [P, P])
        before = sb("before", [P, P], BF16)
        ones_b = sb("ones_b", [P, P], BF16)
        rev = sb("rev", [P, E])
        head_map = sb("head_map", [64, 64])
        bias_col = sb("bias_col", [64, P])
        ones = sb("ones", [64, P])
        w_out = sb("w_out", [P, KC, C])
        b_out = sb("b_out", [P, C])
        eps = sb("eps", [P, 1])
        zero_rows = sb("zero_rows", [P, 2048])
        yr = sb("yr", [P, SUBS, TT, C])
        yt = sb("yt", [P, KC, CH])
        xr = sb("xr", [P, SUBS, TT, C])
        xb = sb("xb", [P, SUBS, TT, C])
        z = sb("z", [P, SUBS, TT, C])
        x1 = sb("x1", [P, ROUND, TT, C])
        stats = sb("stats", [P, SUBS, TT, 6])
        moments = sb("moments", [P, SUBS, TT, 2])
        std = sb("std", [P, SUBS, TT])
        rstd = sb("rstd", [P, SUBS, TT])
        shift = sb("shift", [P, SUBS, TT])
        x1t_high = sb("x1t_high", [P, KC, CH], F32R)
        x1t_low = sb("x1t_low", [P, KC, CH], F32R)
        hid = sb("hid", [P, MC, CH])
        l2 = sb("l2", [P, CH])
        logits = sb("logits", [P, TT, E])
        rest = sb("rest", [P, TT, E])
        top = sb("top", [P, 2, TT])
        cand = sb("cand", [P, 2, TT, E])
        rank = sb("rank", [P, 2, TT])
        hot = sb("hot", [P, 2, TT, E])
        hot_b = sb("hot_b", [P, SUBS, TT, E], BF16)
        seen = sb("seen", [P, E])
        seen_add = sb("seen_add", [P, E])
        seen_b = sb("seen_b", [P, SUBS, E], BF16)
        at_pos = sb("at_pos", [P, 2, TT, E])
        pos = sb("pos", [P, 2 * TT])
        fits = sb("fits", [P, 2 * TT])
        slot = sb("slot", [P, 2 * TT])
        off = sb("off", [P, 2 * TT])
        clipped = sb("clipped", [P, 2 * TT])
        scatter_idx = sb("scatter_idx", [P, SUBS, 2 * TT], U32)
        mix_ps = [ps(f"mix{i}", [P, 2, C]) for i in range(2)]
        xt_ps = [ps(f"xt{i}", [P, CH]) for i in range(2)]
        hid_ps = [ps(f"hid{i}", [P, CH]) for i in range(2)]
        l2_ps = ps("l2", [P, CH])
        small = ps("small", [P, 2, TT, E])

        consts_in = sem("consts_in")
        set_up = sem("set_up")
        folded = sem("folded")
        disp_zeroed = sem("disp_zeroed")
        chunk_in = [sem(f"chunk_in{i}") for i in range(SUBS)]
        biased = sem("biased")
        mixed = sem("mixed")
        z_done = sem("z_done")
        stats_done = sem("stats_done")
        moments_done = sem("moments_done")
        aggr_due = sem("aggr_due")
        std_done = sem("std_done")
        rstd_done = sem("rstd_done")
        norm_ready = sem("norm_ready")
        x1_done = sem("x1_done")
        turned = sem("turned")
        high_done = sem("high_done")
        rw1_split = sem("rw1_split")
        turned_copied = sem("turned_copied")
        x1t_split = sem("x1t_split")
        hid_ready = sem("hid_ready")
        hid_done = sem("hid_done")
        l2_ready = sem("l2_ready")
        l2_copied = sem("l2_copied")
        logits_ready = sem("logits_ready")
        step_done = sem("step_done")
        hot_done = sem("hot_done")
        pos_ready = sem("pos_ready")
        pos_read = sem("pos_read")
        slots_done = sem("slots_done")
        scatter_due = sem("scatter_due")
        scattered = [sem(f"scattered{i}") for i in range(ROUND)]
        rows_free = sem("rows_free")
        x1_out = [sem(f"x1_out{i}") for i in range(ROUND)]
        for free in (z_done, turned_copied, l2_copied, pos_read, *x1_out, hid_ready, logits_ready, x1_done,
                     hid_done, mixed, x1t_split):
            nc.sync.sem_inc(free, FREE)
        nc.sync.sem_inc(rows_free, ROUND)
        block = ctx.enter_context(nc.Block())

        loads = [
            (l2o[:], a["l2o"]), (kv2l[:], a["kv2l"]), (kv2l_b[:], a["kv2l_b"]), (l2o_b[:], a["l2o_b"]),
            (cproj[:], a["cproj_t"].rearrange("(g r) n -> r g n", r=64)), (cproj_b[:], a["cproj_b"]),
            (rw1[:], a["rw1"].rearrange("(k p) n -> p k n", p=P)), (rb1[:], a["rb1"]),
            (rw2[:, :, 0:E], a["rw2"].rearrange("(m p) n -> p m n", p=P)), (rb2[:], a["rb2"]), (ident[:], a["ident"]),
            (fold8[:], a["fold8"]), (before_f[:], a["before"]), (rev[:], a["rev"]),
        ]
        SET_UP = 7
        FOLDED = 8
        disp_rows = d["disp"].rearrange("(i p r) c -> i p (r c)", p=P, r=8)
        x_src = a["x"].rearrange("(i t p) c -> i p t c", p=P, t=TT)

        def after(c, k):
            return c[0], c[1] + k

        def count(c, per, plus=0, bufs=1):
            body, r = c
            return body * (ROUND // bufs * per) + (r // bufs * per + plus)

        def run_steps(engine, step):
            step((0, 0))
            with engine.Fori(0, BODIES) as it:
                for r in range(1, ROUND + 1):
                    step((it, r))
            for c in range(BODIES * ROUND + 1, NCH):
                step((0, c))

        def is_first(c):
            return isinstance(c[0], int) and c[1] == 0

        def is_last(c, ahead):
            return isinstance(c[0], int) and c[1] + ahead >= NCH

        @block.sync
        def _(sp):
            def load(chunk, buf):
                sp.dma_start(yr[:, buf], d["y"].rearrange("b c p t n -> (b c) p t n")[chunk]).then_inc(chunk_in[buf], 16)
                sp.dma_start(xr[:, buf], x_src[chunk]).then_inc(chunk_in[buf], 16)

            def store(c, chunk):
                sp.wait_ge(x1_done, count(c, TT, TT + FREE))
                buf = c[1] % ROUND
                sp.dma_start(d["x1"][chunk], x1[:, buf].rearrange("p t c -> p (t c)")).then_inc(x1_out[buf], 16)

            for c in range(SUBS):
                load(c, c)
            for dst, src in loads:
                sp.dma_start(dst, src).then_inc(consts_in, 16)
            sp.wait_ge(set_up, SET_UP)
            for i in range(E):
                sp.dma_start(disp_rows[i], zero_rows[:]).then_inc(disp_zeroed, 16)
            sp.wait_ge(turned, KC)
            sp.wait_ge(biased, 1)
            load(2, 0)
            store((0, 0), 0)

            def step(c):
                chunk = {k: c[0] * ROUND + (c[1] + k) for k in (1, 3)}
                if not isinstance(c[0], int):
                    chunk = {k: sp.snap(v) for k, v in chunk.items()}
                if not is_last(c, 3):
                    sp.wait_ge(turned, count(c, 2 * KC, 3 * KC))
                    sp.wait_ge(biased, count(c, 1, 2))
                    load(chunk[3], (c[1] + 3) % SUBS)
                if not is_last(c, 1):
                    store(after(c, 1), chunk[1])
                if not is_first(c):
                    done = after(c, -1)
                    sp.wait_ge(scattered[done[1] % ROUND], count(done, 16 * 2 * TT, 16 * 2 * TT, bufs=ROUND))
                    sp.sem_inc(rows_free, 1)

            run_steps(sp, step)
            for i in range(ROUND):
                sp.wait_ge(x1_out[i], 16 * NCH // ROUND + FREE)

        @block.gpsimd
        def _(pool):
            pool.memset(eps[:], EPS).then_inc(set_up, 1)
            pool.memset(ones[:], 1.0).then_inc(set_up, 1)
            pool.memset(seen[:], 0.0).then_inc(set_up, 1)
            pool.memset(seen_b[:], 0.0).then_inc(set_up, 1)
            pool.memset(zero_rows[:], 0.0).then_inc(set_up, 1)
            pool.memset(ones_b[:], 1.0).then_inc(set_up, 1)
            pool.wait_ge(folded, FOLDED)
            last_slot = pool.to_reg(E * CAP - 1)

            def bias(c):
                sub = c[1] % SUBS
                pool.wait_ge(chunk_in[sub], count(c, 32, 32, bufs=SUBS))
                if c[1] >= SUBS:
                    pool.wait_ge(z_done, count(c, 2, 2 - 2 * SUBS + FREE))
                nc.gpsimd.tensor_tensor(xb[:, sub], xr[:, sub], b_out[:].unsqueeze(1).broadcast_to([P, TT, C]),
                                        ALU.add).then_inc(biased, 1)

            def scatter(c):
                pool.wait_ge(slots_done, count(c, 1, 1))
                pool.sem_inc(scatter_due, 1)
                pool.wait_ge(disp_zeroed, 16 * E)
                for kt in range(2 * TT):
                    pool.indirect_dma_start(
                        d["disp"], bass.IndirectOffsetOnAxis(ap=scatter_idx[:, c[1] % SUBS, kt:kt + 1], axis=0),
                        x1[:, c[1] % ROUND, kt % TT, :], None, bounds_check=last_slot, oob_is_err=False,
                    ).then_inc(scattered[c[1] % ROUND], 16)

            def step(c):
                if not is_first(c):
                    scatter(after(c, -1))
                if not is_last(c, 2):
                    bias(after(c, 2))

            bias((0, 0))
            bias((0, 1))
            run_steps(pool, step)
            scatter((0, NCH - 1))
            for i in range(ROUND):
                pool.wait_ge(scattered[i], 16 * 2 * TT * NCH // ROUND)

        @block.tensor
        def _(pe):
            pe.wait_ge(consts_in, 16 * len(loads))
            pe.wait_ge(set_up, SET_UP)
            nc.tensor.matmul(mix_ps[0][0:64, 0, 0:64], l2o[:], kv2l[:], start=True, stop=True)
            nc.tensor.matmul(mix_ps[0][0:64, 0, 64:65], l2o[:], kv2l_b[:], start=True, stop=True).then_inc(folded, 1)
            pe.wait_ge(folded, 3)
            for g in range(G):
                half = 64 * (g % 2)
                nc.tensor.matmul(mix_ps[1][half:half + 64, g // 2, :], head_map[:], cproj[:, g], start=True, stop=True)
            for g in range(G):
                last = nc.tensor.matmul(xt_ps[0][:, 0:C], bias_col[:], cproj[:, g], start=(g == 0), stop=(g == G - 1))
            last.then_inc(folded, 1)
            pe.wait_ge(folded, FOLDED)

            def turn(source, wait_free):
                for k in range(KC):
                    wait_free(k)
                    for t in range(TT):
                        last = nc.tensor.transpose(xt_ps[k][:, t * P:(t + 1) * P], source(t)[:, k * P:(k + 1) * P], ident[:])
                    last.then_inc(turned, 1)

            def turn_x1(c):
                pe.wait_ge(x1_done, count(c, TT, TT + FREE))
                turn(lambda t: x1[:, c[1] % ROUND, t], lambda k: pe.wait_ge(turned_copied, count(c, KC, k + 1 + FREE)))

            def turn_y(c):
                pe.wait_ge(chunk_in[c[1] % SUBS], count(c, 32, 32, bufs=SUBS))
                turn(lambda t: yr[:, c[1] % SUBS, t], lambda k: None if is_first(c) else
                     pe.wait_ge(x1t_split, count(c, KC, k + 1 - KC + FREE)))

            def mix(c):
                pe.wait_ge(turned_copied, count(c, KC, KC + FREE))
                for i in range(2):
                    if not is_first(c):
                        pe.wait_ge(z_done, count(c, 2, i - 1 + FREE))
                    for t in range(2):
                        for k in range(KC):
                            last = nc.tensor.matmul(mix_ps[i][:, t, :], yt[:, k, (2 * i + t) * P:(2 * i + t + 1) * P],
                                                    w_out[:, k], start=(k == 0), stop=(k == KC - 1))
                    last.then_inc(mixed, 1)

            def router(c, m):
                if m == 0:
                    pe.wait_ge(x1t_split, count(c, 2, 2 + FREE))
                if not is_first(c) or m >= 2:
                    pe.wait_ge(hid_done, count(c, MC, m - 1 + FREE))
                terms = [(w, x, k) for k in range(KC) for w, x in ((rw1_high, x1t_high), (rw1_high, x1t_low), (rw1_low, x1t_high))]
                for i, (w, x, k) in enumerate(terms):
                    last = nc.tensor.matmul(hid_ps[m % 2][:], w[:, k, m * P:(m + 1) * P], x[:, k, :],
                                            start=(i == 0), stop=(i == len(terms) - 1))
                last.then_inc(hid_ready, 1)

            def router_out(c):
                pe.wait_ge(hid_done, count(c, MC, MC + FREE))
                pe.wait_ge(l2_copied, count(c, 1, FREE))
                for m in range(MC):
                    j = m % HG
                    last = nc.tensor.matmul(l2_ps[j * L:(j + 1) * L, :], rw2[:, m, :], hid[:, m, :],
                                            start=(m < HG), stop=(m >= HG), skip_group_check=True)
                last.then_inc(l2_ready, 1)
                pe.wait_ge(l2_copied, count(c, 1, 1 + FREE))
                pe.wait_ge(pos_read, count(c, 1, FREE))
                for t in range(TT):
                    last = nc.tensor.matmul(small[:, 0, t, :], l2[:, t * P:(t + 1) * P], fold8[:], start=True, stop=True)
                last.then_inc(logits_ready, 1)

            def positions(c):
                pe.wait_ge(hot_done, count(c, 1, 1))
                for t in range(TT):
                    nc.tensor.matmul(small[:, 1, t, :], before[:], hot_b[:, c[1] % SUBS, t, :], start=True, stop=False)
                    for t0 in range(t):
                        nc.tensor.matmul(small[:, 1, t, :], ones_b[:], hot_b[:, c[1] % SUBS, t0, :], start=False, stop=False)
                    last = nc.tensor.matmul(small[:, 1, t, :], ones_b[:], seen_b[:, c[1] % SUBS, :], start=False, stop=True)
                last.then_inc(pos_ready, 1)

            def step(c):
                ahead = not is_last(c, 1)
                turn_x1(c)
                if ahead:
                    turn_y(after(c, 1))
                for m in range(MC):
                    router(c, m)
                    if m == 1 and ahead:
                        mix(after(c, 1))
                    if m == 1 and not is_first(c):
                        positions(after(c, -1))
                router_out(c)

            turn_y((0, 0))
            mix((0, 0))
            run_steps(pe, step)
            positions((0, NCH - 1))

        @block.scalar
        def _(act):
            act.wait_ge(set_up, SET_UP)
            act.wait_ge(consts_in, 16 * len(loads))
            nc.scalar.activation(rw1_high[:], rw1[:], ACT.Copy).then_inc(rw1_split, 1)

            def deviation(c):
                act.wait_ge(moments_done, count(c, TT, TT))
                nc.scalar.activation(std[:, c[1] % SUBS], moments[:, c[1] % SUBS, :, 1], ACT.Sqrt,
                                     bias=eps[:]).then_inc(std_done, 1)

            def norm(c, tiles):
                sub, buf = c[1] % SUBS, c[1] % ROUND
                act.wait_ge(norm_ready, count(c, 1, 1))
                act.wait_ge(rows_free, count(c, 1, 1))
                act.wait_ge(x1_out[buf], count(c, 16, FREE, bufs=ROUND))
                for t in tiles:
                    nc.scalar.activation(x1[:, buf, t], z[:, sub, t], ACT.Identity, bias=shift[:, sub, t:t + 1],
                                         scale=rstd[:, sub, t:t + 1]).then_inc(x1_done, 1)

            def copy_y(c):
                for k in range(KC):
                    act.wait_ge(turned, count(c, 2 * KC, k + 1))
                    if not is_first(c):
                        act.wait_ge(mixed, count(c, 2, FREE))
                    nc.scalar.activation(yt[:, k], xt_ps[k][:], ACT.Copy).then_inc(turned_copied, 1)

            def step(c):
                ahead = not is_last(c, 1)
                for k in range(KC):
                    act.wait_ge(turned, count(c, 2 * KC, KC + k + 1))
                    act.wait_ge(hid_ready, count(c, MC, FREE))
                    nc.scalar.activation(x1t_high[:, k], xt_ps[k][:], ACT.Copy).then_inc(high_done, 1)
                if ahead:
                    copy_y(after(c, 1))
                for m in range(MC):
                    act.wait_ge(hid_ready, count(c, MC, m + 1 + FREE))
                    nc.scalar.activation(hid[:, m], hid_ps[m % 2][:], ACT.Relu, bias=rb1[:, m:m + 1]).then_inc(hid_done, 1)
                    if m == 4 and ahead:
                        deviation(after(c, 1))
                    if m >= 5 and ahead:
                        norm(after(c, 1), range(m - 5, TT if m == MC - 1 else m - 4))
                act.wait_ge(l2_ready, count(c, 1, 1))
                act.wait_ge(logits_ready, count(c, 1, FREE))
                nc.scalar.activation(l2[:], l2_ps[:], ACT.Copy).then_inc(l2_copied, 1)

            copy_y((0, 0))
            deviation((0, 0))
            norm((0, 0), range(TT))
            run_steps(act, step)

        @block.vector
        def _(dve):
            nc.vector.memset(rw2[:, :, E:L], 0.0).then_inc(set_up, 1)
            dve.wait_ge(set_up, SET_UP)
            dve.wait_ge(consts_in, 16 * len(loads))
            dve.wait_ge(folded, 1)
            nc.vector.tensor_copy(head_map[:], mix_ps[0][0:64, 0, 0:64]).then_inc(folded, 1)
            nc.vector.tensor_scalar(bias_col[:], ones[:], mix_ps[0][0:64, 0, 64:65], l2o_b[:], ALU.mult, ALU.add).then_inc(folded, 1)
            dve.wait_ge(folded, 4)
            nc.vector.tensor_copy(w_out[:], mix_ps[1][:]).then_inc(folded, 1)
            nc.vector.tensor_copy(before[:], before_f[:]).then_inc(folded, 1)
            nc.vector.tensor_tensor(b_out[:], xt_ps[0][:, 0:C], cproj_b[:], ALU.add).then_inc(folded, 1)
            dve.wait_ge(rw1_split, 1)
            nc.vector.tensor_tensor(rw1_low[:], rw1[:], rw1_high[:].bitcast(F32), ALU.subtract).then_inc(folded, 1)

            def split_x1(c):
                for k in range(KC):
                    dve.wait_ge(high_done, count(c, KC, k + 1))
                    nc.vector.tensor_tensor(x1t_low[:, k], xt_ps[k][:], x1t_high[:, k].bitcast(F32),
                                            ALU.subtract).then_inc(x1t_split, 1)

            def moments_of(c):
                sub = c[1] % SUBS
                for i in range(2):
                    dve.wait_ge(mixed, count(c, 2, i + 1 + FREE))
                    dve.wait_ge(biased, count(c, 1, 1))
                    if c[1] >= SUBS:
                        dve.wait_ge(x1_done, count(c, TT, TT - TT * SUBS + FREE))
                    nc.vector.tensor_tensor(z[:, sub, 2 * i:2 * i + 2], mix_ps[i][:], xb[:, sub, 2 * i:2 * i + 2],
                                            ALU.add).then_inc(z_done, 1)
                for t in range(TT):
                    if t % 2 == 0:
                        dve.wait_ge(z_done, count(c, 2, t // 2 + 1 + FREE))
                    nc.vector.bn_stats(stats[:, sub, t], z[:, sub, t]).then_inc(stats_done, 1)
                for t in range(TT):
                    dve.wait_ge(stats_done, count(c, TT, t + 1))
                    dve.sem_inc(aggr_due, 1)
                    nc.vector.bn_aggr(moments[:, sub, t], stats[:, sub, t]).then_inc(moments_done, 1)
                dve.wait_ge(std_done, count(c, 1, 1))
                nc.vector.reciprocal(rstd[:, sub], std[:, sub]).then_inc(rstd_done, 1)
                dve.wait_ge(rstd_done, count(c, 1, 1))
                nc.vector.scalar_tensor_tensor(shift[:, sub], moments[:, sub, :, 0], -1.0, rstd[:, sub],
                                               ALU.mult, ALU.mult).then_inc(norm_ready, 1)

            STEPS = 22

            def chained(c, first, steps):
                for i, issue in enumerate(steps):
                    issue().then_inc(step_done, 1)
                    dve.wait_ge(step_done, count(c, STEPS, first + i + 1))
                return len(steps)

            rev_b = rev[:].unsqueeze(1).broadcast_to([P, TT, E])

            def wide(ap):
                return ap.unsqueeze(2).broadcast_to([P, TT, E])

            def choose(c):
                dve.wait_ge(logits_ready, count(c, 1, 1 + FREE))
                v = nc.vector
                sub, ci = c[1] % SUBS, c[0] * ROUND + c[1]
                n = chained(c, 0, [lambda: v.tensor_tensor(logits[:], small[:, 0], rb2[:], ALU.add)])
                for k, vals in enumerate((logits, rest)):
                    n += chained(c, n, [
                        lambda: v.tensor_reduce(top[:, k], vals[:], AX.X, ALU.max),
                        lambda: v.tensor_tensor(cand[:, k], vals[:], wide(top[:, k]), ALU.is_equal),
                        lambda: v.tensor_tensor(cand[:, k], cand[:, k], rev_b, ALU.mult),
                        lambda: v.tensor_reduce(rank[:, k], cand[:, k], AX.X, ALU.max),
                        lambda: v.tensor_tensor(hot[:, k], wide(rank[:, k]), rev_b, ALU.is_equal),
                    ])
                    if k == 0:
                        n += chained(c, n, [
                            lambda: v.scalar_tensor_tensor(rest[:], hot[:, 0], -3.0e38, logits[:], ALU.mult, ALU.add)])
                n += chained(c, n, [
                    lambda: v.tensor_copy(seen_b[:, sub], seen[:]),
                    lambda: v.tensor_copy(top_vals[:, ci], top[:].rearrange("p k t -> p (k t)"))])
                nc.vector.tensor_tensor(hot_b[:, sub], hot[:, 0], hot[:, 1], ALU.add).then_inc(hot_done, 1)
                dve.wait_ge(hot_done, count(c, 1, 1))
                n += chained(c, n, [
                    lambda: v.tensor_reduce(seen_add[:], hot_b[:, sub].rearrange("p t e -> p e t"), AX.X, ALU.add),
                    lambda: v.tensor_tensor(seen[:], seen[:], seen_add[:], ALU.add)])
                return n

            def place(c, n):
                v = nc.vector
                sub, ci = c[1] % SUBS, c[0] * ROUND + c[1]
                for k in range(2):
                    dve.wait_ge(pos_ready, count(c, 1, 1))
                    last = v.tensor_tensor(at_pos[:, k], hot[:, k], small[:, 1], ALU.mult)
                last.then_inc(pos_read, 1)
                dve.wait_ge(pos_read, count(c, 1, 1 + FREE))
                flat = rank[:].rearrange("p k t -> p (k t)")
                n += chained(c, n, [
                    lambda: v.tensor_reduce(pos[:], at_pos[:].rearrange("p k t e -> p (k t) e"), AX.X, ALU.add),
                    lambda: v.tensor_scalar(fits[:], pos[:], float(CAP), None, ALU.is_lt),
                    lambda: v.tensor_scalar(off[:], fits[:], -float(DROPPED), float(DROPPED + E * CAP), ALU.mult, ALU.add),
                    lambda: v.scalar_tensor_tensor(slot[:], flat, -float(CAP), pos[:], ALU.mult, ALU.add)])
                dve.wait_ge(rows_free, count(c, 1, ROUND - 1))
                n += chained(c, n, [
                    lambda: v.tensor_tensor(scatter_idx[:, sub], slot[:], off[:], ALU.add),
                    lambda: v.tensor_scalar(clipped[:], pos[:], float(CAP - 1), float(E * CAP), ALU.min, ALU.add)])
                v.tensor_copy(kept[:, ci], fits[:])
                v.scalar_tensor_tensor(gather_idx[:, ci], flat, -float(CAP), clipped[:], ALU.mult, ALU.add).then_inc(slots_done, 1)
                assert n == STEPS, n

            def step(c):
                split_x1(c)
                if not is_first(c):
                    n = choose(after(c, -1))
                if not is_last(c, 1):
                    moments_of(after(c, 1))
                if not is_first(c):
                    place(after(c, -1), n)

            moments_of((0, 0))
            run_steps(dve, step)
            place((0, NCH - 1), choose((0, NCH - 1)))


def experts(nc, a, d):
    ITS = E // SUBS
    HALVES = SUBS * CAP // CH
    with ExitStack() as ctx:
        s = Scope(nc, ctx, "exp")
        sb, ps, sem = s.sb, s.ps, s.sem
        ident = sb("ident", [P, P])
        w1 = sb("w1", [P, SUBS, KC, HID])
        w2 = sb("w2", [P, SUBS, MC, C])
        b1 = sb("b1", [P, SUBS, MC])
        b2 = sb("b2", [P, SUBS, C])
        rows = sb("rows", [P, HALVES, TT, C])
        w1_high = sb("w1_high", [P, SUBS, KC, HID], F32R)
        w1_low = sb("w1_low", [P, SUBS, KC, HID], F32R)
        w2_high = sb("w2_high", [P, SUBS, MC, C], F32R)
        w2_low = sb("w2_low", [P, SUBS, MC, C], F32R)
        rows_high = sb("rows_high", [P, 2, KC, CH], F32R)
        rows_low = sb("rows_low", [P, 2, KC, CH], F32R)
        hid = sb("hid", [P, 2, CH])
        hid_high = sb("hid_high", [P, MC, CH], F32R)
        hid_low = sb("hid_low", [P, MC, CH], F32R)
        eo = sb("eo", [P, 2, TT, C])
        xt_ps = [ps(f"xt{i}", [P, CH]) for i in range(KC)]
        hid_ps = [ps(f"hid{i}", [P, CH]) for i in range(4)]
        eo_ps = [ps(f"eo{i}", [P, 2, C]) for i in range(2)]

        ident_in = sem("ident_in")
        rows_in = [sem(f"rows_in{i}") for i in range(HALVES)]
        w_in = [sem(f"w_in{i}") for i in range(SUBS)]
        b_in = [sem(f"b_in{i}") for i in range(SUBS)]
        turned = sem("turned")
        weights_high = sem("weights_high")
        weights_split = sem("weights_split")
        rows_high_done = sem("rows_high_done")
        turned_copied = sem("turned_copied")
        hid_high_done = sem("hid_high_done")
        hid_ready = sem("hid_ready")
        hid_done = sem("hid_done")
        eo_ready = sem("eo_ready")
        eo_done = sem("eo_done")
        eo_out = [sem(f"eo_out{i}") for i in range(2)]
        for free in (turned_copied, eo_done, eo_ready, hid_ready, hid_done, *eo_out):
            nc.sync.sem_inc(free, FREE)
        block = ctx.enter_context(nc.Block())

        rows_src = d["disp"].rearrange("(h t p) c -> h p t c", p=P, t=TT)
        eo_dst = d["eo"].rearrange("(h t p) c -> h p t c", p=P, t=TT)

        def run_bodies(engine, body):
            with engine.Fori(0, ITS - 1) as it:
                body(it, False)
            body(ITS - 1, True)

        @block.sync
        def _(sp):
            def load_rows(h, q):
                sp.dma_start(rows[:, q], rows_src[h]).then_inc(rows_in[q], 16)

            def load_weights(e, sub):
                for dst, src in ((w1[:, sub], a["ew1"][e].rearrange("(k p) n -> p k n", p=P)),
                                 (w2[:, sub], a["ew2"][e].rearrange("(m p) n -> p m n", p=P))):
                    sp.dma_start(dst, src).then_inc(w_in[sub], 16)

            def load_biases(e, sub):
                for dst, src in ((b1[:, sub], a["eb1"][e]), (b2[:, sub], a["eb2"][e])):
                    sp.dma_start(dst, src).then_inc(b_in[sub], 16)

            sp.dma_start(ident[:], a["ident"]).then_inc(ident_in, 16)
            for q in range(HALVES):
                if q % 2 == 0:
                    load_weights(q // 2, q // 2)
                    load_biases(q // 2, q // 2)
                load_rows(q, q)

            def body(it, half, ahead, expert_ahead):
                for q in range(HALVES):
                    if ahead is not None and q % 2 == 0:
                        sp.wait_ge(weights_split, it * (2 * SUBS) + (q + 2))
                        load_weights(expert_ahead[q // 2], q // 2)
                    if ahead is not None:
                        sp.wait_ge(turned, it * (KC * HALVES) + KC * (q + 1))
                        load_rows(ahead[q], q)
                    sp.wait_ge(eo_done, it * (2 * HALVES) + (2 * (q + 1) + FREE))
                    sp.dma_start(eo_dst[half[q]], eo[:, q % 2]).then_inc(eo_out[q % 2], 16)
                    if ahead is not None and q % 2:
                        load_biases(expert_ahead[q // 2], q // 2)

            with sp.Fori(0, ITS - 1) as it:
                body(it, [sp.snap(it * HALVES + q) for q in range(HALVES)],
                     [sp.snap(it * HALVES + (HALVES + q)) for q in range(HALVES)],
                     [sp.snap(it * SUBS + (SUBS + i)) for i in range(SUBS)])
            body(ITS - 1, [(ITS - 1) * HALVES + q for q in range(HALVES)], None, None)
            for i in range(2):
                sp.wait_ge(eo_out[i], 16 * ITS * HALVES // 2 + FREE)

        @block.tensor
        def _(pe):
            pe.wait_ge(ident_in, 16)

            def turn(it, q):
                pe.wait_ge(rows_in[q % HALVES], it * 16 + 16 * (q // HALVES + 1))
                for k in range(KC):
                    pe.wait_ge(turned_copied, it * (KC * HALVES) + ((KC * q + max(k - 1, 0) if q or k else 0) + FREE))
                    for t in range(TT):
                        last = nc.tensor.transpose(xt_ps[k][:, t * P:(t + 1) * P], rows[:, q % HALVES, t, k * P:(k + 1) * P], ident[:])
                    last.then_inc(turned, 1)

            def first(it, q):
                sub = q // 2
                if q % 2 == 0:
                    pe.wait_ge(weights_split, it * (2 * SUBS) + 2 * (sub + 1))
                pe.wait_ge(turned_copied, it * (KC * HALVES) + (KC * (q + 1) + FREE))
                terms = [(w, x, k) for k in range(KC)
                         for w, x in ((w1_high, rows_high), (w1_high, rows_low), (w1_low, rows_high))]
                for m in range(MC):
                    if q or m >= 4:
                        pe.wait_ge(hid_done, it * (MC * HALVES) + (MC * q + m - 3 + FREE))
                    for i, (w, x, k) in enumerate(terms):
                        last = nc.tensor.matmul(hid_ps[m % 4][:], w[:, sub, k, m * P:(m + 1) * P], x[:, q % 2, k],
                                                start=(i == 0), stop=(i == len(terms) - 1))
                    last.then_inc(hid_ready, 1)

            def second(it, q):
                sub = q // 2
                terms = [(x, w, m) for m in range(MC)
                         for x, w in ((hid_high, w2_high), (hid_high, w2_low), (hid_low, w2_high))]
                pe.wait_ge(hid_done, it * (MC * HALVES) + (MC * (q + 1) + FREE))
                for i in range(2):
                    pe.wait_ge(eo_done, it * (2 * HALVES) + ((max(2 * q + i - 1, 0)) + FREE))
                    for t in range(2):
                        for n, (x, w, m) in enumerate(terms):
                            last = nc.tensor.matmul(eo_ps[i][:, t, :], x[:, m, (2 * i + t) * P:(2 * i + t + 1) * P],
                                                    w[:, sub, m], start=(n == 0), stop=(n == len(terms) - 1))
                    last.then_inc(eo_ready, 1)

            def body(it, last):
                for q in range(HALVES):
                    first(it, q)
                    if not last or q + 1 < HALVES:
                        turn(it, q + 1)
                    second(it, q)

            turn(0, 0)
            run_bodies(pe, body)

        @block.scalar
        def _(act):
            def high_weights(it, sub):
                sub, turns = sub % SUBS, sub // SUBS
                act.wait_ge(w_in[sub], it * 32 + 32 * (turns + 1))
                act.wait_ge(eo_ready, it * (2 * HALVES) + (max(4 * (sub + SUBS * turns) - 4, 0) + FREE))
                nc.scalar.activation(w1_high[:, sub], w1[:, sub], ACT.Copy).then_inc(weights_high, 1)
                nc.scalar.activation(w2_high[:, sub], w2[:, sub], ACT.Copy).then_inc(weights_high, 1)

            def rows_of(it, q):
                for k in range(KC):
                    act.wait_ge(turned, it * (KC * HALVES) + (KC * q + k + 1))
                    act.wait_ge(hid_ready, it * (MC * HALVES) + (max(MC * (q - 1), 0) + FREE))
                    nc.scalar.activation(rows_high[:, q % 2, k], xt_ps[k][:], ACT.Copy).then_inc(rows_high_done, 1)

            def body(it, last):
                for q in range(HALVES):
                    if q % 2 == 0:
                        act.wait_ge(b_in[q // 2], it * 32 + 32)
                    for m in range(MC):
                        act.wait_ge(hid_ready, it * (MC * HALVES) + (MC * q + m + 1 + FREE))
                        nc.scalar.activation(hid_high[:, m], hid_ps[m % 4][:], ACT.Relu, bias=b1[:, q // 2, m:m + 1])
                        act.wait_ge(hid_done, it * (MC * HALVES) + (max(MC * q + m - 1, 0) + FREE))
                        nc.scalar.activation(hid[:, m % 2], hid_ps[m % 4][:], ACT.Relu,
                                             bias=b1[:, q // 2, m:m + 1]).then_inc(hid_high_done, 1)
                    if not last or q + 1 < HALVES:
                        rows_of(it, q + 1)
                    if q % 2 == 0 and not (last and q):
                        high_weights(it, q // 2 + 1)

            high_weights(0, 0)
            rows_of(0, 0)
            run_bodies(act, body)

        @block.vector
        def _(dve):
            def low_weights(it, sub):
                for i, (w, high, low) in enumerate(((w1, w1_high, w1_low), (w2, w2_high, w2_low))):
                    dve.wait_ge(weights_high, it * (2 * SUBS) + (2 * sub + i + 1))
                    nc.vector.tensor_tensor(low[:, sub % SUBS], w[:, sub % SUBS], high[:, sub % SUBS].bitcast(F32),
                                            ALU.subtract).then_inc(weights_split, 1)

            def rows_of(it, q):
                for k in range(KC):
                    dve.wait_ge(rows_high_done, it * (KC * HALVES) + (KC * q + k + 1))
                    nc.vector.tensor_tensor(rows_low[:, q % 2, k], xt_ps[k][:], rows_high[:, q % 2, k].bitcast(F32),
                                            ALU.subtract).then_inc(turned_copied, 1)

            def add_bias(it, q):
                dve.wait_ge(eo_out[q % 2], it * (16 * HALVES // 2) + (16 * (q // 2) + FREE))
                if q % 2 == 0:
                    dve.wait_ge(b_in[q // 2], it * 32 + 32)
                for i in range(2):
                    dve.wait_ge(eo_ready, it * (2 * HALVES) + (2 * q + i + 1 + FREE))
                    nc.vector.tensor_tensor(eo[:, q % 2, 2 * i:2 * i + 2], eo_ps[i][:],
                                            b2[:, q // 2].unsqueeze(1).broadcast_to([P, 2, C]), ALU.add).then_inc(eo_done, 1)

            def body(it, last):
                for q in range(HALVES):
                    for m in range(MC):
                        dve.wait_ge(hid_high_done, it * (MC * HALVES) + (MC * q + m + 1))
                        nc.vector.tensor_tensor(hid_low[:, m], hid[:, m % 2], hid_high[:, m].bitcast(F32),
                                                ALU.subtract).then_inc(hid_done, 1)
                    if not last or q + 1 < HALVES:
                        rows_of(it, q + 1)
                    if q % 2 == 0 and not (last and q):
                        low_weights(it, q // 2 + 1)
                    add_bias(it, q)

            low_weights(0, 0)
            rows_of(0, 0)
            run_bodies(dve, body)


def combine(nc, a, d, keep_on_chip, out):
    NCH = B * NC
    ITS = NCH // SUBS
    gather_idx, kept, top_vals = keep_on_chip
    with ExitStack() as ctx:
        s = Scope(nc, ctx, "fin")
        sb, sem = s.sb, s.sem
        gap = sb("gap", [P, NCH, TT])
        ratio = sb("ratio", [P, NCH, TT])
        total = sb("total", [P, NCH, TT])
        inv = sb("inv", [P, NCH, TT])
        weight = sb("weight", [P, NCH, 2 * TT])
        w_here = sb("w_here", [P, SUBS, 2 * TT])
        eps = sb("eps", [P, 1])
        x1 = sb("x1", [P, SUBS, TT, C])
        eo = sb("eo", [P, SUBS, 2 * TT, C])
        half_z = sb("half_z", [P, SUBS, TT, C])
        z = sb("z", [P, SUBS, TT, C])
        stats = sb("stats", [P, SUBS, TT, 6])
        moments = sb("moments", [P, SUBS, TT, 2])
        std = sb("std", [P, SUBS, TT])
        rstd = sb("rstd", [P, SUBS, TT])
        shift = sb("shift", [P, SUBS, TT])
        result = sb("result", [P, SUBS, TT, C])

        set_up = sem("set_up")
        gap_done = sem("gap_done")
        ratio_done = sem("ratio_done")
        weights = sem("weights")
        x1_in = [sem(f"x1_in{i}") for i in range(SUBS)]
        gathered = [sem(f"gathered{i}") for i in range(SUBS)]
        w_copied = sem("w_copied")
        half_done = sem("half_done")
        z_done = sem("z_done")
        stats_done = sem("stats_done")
        moments_done = sem("moments_done")
        aggr_due = sem("aggr_due")
        std_done = sem("std_done")
        rstd_done = sem("rstd_done")
        norm_ready = sem("norm_ready")
        result_done = sem("result_done")
        stored = [sem(f"stored{i}") for i in range(SUBS)]
        for free in (*stored, result_done):
            nc.sync.sem_inc(free, FREE)
        block = ctx.enter_context(nc.Block())

        out_dst = out.rearrange("b (i t p) c -> (b i) p t c", p=P, t=TT)

        @block.gpsimd
        def _(pool):
            pool.memset(eps[:], EPS).then_inc(set_up, 1)
            for ci in range(NCH):
                if ci >= SUBS:
                    pool.wait_ge(z_done, TT * (ci - 1))
                for kt in range(2 * TT):
                    pool.indirect_dma_start(
                        eo[:, ci % SUBS, kt, :], None, d["eo"],
                        bass.IndirectOffsetOnAxis(ap=gather_idx[:, ci, kt:kt + 1], axis=0),
                    ).then_inc(gathered[ci % SUBS], 16)

        @block.sync
        def _(sp):
            def load(ci, sub):
                sp.dma_start(x1[:, sub].rearrange("p t c -> p (t c)"), d["x1"][ci]).then_inc(x1_in[sub], 16)

            def body(it, ci, ahead):
                for sub in range(SUBS):
                    if ahead is not None:
                        sp.wait_ge(half_done, it * (SUBS * TT) + TT * (sub + 1))
                        load(ahead[sub], sub)
                    sp.wait_ge(result_done, it * (SUBS * TT) + (TT * (sub + 1) + FREE))
                    sp.dma_start(out_dst[ci[sub]], result[:, sub]).then_inc(stored[sub], 16)

            for sub in range(SUBS):
                load(sub, sub)
            with sp.Fori(0, ITS - 1) as it:
                body(it, [sp.snap(it * SUBS + i) for i in range(SUBS)], [sp.snap(it * SUBS + (SUBS + i)) for i in range(SUBS)])
            body(ITS - 1, [(ITS - 1) * SUBS + i for i in range(SUBS)], None)
            for i in range(SUBS):
                sp.wait_ge(stored[i], 16 * ITS + FREE)

        @block.scalar
        def _(act):
            act.wait_ge(gap_done, 1)
            nc.scalar.activation(ratio[:], gap[:], ACT.Exp).then_inc(ratio_done, 1)
            act.wait_ge(set_up, 1)
            with act.Fori(0, ITS) as it:
                for sub in range(SUBS):
                    act.wait_ge(moments_done, it * (SUBS * TT) + TT * (sub + 1))
                    nc.scalar.activation(std[:, sub], moments[:, sub, :, 1], ACT.Sqrt, bias=eps[:]).then_inc(std_done, 1)
                    act.wait_ge(norm_ready, it * SUBS + (sub + 1))
                    act.wait_ge(stored[sub], it * 16 + FREE)
                    for t in range(TT):
                        nc.scalar.activation(result[:, sub, t], z[:, sub, t], ACT.Identity, bias=shift[:, sub, t:t + 1],
                                             scale=rstd[:, sub, t:t + 1]).then_inc(result_done, 1)

        @block.vector
        def _(dve):
            first, second = top_vals[:, :, 0:TT], top_vals[:, :, TT:2 * TT]
            nc.vector.tensor_tensor(gap[:], second, first, ALU.subtract).then_inc(gap_done, 1)
            dve.wait_ge(ratio_done, 1)
            nc.vector.tensor_scalar(total[:], ratio[:], 1.0, None, ALU.add).then_inc(weights, 1)
            dve.wait_ge(weights, 1)
            nc.vector.reciprocal(inv[:], total[:]).then_inc(weights, 1)
            dve.wait_ge(weights, 2)
            nc.vector.tensor_tensor(ratio[:], ratio[:], inv[:], ALU.mult).then_inc(weights, 1)
            nc.vector.tensor_tensor(weight[:, :, 0:TT], inv[:], kept[:, :, 0:TT], ALU.mult).then_inc(weights, 1)
            dve.wait_ge(weights, 4)
            nc.vector.tensor_tensor(weight[:, :, TT:2 * TT], ratio[:], kept[:, :, TT:2 * TT], ALU.mult).then_inc(weights, 1)
            dve.wait_ge(weights, 5)
            with dve.Fori(0, ITS) as it:
                for sub in range(SUBS):
                    nc.vector.tensor_copy(w_here[:, sub], weight[:, it * SUBS + sub]).then_inc(w_copied, 1)
                    dve.wait_ge(w_copied, it * SUBS + (sub + 1))
                    dve.wait_ge(x1_in[sub], it * 16 + 16)
                    dve.wait_ge(gathered[sub], it * (16 * 2 * TT) + 16 * 2 * TT)
                    dve.wait_ge(result_done, it * (SUBS * TT) + FREE)
                    for t in range(TT):
                        nc.vector.scalar_tensor_tensor(half_z[:, sub, t], eo[:, sub, t], w_here[:, sub, t:t + 1], x1[:, sub, t],
                                                       ALU.mult, ALU.add).then_inc(half_done, 1)
                    for t in range(TT):
                        dve.wait_ge(half_done, it * (SUBS * TT) + (TT * sub + t + 1))
                        nc.vector.scalar_tensor_tensor(z[:, sub, t], eo[:, sub, TT + t], w_here[:, sub, TT + t:TT + t + 1],
                                                       half_z[:, sub, t], ALU.mult, ALU.add).then_inc(z_done, 1)
                    for t in range(TT):
                        dve.wait_ge(z_done, it * (SUBS * TT) + (TT * sub + t + 1))
                        nc.vector.bn_stats(stats[:, sub, t], z[:, sub, t]).then_inc(stats_done, 1)
                    for t in range(TT):
                        dve.wait_ge(stats_done, it * (SUBS * TT) + (TT * sub + t + 1))
                        dve.sem_inc(aggr_due, 1)
                        nc.vector.bn_aggr(moments[:, sub, t], stats[:, sub, t]).then_inc(moments_done, 1)
                    dve.wait_ge(std_done, it * SUBS + (sub + 1))
                    nc.vector.reciprocal(rstd[:, sub], std[:, sub]).then_inc(rstd_done, 1)
                    dve.wait_ge(rstd_done, it * SUBS + (sub + 1))
                    nc.vector.scalar_tensor_tensor(shift[:, sub], moments[:, sub, :, 0], -1.0, rstd[:, sub],
                                                   ALU.mult, ALU.mult).then_inc(norm_ready, 1)


def const_arrays():
    f = np.float32
    inv = (f(1.0) / np.power(f(10000.0), np.arange(0, L, 2, dtype=f) / f(L))).astype(f)
    angle = np.outer(np.arange(T, dtype=f), inv).astype(f)
    cos = np.tile(np.repeat(np.cos(angle), 2, axis=1).T, (HG, 1)).astype(f)
    sin = np.tile(np.repeat(np.sin(angle), 2, axis=1).T, (HG, 1)).astype(f)
    rot = np.zeros((2, P, P), f)
    even = np.arange(0, P, 2)
    rot[0, even, even + 1], rot[0, even + 1, even] = -1.0, 1.0
    rot[1, even + 1, even], rot[1, even, even + 1] = -1.0, 1.0
    row = np.arange(P)
    return {
        "cos": cos, "sin": sin, "rot": rot, "ident": np.eye(P, dtype=f),
        "rev": np.tile(E - np.arange(E, dtype=f), (P, 1)),
        "before": (row[:, None] < row[None, :]).astype(f),
        "fold8": ((row[:, None] % L) == np.arange(E)[None, :]).astype(f),
        "cap": np.tile(np.where(row[None, :] >= row[:, None], 3.0e38, 0.0).astype(f)[:, None, :], (1, 2, 1)), "mask": np.where(row[None, :] > row[:, None], NEG, 0.0).astype(f),
    }


def laid_out(w):
    def blocks(m, n, dtype=np.float32):
        out = np.zeros((m.shape[0] * n, m.shape[1] * n), dtype)
        for i in range(n):
            out[i * m.shape[0]:(i + 1) * m.shape[0], i * m.shape[1]:(i + 1) * m.shape[1]] = m
        return out

    bias = w["L0_attn_c_attn_b"]
    return {
        "x_t": w["L0_attn_x"].reshape(N, C).T,
        "c_attn_w": w["L0_attn_c_attn_w"],
        "wv_t": w["L0_attn_c_attn_w"][2 * C:].T,
        "fold_q": blocks(w["L0_attn_q2l_w"].T, HG),
        "fold_k": blocks(w["L0_attn_kv2l_w"].T, HG),
        "b_cq": bias[0:C].reshape(G, HG * HD).T,
        "b_ck": bias[C:2 * C].reshape(G, HG * HD).T,
        "b_v": np.tile(bias[2 * C:], (P, 1)),
        "b_small": np.stack([np.tile(w[f"L0_attn_{n}_b"], HG) for n in ("q2l", "kv2l", "wqk")], axis=1),
        "wqk_t": blocks(w["L0_attn_wqk_w"].T, HG),
        "x": w["L0_attn_x"].reshape(N, C),
        "l2o": blocks(w["L0_attn_l2o_w"].T, HG),
        "kv2l": blocks(w["L0_attn_kv2l_w"], HG),
        "kv2l_b": np.tile(w["L0_attn_kv2l_b"], HG)[:, None],
        "l2o_b": np.tile(w["L0_attn_l2o_b"], HG)[:, None],
        "cproj_t": w["L0_attn_cproj_w"].T,
        "cproj_b": np.tile(w["L0_attn_cproj_b"], (P, 1)),
        "rw1": w["L0_ffn_rw1"], "rw2": w["L0_ffn_rw2"],
        "rb1": w["L0_ffn_rb1"].reshape(MC, P).T,
        "rb2": np.tile(w["L0_ffn_rb2"], (P, TT, 1)),
        "ew1": w["L0_ffn_ew1"], "ew2": w["L0_ffn_ew2"],
        "eb1": w["L0_ffn_eb1"].reshape(E, MC, P).transpose(0, 2, 1),
        "eb2": np.tile(w["L0_ffn_eb2"][:, None, :], (1, P, 1)),
    }


def program(nc, a, out):
    def scratch(name, shape, dt=F32):
        return nc.dram_tensor(name, shape, dt, kind="Internal").ap()

    d = {
        "qk": scratch("qk_parts", (SLOTS + 1, NC, 4, P, CH)),
        "v": scratch("v_tokens", (SLOTS + 1, NC, P, TT, HG * L)),
        "y": scratch("y_heads", (B, NC, P, TT, C)),
    }
    d |= {
        "x1": scratch("x1_rows", (B * NC, P, TT * C)),
        "disp": scratch("dispatched", (E * CAP, C)),
        "eo": scratch("expert_out", (E * CAP, C)),
    }
    with ExitStack() as ctx:
        keep = Scope(nc, ctx, "keep")
        keep_on_chip = (keep.sb("gather_idx", [P, B * NC, 2 * TT], U32), keep.sb("kept", [P, B * NC, 2 * TT]),
                        keep.sb("top_vals", [P, B * NC, 2 * TT]))
        project_heads(nc, a, d)
        attend(nc, a, d)
        mix_and_route(nc, a, d, keep_on_chip)
        experts(nc, a, d)
        combine(nc, a, d, keep_on_chip, out)


def kernel(**inputs):
    import concourse.bacc as bacc
    from concourse.bass_utils import run_bass_kernel_spmd

    nc = bacc.Bacc("TRN2", target_bir_lowering=False, num_devices=1)
    arrays = {**laid_out({k: np.asarray(v) for k, v in inputs.items()}), **const_arrays()}
    arrays = {f"in_{n}": np.ascontiguousarray(v) for n, v in arrays.items()}
    a = {n[3:]: nc.dram_tensor(n, v.shape, mybir.dt.from_np(v.dtype), kind="ExternalInput").ap()
         for n, v in arrays.items()}
    out = nc.dram_tensor("out_0", (B, T, C), F32, kind="ExternalOutput").ap()
    program(nc, a, out)
    r = run_bass_kernel_spmd(nc, [arrays], core_ids=[0])
    return r.results[0]["out_0"]
```

```python
from contextlib import ExitStack

import numpy as np
import concourse.bass as bass
from concourse import mybir

F32 = mybir.dt.float32
F32R = mybir.dt.float32r
BF16 = mybir.dt.bfloat16
U32 = mybir.dt.uint32
ALU = mybir.AluOpType
ACT = mybir.ActivationFunctionType
AX = mybir.AxisListType

P = 128
B, T, C = 4, 2048, 256
N = B * T
H, HD, L = 16, 16, 32
HG = P // L
G = H // HG
CH = 512
NC = T // CH
TT = CH // P
KC = C // P
SLOTS = B * G
SCALE = float(L) ** -0.5
E, CAP, HID = 8, 1024, 1024
MC = HID // P
NEG = -1.0e30
FREE = 1


class Scope:

    def __init__(self, nc, ctx, stage):
        self.nc, self.ctx, self.stage = nc, ctx, stage

    def sb(self, name, shape, dt=F32):
        return self.ctx.enter_context(self.nc.sbuf_tensor(f"{self.stage}_{name}", shape, dt))

    def ps(self, name, shape, dt=F32):
        return self.ctx.enter_context(self.nc.psum_tensor(f"{self.stage}_{name}_bank", shape, dt))

    def sem(self, name):
        return self.ctx.enter_context(self.nc.semaphore(f"{self.stage}_{name}"))


def project_heads(nc, a, d):
    NU = NC * G
    LAG = 2
    OPS = 4
    with ExitStack() as ctx:
        s = Scope(nc, ctx, "proj")
        sb, ps, sem = s.sb, s.ps, s.sem
        cq = sb("cq", [64, G, C])
        ck = sb("ck", [64, G, C])
        wv = sb("wv", [P, KC, C])
        fold_q = sb("fold_q", [64, P])
        fold_k = sb("fold_k", [64, P])
        b_cq = sb("b_cq", [64, G])
        b_ck = sb("b_ck", [64, G])
        b_small = sb("b_small", [P, 3])
        b_v = sb("b_v", [P, C])
        wqk = sb("wqk", [P, P])
        rot = sb("rot", [P, 2, P])
        cos = sb("cos", [P, T])
        sin = sb("sin", [P, T])
        b_q = sb("b_q", [P, G])
        b_k = sb("b_k", [P, G])
        b_qk = sb("b_qk", [P, 1])
        zeros = sb("zeros", [P, CH])
        lat_high = [sb(f"{x}_lat_high", [P, KC, G, P], F32R) for x in "qk"]
        lat_low = [sb(f"{x}_lat_low", [P, KC, G, P], F32R) for x in "qk"]
        wv_high = sb("wv_high", [P, KC, C], F32R)
        wv_low = sb("wv_low", [P, KC, C], F32R)
        wqk_high = sb("wqk_high", [P, 2, P], F32R)
        wqk_low = sb("wqk_low", [P, 2, P], F32R)
        rot_r = sb("rot_r", [P, P], F32R)
        xt = sb("xt", [P, 2, KC, CH])
        x_high = sb("x_high", [P, 2, KC, CH], F32R)
        x_low = sb("x_low", [P, 2, KC, CH], F32R)
        turned = sb("turned", [P, 2, 3, CH])
        op_high = sb("op_high", [P, OPS, 3, CH], F32R)
        op_low = sb("op_low", [P, OPS, 3, CH], F32R)
        k_cos = sb("k_cos", [P, OPS, CH])
        q_full = sb("q_full", [P, 2, CH])
        k_full = sb("k_full", [P, 2, CH])
        parts = sb("parts", [P, 2, 4, CH], F32R)
        v_tok = sb("v_tok", [P, 2, TT, H, L])
        lat = [[ps(f"lat{i}{x}", [P, CH]) for x in "qk"] for i in range(2)]
        fin_q = ps("fin_q", [P, CH])
        fin_k = ps("fin_k", [P, CH])
        v_ps = [ps(f"v{i}", [P, 2, C]) for i in range(2)]

        fold_in = sem("fold_in")
        consts_in = sem("consts_in")
        filled = sem("filled")
        folded = sem("folded")
        weights_ready = sem("weights_ready")
        zeros_out = sem("zeros_out")
        xt_in = [sem(f"xt_in{i}") for i in range(2)]
        x_high_done = sem("x_high_done")
        x_split = sem("x_split")
        high_weights = sem("high_weights")
        lat_ready = sem("lat_ready")
        highs_done = sem("highs_done")
        lows_done = sem("lows_done")
        roped = sem("roped")
        fin_q_ready = sem("fin_q_ready")
        fin_k_ready = sem("fin_k_ready")
        q_done = sem("q_done")
        k_full_done = sem("k_full_done")
        k_high_done = sem("k_high_done")
        parts_done = sem("parts_done")
        parts_out = [sem(f"parts_out{i}") for i in range(2)]
        v_ready = sem("v_ready")
        v_copied = sem("v_copied")
        v_out = [sem(f"v_out{i}") for i in range(2)]
        for free in (q_done, k_full_done, *parts_out, *v_out):
            nc.sync.sem_inc(free, FREE)
        for free, buffers in ((fin_q_ready, OPS), (fin_k_ready, OPS), (parts_done, 2), (k_high_done, 2), (v_copied, 2)):
            nc.sync.sem_inc(free, buffers)
        block = ctx.enter_context(nc.Block())

        loads = [
            (cq[:], a["c_attn_w"][0:C].rearrange("(g r) c -> r g c", r=64)),
            (ck[:], a["c_attn_w"][C:2 * C].rearrange("(g r) c -> r g c", r=64)),
            (fold_q[:], a["fold_q"]), (fold_k[:], a["fold_k"]), (b_cq[:], a["b_cq"]), (b_ck[:], a["b_ck"]),
            (wqk[:], a["wqk_t"]), (rot[:], a["rot"].rearrange("m p n -> p m n")),
            (wv[:], a["wv_t"].rearrange("(k p) n -> p k n", p=P)),
            (b_small[:], a["b_small"]), (b_v[:], a["b_v"]), (cos[:], a["cos"]), (sin[:], a["sin"]),
        ]
        FOLD_LOADS = 9
        xt_src = a["x_t"].rearrange("(k p) (i n) -> i p k n", p=P, n=CH)

        WEIGHTS = 11

        def after(c, k):
            return c[0], c[1] + k

        def units(c, per, plus=0, bufs=1):
            return c[0] * (NU // bufs * per) + (c[1] // bufs * per + plus)

        def chunks(c, per, plus=0, bufs=1):
            return c[0] * (NC // bufs * per) + (c[1] // G // bufs * per + plus)

        def run_units(engine, step):
            for r in range(LAG + 1):
                step((0, r))
            with engine.Fori(0, B - 1) as seq:
                for r in range(LAG + 1, NU + LAG + 1):
                    step((seq, r))
            for r in range((B - 1) * NU + LAG + 1, B * NU):
                step((0, r))

        LAST = [(0, B * NU - LAG + i) for i in range(LAG)]

        def has_chunk(c, ahead):
            return not isinstance(c[0], int) or c[1] // G + ahead < B * NC

        @block.gpsimd
        def _(pool):
            def load(chunk, buf):
                pool.dma_start(xt[:, buf], xt_src[chunk]).then_inc(xt_in[buf], 16)

            def low_x(c):
                buf = c[1] // G % 2
                more = has_chunk(c, 2)
                if more:
                    nxt = c[0] * NC + (c[1] // G + 2)
                    nxt = nxt if isinstance(nxt, int) else pool.snap(nxt)
                pool.wait_ge(x_high_done, chunks(c, 1, 1))
                nc.gpsimd.tensor_tensor(x_low[:, buf], xt[:, buf], x_high[:, buf].bitcast(F32),
                                        ALU.subtract).then_inc(x_split, 1)
                if more:
                    pool.wait_ge(x_split, chunks(c, 1, 1))
                    load(nxt, buf)

            def step(c):
                if c[1] % G == 0 and has_chunk(c, 1):
                    low_x(after(c, G))
                for i in range(3):
                    pool.wait_ge(highs_done, units(c, 3, i + 1))
                    nc.gpsimd.tensor_tensor(op_low[:, c[1] % OPS, i], turned[:, c[1] % 2, i],
                                            op_high[:, c[1] % OPS, i].bitcast(F32), ALU.subtract).then_inc(lows_done, 1)

            load(0, 0)
            load(1, 1)
            low_x((0, 0))
            run_units(pool, step)

        @block.sync
        def _(sp):
            for dst, src in loads[:FOLD_LOADS]:
                sp.dma_start(dst, src).then_inc(fold_in, 16)
            for dst, src in loads[FOLD_LOADS:]:
                sp.dma_start(dst, src).then_inc(consts_in, 16)
            sp.wait_ge(filled, 1)
            for c in range(NC):
                for f in range(4):
                    sp.dma_start(d["qk"][SLOTS, c, f], zeros[:]).then_inc(zeros_out, 16)
                sp.dma_start(d["v"][SLOTS, c].rearrange("p t n -> p (t n)"), zeros[:]).then_inc(zeros_out, 16)
            with sp.Fori(0, B) as seq:
                slot = [sp.snap(seq * G + g) for g in range(G)]
                for r in range(NU):
                    chunk, g = divmod(r, G)
                    sp.wait_ge(parts_done, units((seq, r), 1, 1 + 2))
                    sp.dma_start(d["qk"][slot[g], chunk].rearrange("f p n -> p f n"),
                                 parts[:, r % 2].bitcast(F32)).then_inc(parts_out[r % 2], 16)
                    if g == G - 1:
                        sp.wait_ge(v_copied, chunks((seq, r), 2, 2 + 2))
                        for g in range(G):
                            sp.dma_start(d["v"][slot[g], chunk],
                                         v_tok[:, chunk % 2, :, g * HG:(g + 1) * HG, :].rearrange("p t j l -> p t (j l)"),
                                         ).then_inc(v_out[chunk % 2], 16)
            sp.wait_ge(zeros_out, 16 * 5 * NC)
            for i in range(2):
                sp.wait_ge(parts_out[i], 16 * B * NU // 2 + FREE)
                sp.wait_ge(v_out[i], 16 * G * B * NC // 2 + FREE)

        @block.tensor
        def _(pe):
            pe.wait_ge(fold_in, 16 * FOLD_LOADS)
            for k in range(KC):
                for x, (c_w, fold) in enumerate(((cq, fold_q), (ck, fold_k))):
                    for g in range(G):
                        last = nc.tensor.matmul(lat[x][k][:, g * P:(g + 1) * P], c_w[:, g, k * P:(k + 1) * P],
                                                fold[:], start=True, stop=True)
            last.then_inc(folded, 1)
            nc.tensor.matmul(fin_q[:, 0:G], fold_q[:], b_cq[:], start=True, stop=True)
            nc.tensor.matmul(fin_q[:, G:2 * G], fold_k[:], b_ck[:], start=True, stop=True)
            nc.tensor.matmul(fin_k[:, 0:P], rot[:, 0], wqk[:], start=True, stop=True).then_inc(folded, 1)
            pe.wait_ge(weights_ready, WEIGHTS)

            def product(out, terms):
                for i, (w, x) in enumerate(terms):
                    last = nc.tensor.matmul(out, w, x, start=(i == 0), stop=(i == len(terms) - 1))
                return last

            def latents(c):
                g, buf = c[1] % G, c[1] // G % 2
                if g == 0:
                    pe.wait_ge(x_split, chunks(c, 1, 1))
                if c[1] >= 2:
                    pe.wait_ge(roped, units(c, 4, -4))
                for x in range(2):
                    product(lat[c[1] % 2][x][:], [
                        (w[:, k, g, :], xs[:, buf, k, :]) for k in range(KC) for w, xs in
                        ((lat_high[x], x_high), (lat_high[x], x_low), (lat_low[x], x_high))]).then_inc(lat_ready, 1)

            def finish(c):
                high, low = op_high[:, c[1] % OPS], op_low[:, c[1] % OPS]
                pe.wait_ge(lows_done, units(c, 3, 2))
                pe.wait_ge(q_done, units(c, 1, FREE))
                product(fin_q[:], [(w[:, i, :], x[:, i]) for i in range(2) for w, x in
                                   ((wqk_high, high), (wqk_high, low), (wqk_low, high))]).then_inc(fin_q_ready, 1)
                pe.wait_ge(lows_done, units(c, 3, 3))
                pe.wait_ge(k_full_done, units(c, 1, FREE))
                product(fin_k[:], [(rot_r[:], high[:, 2]), (rot_r[:], low[:, 2])]).then_inc(fin_k_ready, 1)

            def values(c):
                buf = c[1] // G % 2
                for pair in range(2):
                    pe.wait_ge(v_copied, chunks(c, 2, pair + 1))
                    for t in range(2):
                        at = slice((2 * pair + t) * P, (2 * pair + t + 1) * P)
                        last = product(v_ps[pair][:, t, :], [
                            (xs[:, buf, k, at], w[:, k, :]) for k in range(KC) for xs, w in
                            ((x_high, wv_high), (x_high, wv_low), (x_low, wv_high))])
                    last.then_inc(v_ready, 1)

            def step(c):
                latents(c)
                if c[1] >= LAG:
                    finish(after(c, -LAG))
                if c[1] % G == G - 1:
                    values(c)

            run_units(pe, step)
            for c in LAST:
                finish(c)

        @block.scalar
        def _(act):
            def high_x(c):
                buf = c[1] // G % 2
                act.wait_ge(xt_in[buf], chunks(c, 16, 16, bufs=2))
                if c[1] >= 2 * G:
                    act.wait_ge(v_ready, chunks(c, 2, -2))
                nc.scalar.activation(x_high[:, buf], xt[:, buf], ACT.Copy).then_inc(x_high_done, 1)

            def finish(c):
                par = c[1] % 2
                act.wait_ge(fin_q_ready, units(c, 1, 1 + OPS))
                act.wait_ge(parts_out[par], units(c, 16, FREE, bufs=2))
                act.wait_ge(parts_done, units(c, 1, 1))
                nc.scalar.activation(q_full[:, par], fin_q[:], ACT.Identity, bias=b_qk[:], scale=SCALE)
                nc.scalar.activation(parts[:, par, 0], fin_q[:], ACT.Identity, bias=b_qk[:],
                                     scale=SCALE).then_inc(q_done, 1)
                act.wait_ge(k_full_done, units(c, 1, 1 + FREE))
                nc.scalar.activation(parts[:, par, 2], k_full[:, par], ACT.Copy).then_inc(k_high_done, 1)

            def step(c):
                if c[1] % G == 0 and has_chunk(c, 1):
                    high_x(after(c, G))
                act.wait_ge(fin_k_ready, units(c, 1, 1))
                for i, roped_by in enumerate((1, 2, 4)):
                    act.wait_ge(roped, units(c, 4, roped_by))
                    nc.scalar.activation(op_high[:, c[1] % OPS, i], turned[:, c[1] % 2, i], ACT.Copy).then_inc(highs_done, 1)
                if c[1] >= LAG:
                    finish(after(c, -LAG))

            high_x((0, 0))
            act.wait_ge(consts_in, 16 * (len(loads) - FOLD_LOADS))
            nc.scalar.mul(b_qk[:], b_small[:, 2:3], SCALE).then_inc(weights_ready, 1)
            act.wait_ge(weights_ready, WEIGHTS)
            run_units(act, step)
            for c in LAST:
                finish(c)

        @block.vector
        def _(dve):
            nc.vector.memset(zeros[:], 0.0).then_inc(filled, 1)
            nc.vector.memset(v_tok[:], 0.0).then_inc(filled, 1)
            dve.wait_ge(filled, 2)
            nc.vector.memset(v_tok[:, :, :, :, HD:HD + 1], 1.0).then_inc(filled, 1)
            dve.wait_ge(fold_in, 16 * FOLD_LOADS)
            dve.wait_ge(folded, 2)
            split = [(lat_high[x][:, k].rearrange("p g n -> p (g n)"), lat_low[x][:, k].rearrange("p g n -> p (g n)"),
                      lat[x][k][:]) for x in range(2) for k in range(KC)]
            split += [(wqk_high[:, 0], wqk_low[:, 0], wqk[:]), (wqk_high[:, 1], wqk_low[:, 1], fin_k[:, 0:P]),
                      (wv_high[:], wv_low[:], wv[:])]
            for high, _, src in split:
                nc.vector.tensor_copy(high, src).then_inc(high_weights, 1)
            nc.vector.tensor_copy(rot_r[:], rot[:, 1]).then_inc(weights_ready, 1)
            for i, (high, low, src) in enumerate(split):
                dve.wait_ge(high_weights, i + 1)
                nc.vector.tensor_tensor(low, src, high.bitcast(F32), ALU.subtract).then_inc(weights_ready, 1)
            dve.wait_ge(consts_in, 16 * (len(loads) - FOLD_LOADS))
            nc.vector.tensor_scalar(b_q[:], fin_q[:, 0:G], b_small[:, 0:1], None, ALU.add).then_inc(weights_ready, 1)
            nc.vector.tensor_scalar(b_k[:], fin_q[:, G:2 * G], b_small[:, 1:2], None, ALU.add).then_inc(weights_ready, 1)
            dve.wait_ge(filled, 3)
            dve.wait_ge(weights_ready, WEIGHTS)

            def rope(c):
                g, par = c[1] % G, c[1] % 2
                at = slice(c[1] // G % NC * CH, (c[1] // G % NC + 1) * CH)
                outs = ((0, b_q, cos, turned[:, par, 0]), (0, b_q, sin, turned[:, par, 1]),
                        (1, b_k, cos, k_cos[:, c[1] % OPS]), (1, b_k, sin, turned[:, par, 2]))
                for i, (x, bias, table, dst) in enumerate(outs):
                    if i % 2 == 0:
                        dve.wait_ge(lat_ready, units(c, 2, x + 1))
                    if c[1] >= 2 and i != 2:
                        dve.wait_ge(lows_done, units(c, 3, -6 + (1, 2, None, 3)[i]))
                    nc.vector.scalar_tensor_tensor(dst, lat[par][x][:], bias[:, g:g + 1], table[:, at],
                                                   ALU.add, ALU.mult).then_inc(roped, 1)

            def finish(c):
                par = c[1] % 2
                dve.wait_ge(fin_k_ready, units(c, 1, 1 + OPS))
                dve.wait_ge(k_high_done, units(c, 1, 1))
                nc.vector.tensor_tensor(k_full[:, par], fin_k[:], k_cos[:, c[1] % OPS], ALU.add).then_inc(k_full_done, 1)

            def low_parts(c):
                par = c[1] % 2
                dve.wait_ge(q_done, units(c, 1, 1 + FREE))
                nc.vector.tensor_tensor(parts[:, par, 1], q_full[:, par], parts[:, par, 0].bitcast(F32), ALU.subtract)
                dve.wait_ge(k_high_done, units(c, 1, 1 + 2))
                nc.vector.tensor_tensor(parts[:, par, 3], k_full[:, par], parts[:, par, 2].bitcast(F32),
                                        ALU.subtract).then_inc(parts_done, 1)

            def values(c):
                buf = c[1] // G % 2
                for pair in range(2):
                    dve.wait_ge(v_ready, chunks(c, 2, pair + 1))
                    dve.wait_ge(v_out[buf], chunks(c, 16 * G, FREE, bufs=2))
                    for t in range(2):
                        last = nc.vector.tensor_tensor(
                            v_tok[:, buf, 2 * pair + t, :, 0:HD],
                            v_ps[pair][:, t, :].rearrange("p (h e) -> p h e", e=HD),
                            b_v[:].rearrange("p (h e) -> p h e", e=HD), ALU.add)
                    last.then_inc(v_copied, 1)

            def step(c):
                rope(c)
                if c[1] > LAG:
                    low_parts(after(c, -LAG - 1))
                if c[1] >= LAG:
                    finish(after(c, -LAG))
                if c[1] % G == G - 1:
                    values(c)

            run_units(dve, step)
            low_parts(after(LAST[0], -1))
            for c in LAST:
                finish(c)
                low_parts(c)


KS = [(p, c, kt) for p in range(2) for c in range(NC) for kt in range(TT * (c + 1))]
KSG = len(KS) // 2
MU = [(c, j, t, kb) for c in range(NC) for j in range(HG) for t in range(TT) for kb in range(c + 1)]
MUG = len(MU)
PER_STEP = MUG // KSG
LEAD = 5 * HG * TT
CHUNK_END = [TT * (c + 1) * (c + 2) // 2 for c in range(NC)]
MU_END = [HG * TT * (c + 1) * (c + 2) // 2 for c in range(NC)]


def maxima_ending(k):
    done = LEAD + PER_STEP * (k + 1)
    group, rest = divmod(done, MUG)
    if rest == 0:
        return NC * group - 1
    return NC * group + MU_END.index(rest) if rest in MU_END else None


def attend(nc, a, d):
    ITS = SLOTS // 2
    NK = len(KS)
    with ExitStack() as ctx:
        s = Scope(nc, ctx, "att")
        sb, ps, sem = s.sb, s.ps, s.sem
        q_st = sb("q_st", [98, NC, HG, CH], F32R)
        k_st = sb("k_st", [98, 2, NC, HG, CH], F32R)
        v_st = sb("v_st", [P, 2, NC, TT, HG * L])
        probs = sb("probs", [P, 4, HG, CH])
        mask_f = sb("mask_f", [P, P])
        mask = sb("mask", [P, P], BF16)
        ident_b = sb("ident_b", [P, P], BF16)
        ident = sb("ident", [P, P])
        partial_max = sb("partial_max", [P, 2, HG * TT, NC])
        neg_max = sb("neg_max", [P, 2, HG * TT])
        max_high = sb("max_high", [HG * TT, 2, P], F32R)
        max_low = sb("max_low", [HG * TT, 2, P], F32R)
        y_raw = sb("y_raw", [P, 2, CH])
        recip = sb("recip", [P, TT, HG])
        y = sb("y", [P, 2, TT, HG, HD])
        score_ps = [ps(f"score{i}", [P, CH]) for i in range(3)]
        max_ps = [ps(f"max{i}", [P, CH]) for i in range(3)]
        acc = ps("acc", [P, CH])
        misc = ps("misc", [P, CH])

        consts_in = sem("consts_in")
        mask_set = sem("mask_set")
        ones_set = sem("ones_set")
        loaded = [sem(f"loaded{c}") for c in range(NC)]
        unit_scored = sem("unit_scored")
        unit_reduced = sem("unit_reduced")
        max_combined = sem("max_combined")
        misc_ready = sem("misc_ready")
        max_split = sem("max_split")
        high_done = sem("high_done")
        shift_in = [sem(f"shift_in{i}") for i in range(2)]
        scored = sem("scored")
        exped = sem("exped")
        masked = sem("masked")
        edge_due = sem("edge_due")
        weighted = sem("weighted")
        acc_read = sem("acc_read")
        recip_done = sem("recip_done")
        y_done = sem("y_done")
        y_out = [sem(f"y_out{i}") for i in range(2)]
        for free in (y_done, max_split, *y_out):
            nc.sync.sem_inc(free, FREE)
        block = ctx.enter_context(nc.Block())

        loads = [(mask_f[:], a["mask"]), (ident[:], a["ident"])]
        qk_src = d["qk"].rearrange("s c f (j p) n -> s c f p j n", p=L)
        MISC_BODY = 2 * NC * 2
        MISC_HEAD = 2

        def misc_uses():
            out = []
            for k in range(NK):
                if k and maxima_ending(k - 1) is not None:
                    out.append(("max", maxima_ending(k - 1)))
                n = sums_at(k)
                if n is not None:
                    out.append(("sum", n))
            if maxima_ending(NK - 1) is not None:
                out.append(("max", maxima_ending(NK - 1)))
            out.append(("sum", 2 * NC - 1))
            return out

        def sums_at(k):
            p, r = divmod(k - 2, KSG)
            if r == 0:
                return NC - 1 if p == 1 else None
            return NC * p + CHUNK_END.index(r) if r in CHUNK_END[:-1] else None

        def max_bank(u):
            return (u - LEAD) % 3

        uses = misc_uses()
        assert len(uses) == MISC_BODY, uses

        def first_of_chunk(k):
            return KS[k][2] == 0

        def chunk_step(k):
            return NC * KS[k][0] + KS[k][1]

        def last_step(n):
            return (n // NC) * KSG + CHUNK_END[n % NC]

        def load(sp, slot, par, c):
            for dst, f in ((q_st[0:L, c], 0), (q_st[L:2 * L, c], 0), (q_st[2 * L:3 * L, c], 1),
                           (k_st[0:L, par, c], 2), (k_st[L:2 * L, par, c], 3), (k_st[2 * L:3 * L, par, c], 2)):
                sp.dma_start(dst.bitcast(F32), qk_src[slot, c, f]).then_inc(loaded[c], 16)
            sp.dma_start(v_st[:, par, c], d["v"][slot, c]).then_inc(loaded[c], 16)

        def put_shift(sp, m):
            for row, src in ((3 * L, max_high), (3 * L + 1, max_low)):
                sp.dma_start(q_st[row:row + 1, m % NC].rearrange("p j (t n) -> p (j t) n", n=P).bitcast(F32),
                             src[:, m % 2].bitcast(F32)).then_inc(shift_in[m % 2], 16)

        @block.sync
        def _(sp):
            for dst, src in loads:
                sp.dma_start(dst, src).then_inc(consts_in, 16)
            for c in range(NC):
                load(sp, 0, 0, c)
            for m in range(2):
                sp.wait_ge(max_split, m + 1 + FREE)
                put_shift(sp, m)
            with sp.Fori(0, B) as b, sp.Fori(0, G // 2) as gp:
                it = sp.snap(b * (G // 2) + gp)
                slot = [sp.snap(it * 2 + p) for p in range(3)]
                cols = [sp.snap(gp * (2 * HG * HD) + p * (HG * HD)) for p in range(2)]
                for k in range(NK + 1):
                    n = chunk_step(k - 1) if k else None
                    if k and (k == NK or first_of_chunk(k)):
                        sp.wait_ge(weighted, it * NK + k)
                        load(sp, slot[n // NC + 1], (n // NC + 1) % 2, n % NC)
                    m = maxima_ending(k - 1) if k else None
                    if m is not None:
                        sp.wait_ge(max_split, it * (2 * NC) + (m + 1 + FREE))
                        put_shift(sp, m)
                    n = 2 * NC - 1 if k == NK else sums_at(k)
                    if n is not None:
                        sp.wait_ge(y_done, it * (2 * NC) + (n + 1 + FREE))
                        sp.dma_start(d["y"][b, n % NC, :, :, bass.ds(cols[n // NC], HG * HD)],
                                     y[:, n % 2].rearrange("p t j e -> p t (j e)")).then_inc(y_out[n % 2], 16)
            for i in range(2):
                sp.wait_ge(y_out[i], 16 * ITS * NC + FREE)
            for c in range(NC):
                sp.wait_ge(loaded[c], 112 * (SLOTS + 1))
            for i in range(2):
                sp.wait_ge(shift_in[i], 32 * (ITS * NC + 1))

        @block.tensor
        def _(pe):
            def max_unit(base, u, wait_free=True):
                group, r = divmod(u, MUG)
                c, j, t, kb = MU[r]
                par = group % 2
                if r == 0 or MU[r - 1][0] != c:
                    pe.wait_ge(loaded[c], base * (2 * 112) + 112 * (group + 1))
                if wait_free:
                    pe.wait_ge(unit_reduced, base * (2 * MUG) + (u - 1 if (u - LEAD) % (2 * MUG) < 2 else u - 2))
                width = CH if kb < c else (t + 1) * P
                out = max_ps[max_bank(u)]
                last = nc.tensor.matmul(out[:, 0:width], q_st[0:3 * L, c, j, t * P:(t + 1) * P],
                                        k_st[0:3 * L, par, kb, j, 0:width], start=True, stop=(kb < c))
                if kb == c:
                    last = nc.tensor.matmul(out[:, width - P:width], ident_b[:], mask[:], start=False, stop=True)
                last.then_inc(unit_scored, 1)

            def misc_free(it, use):
                before = [what for what, _ in uses[:max(use - MISC_HEAD, 0)]]
                if use:
                    pe.wait_ge(max_split, it * (2 * NC) + ((min(use, MISC_HEAD) + before.count("max")) + FREE))
                if use >= MISC_HEAD:
                    pe.wait_ge(y_done, it * (2 * NC) + (before.count("sum") + FREE))

            def transpose_max(it, m, use):
                pe.wait_ge(max_combined, it * (2 * NC) + (m + 1))
                misc_free(it, use)
                nc.tensor.transpose(misc[0:HG * TT, 0:P], neg_max[:, m % 2], ident[:]).then_inc(misc_ready, 1)

            def turn_sums(it, n, use):
                pe.wait_ge(acc_read, it * (2 * NC) + (n + 1))
                misc_free(it, use)
                for t in range(TT):
                    last = nc.tensor.transpose(misc[:, t * P:(t + 1) * P], y_raw[:, n % 2, t * P:(t + 1) * P], ident[:])
                last.then_inc(misc_ready, 1)

            def exps_through(h):
                return exps_next + (h - HG * NK)

            def score(it, k, j):
                p, c, kt = KS[k % NK]
                n = NC * p + c + 2 * NC * (k // NK)
                h = HG * k + j
                if kt == 0 and j == 0:
                    pe.wait_ge(shift_in[n % 2], it * (32 * NC) + 32 * (n // 2 + 1))
                if h >= 3:
                    pe.wait_ge(exped, exps_through(h - 1 if k == NK and j < 2 else h - 2))
                q0 = max(kt - TT * c, 0) * P
                nc.tensor.matmul(score_ps[h % (HG * NK) % 3][:, q0:CH],
                                 k_st[:, p, kt // TT, j, (kt % TT) * P:(kt % TT + 1) * P],
                                 q_st[:, c, j, q0:CH], start=True, stop=True).then_inc(scored, 1)

            def weigh(it, k):
                p, c, kt = KS[k]
                diag = kt >= TT * c
                pe.wait_ge(exped, exps_through(HG * (k + 1)))
                if diag:
                    before = (NC * p + c) * TT + (kt - TT * c)
                    pe.wait_ge(masked, it * (2 * NC * TT) + (before + 1))
                if kt == 0 and k:
                    pe.wait_ge(acc_read, it * (2 * NC) + (NC * p + c))
                q0 = max(kt - TT * c, 0) * P
                for j in range(HG):
                    last = nc.tensor.matmul(acc[j * L:(j + 1) * L, q0:CH], v_st[:, p, kt // TT, kt % TT, j * L:(j + 1) * L],
                                            probs[:, k % 4, j, q0:CH], start=(kt == 0), stop=(kt == TT * (c + 1) - 1),
                                            skip_group_check=True)
                last.then_inc(weighted, 1)

            pe.wait_ge(consts_in, 16 * len(loads))
            pe.wait_ge(mask_set, 2)
            for u in range(LEAD):
                max_unit(0, u, wait_free=(u >= 2))
                if u + 1 in MU_END:
                    m = MU_END.index(u + 1)
                    transpose_max(0, m, m)
            pe.wait_ge(ones_set, 1)
            for j in range(HG - 1):
                score(0, 0, j)
            with pe.Fori(0, ITS) as it:
                use = 0
                exps_next = pe.snap((it + 1) * (HG * NK))
                score(it, 0, HG - 1)
                for k in range(NK):
                    for j in range(HG):
                        if k < NK - 1 or j < HG - 1:
                            score(it, k + 1, j)
                        if k < NK - 1:
                            max_unit(it, LEAD + PER_STEP * k + j)
                    if k and maxima_ending(k - 1) is not None:
                        transpose_max(it, maxima_ending(k - 1), MISC_HEAD + use)
                        use += 1
                    weigh(it, k)
                    if k == NK - 1:
                        for j in range(HG):
                            max_unit(it, LEAD + PER_STEP * k + j)
                    if sums_at(k) is not None:
                        turn_sums(it, sums_at(k), MISC_HEAD + use)
                        use += 1
                if maxima_ending(NK - 1) is not None:
                    transpose_max(it, maxima_ending(NK - 1), MISC_HEAD + use)
                    use += 1
                turn_sums(it, 2 * NC - 1, MISC_HEAD + use)

        @block.scalar
        def _(act):
            def read_acc(it, n):
                act.wait_ge(weighted, it * NK + last_step(n))
                act.wait_ge(y_done, it * (2 * NC) + (max(n - 1, 0) + FREE))
                nc.scalar.activation(y_raw[:, n % 2], acc[:], ACT.Copy).then_inc(acc_read, 1)

            with act.Fori(0, ITS) as it:
                for k in range(NK):
                    p, c, kt = KS[k]
                    q0 = max(kt - TT * c, 0) * P
                    if k >= 4:
                        act.wait_ge(weighted, it * NK + (k - 3))
                    for j in range(HG):
                        act.wait_ge(scored, it * (HG * NK) + (HG * k + j + 1))
                        nc.scalar.activation(probs[:, k % 4, j, q0:CH], score_ps[(HG * k + j) % 3][:, q0:CH],
                                             ACT.Exp).then_inc(exped, 1)
                    if k and first_of_chunk(k):
                        read_acc(it, chunk_step(k) - 1)
                read_acc(it, 2 * NC - 1)

        @block.gpsimd
        def _(pool):
            nc.gpsimd.memset(k_st[3 * L:3 * L + 2].bitcast(F32), 1.0).then_inc(ones_set, 1)
            zero = pool.to_reg(0.0)
            with pool.Fori(0, ITS) as it:
                for k in range(NK):
                    p, c, kt = KS[k]
                    if kt < TT * c:
                        continue
                    q0 = (kt - TT * c) * P
                    pool.wait_ge(exped, it * (HG * NK) + HG * (k + 1))
                    pool.sem_inc(edge_due, 1)
                    edge = probs[:, k % 4, :, q0:q0 + P]
                    nc.gpsimd.affine_select(out=edge, in_=edge, pattern=[[0, HG], [1, P]], compare_op=ALU.is_ge,
                                            fill=zero, base=0, channel_multiplier=-1).then_inc(masked, 1)

        @block.vector
        def _(dve):
            dve.wait_ge(consts_in, 16 * len(loads))
            nc.vector.tensor_copy(mask[:], mask_f[:]).then_inc(mask_set, 1)
            nc.vector.tensor_copy(ident_b[:], ident[:]).then_inc(mask_set, 1)

            def reduce_unit(base, u):
                r = u % MUG
                c, j, t, kb = MU[r]
                m = NC * (u // MUG) + c
                width = CH if kb < c else (t + 1) * P
                dve.wait_ge(unit_scored, base * (2 * MUG) + (u + 1))
                nc.vector.tensor_reduce(partial_max[:, m % 2, j * TT + t, kb:kb + 1], max_ps[max_bank(u)][:, 0:width],
                                        AX.X, ALU.max).then_inc(unit_reduced, 1)

            def combine_max(base, m, units):
                dve.wait_ge(unit_reduced, base * (2 * MUG) + units)
                if m >= 2:
                    dve.wait_ge(max_split, base * (2 * NC) + (m - 1 + FREE))
                nc.vector.tensor_reduce(neg_max[:, m % 2], partial_max[:, m % 2, :, 0:m % NC + 1],
                                        AX.X, ALU.max, negate=True).then_inc(max_combined, 1)

            def split_max(base, m, use):
                dve.wait_ge(misc_ready, base * MISC_BODY + (use + 1))
                dve.wait_ge(shift_in[m % 2], base * (32 * NC) + 32 * (m // 2))
                nc.vector.tensor_copy(max_high[:, m % 2], misc[0:HG * TT, 0:P]).then_inc(high_done, 1)
                dve.wait_ge(high_done, base * (2 * NC) + (m + 1))
                nc.vector.tensor_tensor(max_low[:, m % 2], misc[0:HG * TT, 0:P], max_high[:, m % 2].bitcast(F32),
                                        ALU.subtract).then_inc(max_split, 1)

            def divide(base, n, use):
                dve.wait_ge(misc_ready, base * MISC_BODY + (use + 1))
                turned = misc[:].rearrange("p (t j l) -> p t j l", t=TT, j=HG)
                nc.vector.reciprocal(recip[:], turned[:, :, :, HD]).then_inc(recip_done, 1)
                dve.wait_ge(recip_done, base * (2 * NC) + (n + 1))
                dve.wait_ge(y_out[n % 2], base * (16 * NC) + (16 * (n // 2) + FREE))
                nc.vector.tensor_tensor(y[:, n % 2], turned[:, :, :, 0:HD],
                                        recip[:].unsqueeze(3).broadcast_to([P, TT, HG, HD]), ALU.mult).then_inc(y_done, 1)

            for u in range(LEAD):
                reduce_unit(0, u)
                if u + 1 in MU_END:
                    m = MU_END.index(u + 1)
                    combine_max(0, m, u + 1)
                    split_max(0, m, m)
            with dve.Fori(0, ITS) as it:
                use = 0
                for k in range(NK):
                    for i in range(PER_STEP):
                        reduce_unit(it, LEAD + PER_STEP * k + i)
                    if k and maxima_ending(k - 1) is not None:
                        split_max(it, maxima_ending(k - 1), MISC_HEAD + use)
                        use += 1
                    if sums_at(k) is not None:
                        divide(it, sums_at(k), MISC_HEAD + use)
                        use += 1
                    if maxima_ending(k) is not None:
                        combine_max(it, maxima_ending(k), LEAD + PER_STEP * (k + 1))
                if maxima_ending(NK - 1) is not None:
                    split_max(it, maxima_ending(NK - 1), MISC_HEAD + use)
                    use += 1
                divide(it, 2 * NC - 1, MISC_HEAD + use)


EPS = 1e-5
SUBS = 2
DROPPED = 65536


def mix_and_route(nc, a, d, keep_on_chip, early):
    NCH = B * NC
    ROUND = 4
    BODIES = (NCH - 1) // ROUND
    gather_idx, kept, top_vals = keep_on_chip
    with ExitStack() as ctx:
        s = Scope(nc, ctx, "mix")
        sb, ps, sem = s.sb, s.ps, s.sem
        l2o = sb("l2o", [P, 64])
        kv2l = sb("kv2l", [P, 64])
        kv2l_b = sb("kv2l_b", [P, 1])
        l2o_b = sb("l2o_b", [64, 1])
        cproj = sb("cproj", [64, G, C])
        cproj_b = sb("cproj_b", [P, C])
        rw1 = sb("rw1", [P, KC, HID])
        rw1_high = sb("rw1_high", [P, KC, HID], F32R)
        rw1_low = sb("rw1_low", [P, KC, HID], F32R)
        rb1 = sb("rb1", [P, MC])
        rw2 = sb("rw2", [P, MC, L])
        rb2 = sb("rb2", [P, TT, E])
        ident = sb("ident", [P, P])
        fold8 = sb("fold8", [P, E])
        before_f = sb("before_f", [P, P])
        before = sb("before", [P, P], BF16)
        ones_b = sb("ones_b", [P, P], BF16)
        rev = sb("rev", [P, E])
        head_map = sb("head_map", [64, 64])
        bias_col = sb("bias_col", [64, P])
        ones = sb("ones", [64, P])
        w_out = sb("w_out", [P, KC, C])
        b_out = sb("b_out", [P, C])
        eps = sb("eps", [P, 1])
        zero_rows = sb("zero_rows", [P, 2048])
        yr = sb("yr", [P, SUBS, TT, C])
        yt = sb("yt", [P, KC, CH])
        xr = sb("xr", [P, SUBS, TT, C])
        xb = sb("xb", [P, SUBS, TT, C])
        z = sb("z", [P, SUBS, TT, C])
        x1 = sb("x1", [P, ROUND, TT, C])
        stats = sb("stats", [P, SUBS, TT, 6])
        moments = sb("moments", [P, SUBS, TT, 2])
        std = sb("std", [P, SUBS, TT])
        rstd = sb("rstd", [P, SUBS, TT])
        shift = sb("shift", [P, SUBS, TT])
        x1t_high = sb("x1t_high", [P, KC, CH], F32R)
        x1t_low = sb("x1t_low", [P, KC, CH], F32R)
        hid = sb("hid", [P, MC, CH])
        l2 = sb("l2", [P, CH])
        logits = sb("logits", [P, TT, E])
        rest = sb("rest", [P, TT, E])
        top = sb("top", [P, 2, TT])
        cand = sb("cand", [P, 2, TT, E])
        rank = sb("rank", [P, 2, TT])
        hot = sb("hot", [P, 2, TT, E])
        hot_b = sb("hot_b", [P, SUBS, TT, E], BF16)
        seen = sb("seen", [P, E])
        seen_add = sb("seen_add", [P, E])
        seen_b = sb("seen_b", [P, SUBS, E], BF16)
        at_pos = sb("at_pos", [P, 2, TT, E])
        pos = sb("pos", [P, 2 * TT])
        fits = sb("fits", [P, 2 * TT])
        slot = sb("slot", [P, 2 * TT])
        off = sb("off", [P, 2 * TT])
        clipped = sb("clipped", [P, 2 * TT])
        scatter_idx = sb("scatter_idx", [P, SUBS, 2 * TT], U32)
        mix_ps = [ps(f"mix{i}", [P, 2, C]) for i in range(2)]
        xt_ps = [ps(f"xt{i}", [P, CH]) for i in range(2)]
        hid_ps = [ps(f"hid{i}", [P, CH]) for i in range(2)]
        l2_ps = ps("l2", [P, CH])
        small = ps("small", [P, 2, TT, E])

        fold_in = sem("fold_in")
        consts_in = sem("consts_in")
        set_up = sem("set_up")
        folded = sem("folded")
        disp_zeroed = sem("disp_zeroed")
        chunk_in = [sem(f"chunk_in{i}") for i in range(SUBS)]
        biased = sem("biased")
        mixed = sem("mixed")
        z_done = sem("z_done")
        stats_done = sem("stats_done")
        moments_done = sem("moments_done")
        aggr_due = sem("aggr_due")
        std_done = sem("std_done")
        rstd_done = sem("rstd_done")
        norm_ready = sem("norm_ready")
        x1_done = sem("x1_done")
        y_turned = sem("y_turned")
        x1_turned = sem("x1_turned")
        high_done = sem("high_done")
        rw1_split = sem("rw1_split")
        turned_copied = sem("turned_copied")
        x1t_split = sem("x1t_split")
        hid_ready = sem("hid_ready")
        hid_done = sem("hid_done")
        l2_ready = sem("l2_ready")
        l2_copied = sem("l2_copied")
        logits_ready = sem("logits_ready")
        step_done = sem("step_done")
        hot_done = sem("hot_done")
        pos_ready = sem("pos_ready")
        pos_read = sem("pos_read")
        slots_done = sem("slots_done")
        scatter_due = sem("scatter_due")
        scattered = [sem(f"scattered{i}") for i in range(ROUND)]
        rows_free = sem("rows_free")
        x1_out = [sem(f"x1_out{i}") for i in range(ROUND)]
        for free in (z_done, turned_copied, l2_copied, pos_read, *x1_out, hid_ready, logits_ready, x1_done,
                     hid_done, mixed, x1t_split):
            nc.sync.sem_inc(free, FREE)
        nc.sync.sem_inc(rows_free, ROUND)
        block = ctx.enter_context(nc.Block())

        loads = [
            (l2o[:], a["l2o"]), (kv2l[:], a["kv2l"]), (kv2l_b[:], a["kv2l_b"]), (l2o_b[:], a["l2o_b"]),
            (cproj[:], a["cproj_t"].rearrange("(g r) n -> r g n", r=64)), (cproj_b[:], a["cproj_b"]),
            (rw1[:], a["rw1"].rearrange("(k p) n -> p k n", p=P)), (rb1[:], a["rb1"]),
            (rw2[:, :, 0:E], a["rw2"].rearrange("(m p) n -> p m n", p=P)), (rb2[:], a["rb2"]), (ident[:], a["ident"]),
            (fold8[:], a["fold8"]), (before_f[:], a["before"]), (rev[:], a["rev"]),
        ]
        FOLD_LOADS = 6
        SET_UP = 7
        FOLDED = 8
        disp_rows = d["disp"].rearrange("(i p r) c -> i p (r c)", p=P, r=8)
        x_src = a["x"].rearrange("(i t p) c -> i p t c", p=P, t=TT)

        def after(c, k):
            return c[0], c[1] + k

        def count(c, per, plus=0, bufs=1):
            body, r = c
            return body * (ROUND // bufs * per) + (r // bufs * per + plus)

        def run_steps(engine, step):
            step((0, 0))
            with engine.Fori(0, BODIES) as it:
                for r in range(1, ROUND + 1):
                    step((it, r))
            for c in range(BODIES * ROUND + 1, NCH):
                step((0, c))

        def is_first(c):
            return isinstance(c[0], int) and c[1] == 0

        def is_last(c, ahead):
            return isinstance(c[0], int) and c[1] + ahead >= NCH

        @block.sync
        def _(sp):
            def load(chunk, buf):
                sp.dma_start(yr[:, buf], d["y"].rearrange("b c p t n -> (b c) p t n")[chunk]).then_inc(chunk_in[buf], 16)
                sp.dma_start(xr[:, buf], x_src[chunk]).then_inc(chunk_in[buf], 16)

            def store(c, chunk):
                sp.wait_ge(x1_done, count(c, TT, TT + FREE))
                buf = c[1] % ROUND
                sp.dma_start(d["x1"][chunk], x1[:, buf].rearrange("p t c -> p (t c)")).then_inc(x1_out[buf], 16)

            for dst, src in loads[:FOLD_LOADS]:
                sp.dma_start(dst, src).then_inc(fold_in, 16)
            load(0, 0)
            for dst, src in loads[FOLD_LOADS:]:
                sp.dma_start(dst, src).then_inc(consts_in, 16)
            load(1, 1)
            sp.wait_ge(set_up, SET_UP)
            for i in range(E):
                sp.dma_start(disp_rows[i], zero_rows[:]).then_inc(disp_zeroed, 16)
            sp.wait_ge(y_turned, KC)
            sp.wait_ge(biased, 1)
            load(2, 0)
            store((0, 0), 0)
            early.load_first(sp)

            def step(c):
                chunk = {k: c[0] * ROUND + (c[1] + k) for k in (1, 3)}
                if not isinstance(c[0], int):
                    chunk = {k: sp.snap(v) for k, v in chunk.items()}
                if not is_last(c, 3):
                    sp.wait_ge(y_turned, count(c, KC, 2 * KC))
                    sp.wait_ge(biased, count(c, 1, 2))
                    load(chunk[3], (c[1] + 3) % SUBS)
                if not is_last(c, 1):
                    store(after(c, 1), chunk[1])
                if not is_first(c):
                    done = after(c, -1)
                    sp.wait_ge(scattered[done[1] % ROUND], count(done, 16 * 2 * TT, 16 * 2 * TT, bufs=ROUND))
                    sp.sem_inc(rows_free, 1)

            run_steps(sp, step)
            for i in range(ROUND):
                sp.wait_ge(x1_out[i], 16 * NCH // ROUND + FREE)

        @block.gpsimd
        def _(pool):
            pool.memset(eps[:], EPS).then_inc(set_up, 1)
            pool.memset(ones[:], 1.0).then_inc(set_up, 1)
            pool.memset(seen[:], 0.0).then_inc(set_up, 1)
            pool.memset(seen_b[:], 0.0).then_inc(set_up, 1)
            pool.memset(zero_rows[:], 0.0).then_inc(set_up, 1)
            pool.memset(ones_b[:], 1.0).then_inc(set_up, 1)
            pool.wait_ge(folded, FOLDED - 2)
            last_slot = pool.to_reg(E * CAP - 1)

            def bias(c):
                sub = c[1] % SUBS
                pool.wait_ge(chunk_in[sub], count(c, 32, 32, bufs=SUBS))
                if c[1] >= SUBS:
                    pool.wait_ge(z_done, count(c, 2, 2 - 2 * SUBS + FREE))
                nc.gpsimd.tensor_tensor(xb[:, sub], xr[:, sub], b_out[:].unsqueeze(1).broadcast_to([P, TT, C]),
                                        ALU.add).then_inc(biased, 1)

            def scatter(c):
                pool.wait_ge(slots_done, count(c, 1, 1))
                pool.sem_inc(scatter_due, 1)
                pool.wait_ge(disp_zeroed, 16 * E)
                for kt in range(2 * TT):
                    pool.indirect_dma_start(
                        d["disp"], bass.IndirectOffsetOnAxis(ap=scatter_idx[:, c[1] % SUBS, kt:kt + 1], axis=0),
                        x1[:, c[1] % ROUND, kt % TT, :], None, bounds_check=last_slot, oob_is_err=False,
                    ).then_inc(scattered[c[1] % ROUND], 16)

            def step(c):
                if not is_first(c):
                    scatter(after(c, -1))
                if not is_last(c, 2):
                    bias(after(c, 2))

            bias((0, 0))
            bias((0, 1))
            run_steps(pool, step)
            scatter((0, NCH - 1))
            for i in range(ROUND):
                pool.wait_ge(scattered[i], 16 * 2 * TT * NCH // ROUND)

        @block.tensor
        def _(pe):
            pe.wait_ge(fold_in, 16 * FOLD_LOADS)
            pe.wait_ge(set_up, SET_UP)
            nc.tensor.matmul(mix_ps[0][0:64, 0, 0:64], l2o[:], kv2l[:], start=True, stop=True)
            nc.tensor.matmul(mix_ps[0][0:64, 0, 64:65], l2o[:], kv2l_b[:], start=True, stop=True).then_inc(folded, 1)
            pe.wait_ge(folded, 3)
            for g in range(G):
                half = 64 * (g % 2)
                nc.tensor.matmul(mix_ps[1][half:half + 64, g // 2, :], head_map[:], cproj[:, g], start=True, stop=True)
            for g in range(G):
                last = nc.tensor.matmul(xt_ps[0][:, 0:C], bias_col[:], cproj[:, g], start=(g == 0), stop=(g == G - 1))
            last.then_inc(folded, 1)
            pe.wait_ge(folded, FOLDED)
            pe.wait_ge(consts_in, 16 * (len(loads) - FOLD_LOADS))

            def turn(source, wait_free, turned):
                for k in range(KC):
                    wait_free(k)
                    for t in range(TT):
                        last = nc.tensor.transpose(xt_ps[k][:, t * P:(t + 1) * P], source(t)[:, k * P:(k + 1) * P], ident[:])
                    last.then_inc(turned, 1)

            def turn_x1(c):
                pe.wait_ge(x1_done, count(c, TT, TT + FREE))
                turn(lambda t: x1[:, c[1] % ROUND, t], lambda k:
                     pe.wait_ge(x1t_split, count(c, KC, k + 1 - KC + FREE)) if is_last(c, 1) else
                     pe.wait_ge(turned_copied, count(c, KC, KC + k + 1 + FREE)), x1_turned)

            def turn_y(c):
                pe.wait_ge(chunk_in[c[1] % SUBS], count(c, 32, 32, bufs=SUBS))
                turn(lambda t: yr[:, c[1] % SUBS, t], lambda k: None if is_first(c) else
                     pe.wait_ge(x1t_split, count(c, KC, k + 1 - 2 * KC + FREE)) if c[1] >= 2 else
                     pe.wait_ge(turned_copied, k + 1 + FREE), y_turned)

            def mix(c):
                pe.wait_ge(turned_copied, count(c, KC, KC + FREE))
                for i in range(2):
                    if not is_first(c):
                        pe.wait_ge(z_done, count(c, 2, i - 1 + FREE))
                    for t in range(2):
                        for k in range(KC):
                            last = nc.tensor.matmul(mix_ps[i][:, t, :], yt[:, k, (2 * i + t) * P:(2 * i + t + 1) * P],
                                                    w_out[:, k], start=(k == 0), stop=(k == KC - 1))
                    last.then_inc(mixed, 1)

            def router(c, m):
                if m == 0:
                    pe.wait_ge(x1t_split, count(c, 2, 2 + FREE))
                if not is_first(c) or m >= 2:
                    pe.wait_ge(hid_done, count(c, MC, m - 1 + FREE))
                terms = [(w, x, k) for k in range(KC) for w, x in ((rw1_high, x1t_high), (rw1_high, x1t_low), (rw1_low, x1t_high))]
                for i, (w, x, k) in enumerate(terms):
                    last = nc.tensor.matmul(hid_ps[m % 2][:], w[:, k, m * P:(m + 1) * P], x[:, k, :],
                                            start=(i == 0), stop=(i == len(terms) - 1))
                last.then_inc(hid_ready, 1)

            def second_layer(c):
                pe.wait_ge(hid_done, count(c, MC, MC + FREE))
                pe.wait_ge(l2_copied, count(c, 1, FREE))
                for m in range(MC):
                    j = m % HG
                    last = nc.tensor.matmul(l2_ps[j * L:(j + 1) * L, :], rw2[:, m, :], hid[:, m, :],
                                            start=(m < HG), stop=(m >= HG), skip_group_check=True)
                last.then_inc(l2_ready, 1)

            def logits_of(c):
                pe.wait_ge(l2_copied, count(c, 1, 1 + FREE))
                pe.wait_ge(pos_read, count(c, 1, FREE))
                for t in range(TT):
                    last = nc.tensor.matmul(small[:, 0, t, :], l2[:, t * P:(t + 1) * P], fold8[:], start=True, stop=True)
                last.then_inc(logits_ready, 1)

            def positions(c):
                pe.wait_ge(hot_done, count(c, 1, 1))
                for t in range(TT):
                    nc.tensor.matmul(small[:, 1, t, :], before[:], hot_b[:, c[1] % SUBS, t, :], start=True, stop=False)
                    for t0 in range(t):
                        nc.tensor.matmul(small[:, 1, t, :], ones_b[:], hot_b[:, c[1] % SUBS, t0, :], start=False, stop=False)
                    last = nc.tensor.matmul(small[:, 1, t, :], ones_b[:], seen_b[:, c[1] % SUBS, :], start=False, stop=True)
                last.then_inc(pos_ready, 1)

            def step(c):
                turn_x1(c)
                if not is_first(c):
                    logits_of(after(c, -1))
                if not is_last(c, 1):
                    mix(after(c, 1))
                for m in range(MC):
                    router(c, m)
                    if m == 3 and not is_first(c):
                        positions(after(c, -1))
                if not is_last(c, 2):
                    turn_y(after(c, 2))
                second_layer(c)

            turn_y((0, 0))
            mix((0, 0))
            turn_y((0, 1))
            run_steps(pe, step)
            logits_of((0, NCH - 1))
            positions((0, NCH - 1))

        @block.scalar
        def _(act):
            act.wait_ge(set_up, SET_UP)
            act.wait_ge(consts_in, 16 * (len(loads) - FOLD_LOADS))
            nc.scalar.activation(rw1_high[:], rw1[:], ACT.Copy).then_inc(rw1_split, 1)

            def deviation(c):
                act.wait_ge(moments_done, count(c, TT, TT))
                nc.scalar.activation(std[:, c[1] % SUBS], moments[:, c[1] % SUBS, :, 1], ACT.Sqrt,
                                     bias=eps[:]).then_inc(std_done, 1)

            def norm(c, tiles):
                sub, buf = c[1] % SUBS, c[1] % ROUND
                act.wait_ge(norm_ready, count(c, 1, 1))
                act.wait_ge(rows_free, count(c, 1, 1))
                act.wait_ge(x1_out[buf], count(c, 16, FREE, bufs=ROUND))
                for t in tiles:
                    nc.scalar.activation(x1[:, buf, t], z[:, sub, t], ACT.Identity, bias=shift[:, sub, t:t + 1],
                                         scale=rstd[:, sub, t:t + 1]).then_inc(x1_done, 1)

            def copy_y(c):
                for k in range(KC):
                    act.wait_ge(y_turned, count(c, KC, k + 1))
                    if not is_first(c):
                        act.wait_ge(mixed, count(c, 2, FREE))
                    nc.scalar.activation(yt[:, k], xt_ps[k][:], ACT.Copy).then_inc(turned_copied, 1)

            def step(c):
                ahead = not is_last(c, 1)
                for k in range(KC):
                    act.wait_ge(x1_turned, count(c, KC, k + 1))
                    act.wait_ge(hid_ready, count(c, MC, FREE))
                    nc.scalar.activation(x1t_high[:, k], xt_ps[k][:], ACT.Copy).then_inc(high_done, 1)
                for m in range(MC):
                    act.wait_ge(hid_ready, count(c, MC, m + 1 + FREE))
                    nc.scalar.activation(hid[:, m], hid_ps[m % 2][:], ACT.Relu, bias=rb1[:, m:m + 1]).then_inc(hid_done, 1)
                    if m == 4 and ahead:
                        deviation(after(c, 1))
                    if m >= 5 and ahead:
                        norm(after(c, 1), range(m - 5, TT if m == MC - 1 else m - 4))
                if not is_last(c, 2):
                    copy_y(after(c, 2))
                act.wait_ge(l2_ready, count(c, 1, 1))
                act.wait_ge(logits_ready, count(c, 1, FREE))
                nc.scalar.activation(l2[:], l2_ps[:], ACT.Copy).then_inc(l2_copied, 1)

            copy_y((0, 0))
            copy_y((0, 1))
            deviation((0, 0))
            norm((0, 0), range(TT))
            run_steps(act, step)

        @block.vector
        def _(dve):
            nc.vector.memset(rw2[:, :, E:L], 0.0).then_inc(set_up, 1)
            dve.wait_ge(set_up, SET_UP)
            dve.wait_ge(fold_in, 16 * FOLD_LOADS)
            dve.wait_ge(folded, 1)
            nc.vector.tensor_copy(head_map[:], mix_ps[0][0:64, 0, 0:64]).then_inc(folded, 1)
            nc.vector.tensor_scalar(bias_col[:], ones[:], mix_ps[0][0:64, 0, 64:65], l2o_b[:], ALU.mult, ALU.add).then_inc(folded, 1)
            dve.wait_ge(folded, 4)
            nc.vector.tensor_copy(w_out[:], mix_ps[1][:]).then_inc(folded, 1)
            nc.vector.tensor_tensor(b_out[:], xt_ps[0][:, 0:C], cproj_b[:], ALU.add).then_inc(folded, 1)
            dve.wait_ge(consts_in, 16 * (len(loads) - FOLD_LOADS))
            nc.vector.tensor_copy(before[:], before_f[:]).then_inc(folded, 1)
            dve.wait_ge(rw1_split, 1)
            nc.vector.tensor_tensor(rw1_low[:], rw1[:], rw1_high[:].bitcast(F32), ALU.subtract).then_inc(folded, 1)

            def split_x1(c):
                for k in range(KC):
                    dve.wait_ge(high_done, count(c, KC, k + 1))
                    nc.vector.tensor_tensor(x1t_low[:, k], xt_ps[k][:], x1t_high[:, k].bitcast(F32),
                                            ALU.subtract).then_inc(x1t_split, 1)

            def moments_of(c):
                sub = c[1] % SUBS
                for i in range(2):
                    dve.wait_ge(mixed, count(c, 2, i + 1 + FREE))
                    dve.wait_ge(biased, count(c, 1, 1))
                    if c[1] >= SUBS:
                        dve.wait_ge(x1_done, count(c, TT, TT - TT * SUBS + FREE))
                    nc.vector.tensor_tensor(z[:, sub, 2 * i:2 * i + 2], mix_ps[i][:], xb[:, sub, 2 * i:2 * i + 2],
                                            ALU.add).then_inc(z_done, 1)
                for t in range(TT):
                    if t % 2 == 0:
                        dve.wait_ge(z_done, count(c, 2, t // 2 + 1 + FREE))
                    nc.vector.bn_stats(stats[:, sub, t], z[:, sub, t]).then_inc(stats_done, 1)
                for t in range(TT):
                    dve.wait_ge(stats_done, count(c, TT, t + 1))
                    dve.sem_inc(aggr_due, 1)
                    nc.vector.bn_aggr(moments[:, sub, t], stats[:, sub, t]).then_inc(moments_done, 1)
                dve.wait_ge(std_done, count(c, 1, 1))
                nc.vector.reciprocal(rstd[:, sub], std[:, sub]).then_inc(rstd_done, 1)
                dve.wait_ge(rstd_done, count(c, 1, 1))
                nc.vector.scalar_tensor_tensor(shift[:, sub], moments[:, sub, :, 0], -1.0, rstd[:, sub],
                                               ALU.mult, ALU.mult).then_inc(norm_ready, 1)

            STEPS = 22

            def chained(c, first, steps):
                for i, issue in enumerate(steps):
                    issue().then_inc(step_done, 1)
                    dve.wait_ge(step_done, count(c, STEPS, first + i + 1))
                return len(steps)

            rev_b = rev[:].unsqueeze(1).broadcast_to([P, TT, E])

            def wide(ap):
                return ap.unsqueeze(2).broadcast_to([P, TT, E])

            def choose(c):
                dve.wait_ge(logits_ready, count(c, 1, 1 + FREE))
                v = nc.vector
                sub, ci = c[1] % SUBS, c[0] * ROUND + c[1]
                n = chained(c, 0, [lambda: v.tensor_tensor(logits[:], small[:, 0], rb2[:], ALU.add)])
                for k, vals in enumerate((logits, rest)):
                    n += chained(c, n, [
                        lambda: v.tensor_reduce(top[:, k], vals[:], AX.X, ALU.max),
                        lambda: v.tensor_tensor(cand[:, k], vals[:], wide(top[:, k]), ALU.is_equal),
                        lambda: v.tensor_tensor(cand[:, k], cand[:, k], rev_b, ALU.mult),
                        lambda: v.tensor_reduce(rank[:, k], cand[:, k], AX.X, ALU.max),
                        lambda: v.tensor_tensor(hot[:, k], wide(rank[:, k]), rev_b, ALU.is_equal),
                    ])
                    if k == 0:
                        n += chained(c, n, [
                            lambda: v.scalar_tensor_tensor(rest[:], hot[:, 0], -3.0e38, logits[:], ALU.mult, ALU.add)])
                n += chained(c, n, [
                    lambda: v.tensor_copy(seen_b[:, sub], seen[:]),
                    lambda: v.tensor_copy(top_vals[:, ci], top[:].rearrange("p k t -> p (k t)"))])
                nc.vector.tensor_tensor(hot_b[:, sub], hot[:, 0], hot[:, 1], ALU.add).then_inc(hot_done, 1)
                dve.wait_ge(hot_done, count(c, 1, 1))
                n += chained(c, n, [
                    lambda: v.tensor_reduce(seen_add[:], hot_b[:, sub].rearrange("p t e -> p e t"), AX.X, ALU.add),
                    lambda: v.tensor_tensor(seen[:], seen[:], seen_add[:], ALU.add)])
                return n

            def place(c, n):
                v = nc.vector
                sub, ci = c[1] % SUBS, c[0] * ROUND + c[1]
                for k in range(2):
                    dve.wait_ge(pos_ready, count(c, 1, 1))
                    last = v.tensor_tensor(at_pos[:, k], hot[:, k], small[:, 1], ALU.mult)
                last.then_inc(pos_read, 1)
                dve.wait_ge(pos_read, count(c, 1, 1 + FREE))
                flat = rank[:].rearrange("p k t -> p (k t)")
                n += chained(c, n, [
                    lambda: v.tensor_reduce(pos[:], at_pos[:].rearrange("p k t e -> p (k t) e"), AX.X, ALU.add),
                    lambda: v.tensor_scalar(fits[:], pos[:], float(CAP), None, ALU.is_lt),
                    lambda: v.tensor_scalar(off[:], fits[:], -float(DROPPED), float(DROPPED + E * CAP), ALU.mult, ALU.add),
                    lambda: v.scalar_tensor_tensor(slot[:], flat, -float(CAP), pos[:], ALU.mult, ALU.add)])
                dve.wait_ge(rows_free, count(c, 1, ROUND - 1))
                n += chained(c, n, [
                    lambda: v.tensor_tensor(scatter_idx[:, sub], slot[:], off[:], ALU.add),
                    lambda: v.tensor_scalar(clipped[:], pos[:], float(CAP - 1), float(E * CAP), ALU.min, ALU.add)])
                v.tensor_copy(kept[:, ci], fits[:])
                v.scalar_tensor_tensor(gather_idx[:, ci], flat, -float(CAP), clipped[:], ALU.mult, ALU.add).then_inc(slots_done, 1)
                assert n == STEPS, n

            def step(c):
                split_x1(c)
                if not is_first(c):
                    n = choose(after(c, -1))
                if not is_last(c, 1):
                    moments_of(after(c, 1))
                if not is_first(c):
                    place(after(c, -1), n)

            moments_of((0, 0))
            run_steps(dve, step)
            place((0, NCH - 1), choose((0, NCH - 1)))


class ExpertOperands:

    def __init__(self, nc, ctx, a):
        s = Scope(nc, ctx, "exp")
        self.a = a
        self.ident = s.sb("ident", [P, P])
        self.w1 = s.sb("w1", [P, SUBS, KC, HID])
        self.w2 = s.sb("w2", [P, SUBS, MC, C])
        self.b1 = s.sb("b1", [P, SUBS, MC])
        self.b2 = s.sb("b2", [P, SUBS, C])
        self.ident_in = s.sem("ident_in")
        self.w_in = [s.sem(f"w_in{i}") for i in range(SUBS)]
        self.b_in = [s.sem(f"b_in{i}") for i in range(SUBS)]

    def load_weights(self, sp, e, sub):
        for dst, src in ((self.w1[:, sub], self.a["ew1"][e].rearrange("(k p) n -> p k n", p=P)),
                         (self.w2[:, sub], self.a["ew2"][e].rearrange("(m p) n -> p m n", p=P))):
            sp.dma_start(dst, src).then_inc(self.w_in[sub], 16)

    def load_biases(self, sp, e, sub):
        for dst, src in ((self.b1[:, sub], self.a["eb1"][e]), (self.b2[:, sub], self.a["eb2"][e])):
            sp.dma_start(dst, src).then_inc(self.b_in[sub], 16)

    def load_first(self, sp):
        sp.dma_start(self.ident[:], self.a["ident"]).then_inc(self.ident_in, 16)
        for sub in range(SUBS):
            self.load_weights(sp, sub, sub)
            self.load_biases(sp, sub, sub)


def experts(nc, a, d, early):
    ITS = E // SUBS
    HALVES = SUBS * CAP // CH
    with ExitStack() as ctx:
        s = Scope(nc, ctx, "exp")
        sb, ps, sem = s.sb, s.ps, s.sem
        ident, w1, w2, b1, b2 = early.ident, early.w1, early.w2, early.b1, early.b2
        ident_in, w_in, b_in = early.ident_in, early.w_in, early.b_in
        rows = sb("rows", [P, HALVES, TT, C])
        w1_high = sb("w1_high", [P, SUBS, KC, HID], F32R)
        w1_low = sb("w1_low", [P, SUBS, KC, HID], F32R)
        w2_high = sb("w2_high", [P, SUBS, MC, C], F32R)
        w2_low = sb("w2_low", [P, SUBS, MC, C], F32R)
        rows_high = sb("rows_high", [P, 2, KC, CH], F32R)
        rows_low = sb("rows_low", [P, 2, KC, CH], F32R)
        hid = sb("hid", [P, 2, CH])
        hid_high = sb("hid_high", [P, MC, CH], F32R)
        hid_low = sb("hid_low", [P, MC, CH], F32R)
        eo = sb("eo", [P, 2, TT, C])
        xt_ps = [ps(f"xt{i}", [P, CH]) for i in range(KC)]
        hid_ps = [ps(f"hid{i}", [P, CH]) for i in range(4)]
        eo_ps = [ps(f"eo{i}", [P, 2, C]) for i in range(2)]

        rows_in = [sem(f"rows_in{i}") for i in range(HALVES)]
        turned = sem("turned")
        weights_high = sem("weights_high")
        weights_split = sem("weights_split")
        rows_high_done = sem("rows_high_done")
        turned_copied = sem("turned_copied")
        hid_high_done = sem("hid_high_done")
        hid_ready = sem("hid_ready")
        hid_done = sem("hid_done")
        eo_ready = sem("eo_ready")
        eo_done = sem("eo_done")
        eo_out = [sem(f"eo_out{i}") for i in range(2)]
        for free in (turned_copied, eo_done, eo_ready, hid_ready, hid_done, *eo_out):
            nc.sync.sem_inc(free, FREE)
        block = ctx.enter_context(nc.Block())

        rows_src = d["disp"].rearrange("(h t p) c -> h p t c", p=P, t=TT)
        eo_dst = d["eo"].rearrange("(h t p) c -> h p t c", p=P, t=TT)

        def run_bodies(engine, body):
            with engine.Fori(0, ITS - 1) as it:
                body(it, False)
            body(ITS - 1, True)

        @block.sync
        def _(sp):
            def load_rows(h, q):
                sp.dma_start(rows[:, q], rows_src[h]).then_inc(rows_in[q], 16)

            for q in range(HALVES):
                load_rows(q, q)

            def body(it, half, ahead, expert_ahead):
                for q in range(HALVES):
                    if ahead is not None and q % 2 == 0:
                        sp.wait_ge(weights_split, it * (2 * SUBS) + (q + 2))
                        early.load_weights(sp, expert_ahead[q // 2], q // 2)
                    if ahead is not None:
                        sp.wait_ge(turned, it * (KC * HALVES) + KC * (q + 1))
                        load_rows(ahead[q], q)
                    sp.wait_ge(eo_done, it * (2 * HALVES) + (2 * (q + 1) + FREE))
                    sp.dma_start(eo_dst[half[q]], eo[:, q % 2]).then_inc(eo_out[q % 2], 16)
                    if ahead is not None and q % 2:
                        early.load_biases(sp, expert_ahead[q // 2], q // 2)

            with sp.Fori(0, ITS - 1) as it:
                body(it, [sp.snap(it * HALVES + q) for q in range(HALVES)],
                     [sp.snap(it * HALVES + (HALVES + q)) for q in range(HALVES)],
                     [sp.snap(it * SUBS + (SUBS + i)) for i in range(SUBS)])
            body(ITS - 1, [(ITS - 1) * HALVES + q for q in range(HALVES)], None, None)
            for i in range(2):
                sp.wait_ge(eo_out[i], 16 * ITS * HALVES // 2 + FREE)

        @block.tensor
        def _(pe):
            pe.wait_ge(ident_in, 16)

            def turn(it, q):
                pe.wait_ge(rows_in[q % HALVES], it * 16 + 16 * (q // HALVES + 1))
                for k in range(KC):
                    pe.wait_ge(turned_copied, it * (KC * HALVES) + ((KC * q + max(k - 1, 0) if q or k else 0) + FREE))
                    for t in range(TT):
                        last = nc.tensor.transpose(xt_ps[k][:, t * P:(t + 1) * P], rows[:, q % HALVES, t, k * P:(k + 1) * P], ident[:])
                    last.then_inc(turned, 1)

            def first(it, q):
                sub = q // 2
                if q % 2 == 0:
                    pe.wait_ge(weights_split, it * (2 * SUBS) + 2 * (sub + 1))
                pe.wait_ge(turned_copied, it * (KC * HALVES) + (KC * (q + 1) + FREE))
                terms = [(w, x, k) for k in range(KC)
                         for w, x in ((w1_high, rows_high), (w1_high, rows_low), (w1_low, rows_high))]
                for m in range(MC):
                    if q or m >= 4:
                        pe.wait_ge(hid_done, it * (MC * HALVES) + (MC * q + m - 3 + FREE))
                    for i, (w, x, k) in enumerate(terms):
                        last = nc.tensor.matmul(hid_ps[m % 4][:], w[:, sub, k, m * P:(m + 1) * P], x[:, q % 2, k],
                                                start=(i == 0), stop=(i == len(terms) - 1))
                    last.then_inc(hid_ready, 1)

            def second(it, q):
                sub = q // 2
                terms = [(x, w, m) for m in range(MC)
                         for x, w in ((hid_high, w2_high), (hid_high, w2_low), (hid_low, w2_high))]
                pe.wait_ge(hid_done, it * (MC * HALVES) + (MC * (q + 1) + FREE))
                for i in range(2):
                    pe.wait_ge(eo_done, it * (2 * HALVES) + ((max(2 * q + i - 1, 0)) + FREE))
                    for t in range(2):
                        for n, (x, w, m) in enumerate(terms):
                            last = nc.tensor.matmul(eo_ps[i][:, t, :], x[:, m, (2 * i + t) * P:(2 * i + t + 1) * P],
                                                    w[:, sub, m], start=(n == 0), stop=(n == len(terms) - 1))
                    last.then_inc(eo_ready, 1)

            def body(it, last):
                for q in range(HALVES):
                    first(it, q)
                    if not last or q + 1 < HALVES:
                        turn(it, q + 1)
                    second(it, q)

            turn(0, 0)
            run_bodies(pe, body)

        @block.scalar
        def _(act):
            def high_weights(it, sub):
                sub, turns = sub % SUBS, sub // SUBS
                act.wait_ge(w_in[sub], it * 32 + 32 * (turns + 1))
                act.wait_ge(eo_ready, it * (2 * HALVES) + (max(4 * (sub + SUBS * turns) - 4, 0) + FREE))
                nc.scalar.activation(w1_high[:, sub], w1[:, sub], ACT.Copy).then_inc(weights_high, 1)
                nc.scalar.activation(w2_high[:, sub], w2[:, sub], ACT.Copy).then_inc(weights_high, 1)

            def rows_of(it, q):
                for k in range(KC):
                    act.wait_ge(turned, it * (KC * HALVES) + (KC * q + k + 1))
                    act.wait_ge(hid_ready, it * (MC * HALVES) + (max(MC * (q - 1), 0) + FREE))
                    nc.scalar.activation(rows_high[:, q % 2, k], xt_ps[k][:], ACT.Copy).then_inc(rows_high_done, 1)

            def body(it, last):
                for q in range(HALVES):
                    if q % 2 == 0:
                        act.wait_ge(b_in[q // 2], it * 32 + 32)
                    for m in range(MC):
                        act.wait_ge(hid_ready, it * (MC * HALVES) + (MC * q + m + 1 + FREE))
                        nc.scalar.activation(hid_high[:, m], hid_ps[m % 4][:], ACT.Relu, bias=b1[:, q // 2, m:m + 1])
                        act.wait_ge(hid_done, it * (MC * HALVES) + (max(MC * q + m - 1, 0) + FREE))
                        nc.scalar.activation(hid[:, m % 2], hid_ps[m % 4][:], ACT.Relu,
                                             bias=b1[:, q // 2, m:m + 1]).then_inc(hid_high_done, 1)
                    if not last or q + 1 < HALVES:
                        rows_of(it, q + 1)
                    if q % 2 == 0 and not (last and q):
                        high_weights(it, q // 2 + 1)

            high_weights(0, 0)
            rows_of(0, 0)
            run_bodies(act, body)

        @block.vector
        def _(dve):
            def low_weights(it, sub):
                for i, (w, high, low) in enumerate(((w1, w1_high, w1_low), (w2, w2_high, w2_low))):
                    dve.wait_ge(weights_high, it * (2 * SUBS) + (2 * sub + i + 1))
                    nc.vector.tensor_tensor(low[:, sub % SUBS], w[:, sub % SUBS], high[:, sub % SUBS].bitcast(F32),
                                            ALU.subtract).then_inc(weights_split, 1)

            def rows_of(it, q):
                for k in range(KC):
                    dve.wait_ge(rows_high_done, it * (KC * HALVES) + (KC * q + k + 1))
                    nc.vector.tensor_tensor(rows_low[:, q % 2, k], xt_ps[k][:], rows_high[:, q % 2, k].bitcast(F32),
                                            ALU.subtract).then_inc(turned_copied, 1)

            def add_bias(it, q):
                dve.wait_ge(eo_out[q % 2], it * (16 * HALVES // 2) + (16 * (q // 2) + FREE))
                if q % 2 == 0:
                    dve.wait_ge(b_in[q // 2], it * 32 + 32)
                for i in range(2):
                    dve.wait_ge(eo_ready, it * (2 * HALVES) + (2 * q + i + 1 + FREE))
                    nc.vector.tensor_tensor(eo[:, q % 2, 2 * i:2 * i + 2], eo_ps[i][:],
                                            b2[:, q // 2].unsqueeze(1).broadcast_to([P, 2, C]), ALU.add).then_inc(eo_done, 1)

            def body(it, last):
                for q in range(HALVES):
                    for m in range(MC):
                        dve.wait_ge(hid_high_done, it * (MC * HALVES) + (MC * q + m + 1))
                        nc.vector.tensor_tensor(hid_low[:, m], hid[:, m % 2], hid_high[:, m].bitcast(F32),
                                                ALU.subtract).then_inc(hid_done, 1)
                    if not last or q + 1 < HALVES:
                        rows_of(it, q + 1)
                    if q % 2 == 0 and not (last and q):
                        low_weights(it, q // 2 + 1)
                    add_bias(it, q)

            low_weights(0, 0)
            rows_of(0, 0)
            run_bodies(dve, body)


def combine(nc, a, d, keep_on_chip, out):
    NCH = B * NC
    ITS = NCH // SUBS
    gather_idx, kept, top_vals = keep_on_chip
    with ExitStack() as ctx:
        s = Scope(nc, ctx, "fin")
        sb, sem = s.sb, s.sem
        gap = sb("gap", [P, NCH, TT])
        ratio = sb("ratio", [P, NCH, TT])
        total = sb("total", [P, NCH, TT])
        inv = sb("inv", [P, NCH, TT])
        weight = sb("weight", [P, NCH, 2 * TT])
        w_here = sb("w_here", [P, SUBS, 2 * TT])
        eps = sb("eps", [P, 1])
        x1 = sb("x1", [P, SUBS, TT, C])
        eo = sb("eo", [P, SUBS, 2 * TT, C])
        half_z = sb("half_z", [P, SUBS, TT, C])
        z = sb("z", [P, SUBS, TT, C])
        stats = sb("stats", [P, SUBS, TT, 6])
        moments = sb("moments", [P, SUBS, TT, 2])
        std = sb("std", [P, SUBS, TT])
        rstd = sb("rstd", [P, SUBS, TT])
        shift = sb("shift", [P, SUBS, TT])
        result = sb("result", [P, SUBS, TT, C])

        set_up = sem("set_up")
        gap_done = sem("gap_done")
        ratio_done = sem("ratio_done")
        weights = sem("weights")
        x1_in = [sem(f"x1_in{i}") for i in range(SUBS)]
        gathered = [sem(f"gathered{i}") for i in range(SUBS)]
        w_copied = sem("w_copied")
        half_done = sem("half_done")
        z_done = sem("z_done")
        stats_done = sem("stats_done")
        moments_done = sem("moments_done")
        aggr_due = sem("aggr_due")
        std_done = sem("std_done")
        rstd_done = sem("rstd_done")
        norm_ready = sem("norm_ready")
        result_done = sem("result_done")
        stored = [sem(f"stored{i}") for i in range(SUBS)]
        for free in (*stored, result_done):
            nc.sync.sem_inc(free, FREE)
        block = ctx.enter_context(nc.Block())

        out_dst = out.rearrange("b (i t p) c -> (b i) p t c", p=P, t=TT)

        @block.gpsimd
        def _(pool):
            pool.memset(eps[:], EPS).then_inc(set_up, 1)
            for ci in range(NCH):
                if ci >= SUBS:
                    pool.wait_ge(z_done, TT * (ci - 1))
                for kt in range(2 * TT):
                    pool.indirect_dma_start(
                        eo[:, ci % SUBS, kt, :], None, d["eo"],
                        bass.IndirectOffsetOnAxis(ap=gather_idx[:, ci, kt:kt + 1], axis=0),
                    ).then_inc(gathered[ci % SUBS], 16)

        @block.sync
        def _(sp):
            def load(ci, sub):
                sp.dma_start(x1[:, sub].rearrange("p t c -> p (t c)"), d["x1"][ci]).then_inc(x1_in[sub], 16)

            def body(it, ci, ahead):
                for sub in range(SUBS):
                    if ahead is not None:
                        sp.wait_ge(half_done, it * (SUBS * TT) + TT * (sub + 1))
                        load(ahead[sub], sub)
                    sp.wait_ge(result_done, it * (SUBS * TT) + (TT * (sub + 1) + FREE))
                    sp.dma_start(out_dst[ci[sub]], result[:, sub]).then_inc(stored[sub], 16)

            for sub in range(SUBS):
                load(sub, sub)
            with sp.Fori(0, ITS - 1) as it:
                body(it, [sp.snap(it * SUBS + i) for i in range(SUBS)], [sp.snap(it * SUBS + (SUBS + i)) for i in range(SUBS)])
            body(ITS - 1, [(ITS - 1) * SUBS + i for i in range(SUBS)], None)
            for i in range(SUBS):
                sp.wait_ge(stored[i], 16 * ITS + FREE)

        @block.scalar
        def _(act):
            act.wait_ge(gap_done, 1)
            nc.scalar.activation(ratio[:], gap[:], ACT.Exp).then_inc(ratio_done, 1)
            act.wait_ge(set_up, 1)
            with act.Fori(0, ITS) as it:
                for sub in range(SUBS):
                    act.wait_ge(moments_done, it * (SUBS * TT) + TT * (sub + 1))
                    nc.scalar.activation(std[:, sub], moments[:, sub, :, 1], ACT.Sqrt, bias=eps[:]).then_inc(std_done, 1)
                    act.wait_ge(norm_ready, it * SUBS + (sub + 1))
                    act.wait_ge(stored[sub], it * 16 + FREE)
                    for t in range(TT):
                        nc.scalar.activation(result[:, sub, t], z[:, sub, t], ACT.Identity, bias=shift[:, sub, t:t + 1],
                                             scale=rstd[:, sub, t:t + 1]).then_inc(result_done, 1)

        @block.vector
        def _(dve):
            first, second = top_vals[:, :, 0:TT], top_vals[:, :, TT:2 * TT]
            nc.vector.tensor_tensor(gap[:], second, first, ALU.subtract).then_inc(gap_done, 1)
            dve.wait_ge(ratio_done, 1)
            nc.vector.tensor_scalar(total[:], ratio[:], 1.0, None, ALU.add).then_inc(weights, 1)
            dve.wait_ge(weights, 1)
            nc.vector.reciprocal(inv[:], total[:]).then_inc(weights, 1)
            dve.wait_ge(weights, 2)
            nc.vector.tensor_tensor(ratio[:], ratio[:], inv[:], ALU.mult).then_inc(weights, 1)
            nc.vector.tensor_tensor(weight[:, :, 0:TT], inv[:], kept[:, :, 0:TT], ALU.mult).then_inc(weights, 1)
            dve.wait_ge(weights, 4)
            nc.vector.tensor_tensor(weight[:, :, TT:2 * TT], ratio[:], kept[:, :, TT:2 * TT], ALU.mult).then_inc(weights, 1)
            dve.wait_ge(weights, 5)
            with dve.Fori(0, ITS) as it:
                for sub in range(SUBS):
                    nc.vector.tensor_copy(w_here[:, sub], weight[:, it * SUBS + sub]).then_inc(w_copied, 1)
                    dve.wait_ge(w_copied, it * SUBS + (sub + 1))
                    dve.wait_ge(x1_in[sub], it * 16 + 16)
                    dve.wait_ge(gathered[sub], it * (16 * 2 * TT) + 16 * 2 * TT)
                    dve.wait_ge(result_done, it * (SUBS * TT) + FREE)
                    for t in range(TT):
                        nc.vector.scalar_tensor_tensor(half_z[:, sub, t], eo[:, sub, t], w_here[:, sub, t:t + 1], x1[:, sub, t],
                                                       ALU.mult, ALU.add).then_inc(half_done, 1)
                    for t in range(TT):
                        dve.wait_ge(half_done, it * (SUBS * TT) + (TT * sub + t + 1))
                        nc.vector.scalar_tensor_tensor(z[:, sub, t], eo[:, sub, TT + t], w_here[:, sub, TT + t:TT + t + 1],
                                                       half_z[:, sub, t], ALU.mult, ALU.add).then_inc(z_done, 1)
                    for t in range(TT):
                        dve.wait_ge(z_done, it * (SUBS * TT) + (TT * sub + t + 1))
                        nc.vector.bn_stats(stats[:, sub, t], z[:, sub, t]).then_inc(stats_done, 1)
                    for t in range(TT):
                        dve.wait_ge(stats_done, it * (SUBS * TT) + (TT * sub + t + 1))
                        dve.sem_inc(aggr_due, 1)
                        nc.vector.bn_aggr(moments[:, sub, t], stats[:, sub, t]).then_inc(moments_done, 1)
                    dve.wait_ge(std_done, it * SUBS + (sub + 1))
                    nc.vector.reciprocal(rstd[:, sub], std[:, sub]).then_inc(rstd_done, 1)
                    dve.wait_ge(rstd_done, it * SUBS + (sub + 1))
                    nc.vector.scalar_tensor_tensor(shift[:, sub], moments[:, sub, :, 0], -1.0, rstd[:, sub],
                                                   ALU.mult, ALU.mult).then_inc(norm_ready, 1)


def const_arrays():
    f = np.float32
    inv = (f(1.0) / np.power(f(10000.0), np.arange(0, L, 2, dtype=f) / f(L))).astype(f)
    angle = np.outer(np.arange(T, dtype=f), inv).astype(f)
    cos = np.tile(np.repeat(np.cos(angle), 2, axis=1).T, (HG, 1)).astype(f)
    sin = np.tile(np.repeat(np.sin(angle), 2, axis=1).T, (HG, 1)).astype(f)
    rot = np.zeros((2, P, P), f)
    even = np.arange(0, P, 2)
    rot[0, even, even + 1], rot[0, even + 1, even] = -1.0, 1.0
    rot[1, even + 1, even], rot[1, even, even + 1] = -1.0, 1.0
    row = np.arange(P)
    return {
        "cos": cos, "sin": sin, "rot": rot, "ident": np.eye(P, dtype=f),
        "rev": np.tile(E - np.arange(E, dtype=f), (P, 1)),
        "before": (row[:, None] < row[None, :]).astype(f),
        "fold8": ((row[:, None] % L) == np.arange(E)[None, :]).astype(f),
        "mask": np.where(row[None, :] > row[:, None], NEG, 0.0).astype(f),
    }


def laid_out(w):
    def blocks(m, n, dtype=np.float32):
        out = np.zeros((m.shape[0] * n, m.shape[1] * n), dtype)
        for i in range(n):
            out[i * m.shape[0]:(i + 1) * m.shape[0], i * m.shape[1]:(i + 1) * m.shape[1]] = m
        return out

    bias = w["L0_attn_c_attn_b"]
    return {
        "x_t": w["L0_attn_x"].reshape(N, C).T,
        "c_attn_w": w["L0_attn_c_attn_w"],
        "wv_t": w["L0_attn_c_attn_w"][2 * C:].T,
        "fold_q": blocks(w["L0_attn_q2l_w"].T, HG),
        "fold_k": blocks(w["L0_attn_kv2l_w"].T, HG),
        "b_cq": bias[0:C].reshape(G, HG * HD).T,
        "b_ck": bias[C:2 * C].reshape(G, HG * HD).T,
        "b_v": np.tile(bias[2 * C:], (P, 1)),
        "b_small": np.stack([np.tile(w[f"L0_attn_{n}_b"], HG) for n in ("q2l", "kv2l", "wqk")], axis=1),
        "wqk_t": blocks(w["L0_attn_wqk_w"].T, HG),
        "x": w["L0_attn_x"].reshape(N, C),
        "l2o": blocks(w["L0_attn_l2o_w"].T, HG),
        "kv2l": blocks(w["L0_attn_kv2l_w"], HG),
        "kv2l_b": np.tile(w["L0_attn_kv2l_b"], HG)[:, None],
        "l2o_b": np.tile(w["L0_attn_l2o_b"], HG)[:, None],
        "cproj_t": w["L0_attn_cproj_w"].T,
        "cproj_b": np.tile(w["L0_attn_cproj_b"], (P, 1)),
        "rw1": w["L0_ffn_rw1"], "rw2": w["L0_ffn_rw2"],
        "rb1": w["L0_ffn_rb1"].reshape(MC, P).T,
        "rb2": np.tile(w["L0_ffn_rb2"], (P, TT, 1)),
        "ew1": w["L0_ffn_ew1"], "ew2": w["L0_ffn_ew2"],
        "eb1": w["L0_ffn_eb1"].reshape(E, MC, P).transpose(0, 2, 1),
        "eb2": np.tile(w["L0_ffn_eb2"][:, None, :], (1, P, 1)),
    }


def program(nc, a, out):
    def scratch(name, shape, dt=F32):
        return nc.dram_tensor(name, shape, dt, kind="Internal").ap()

    d = {
        "qk": scratch("qk_parts", (SLOTS + 1, NC, 4, P, CH)),
        "v": scratch("v_tokens", (SLOTS + 1, NC, P, TT, HG * L)),
        "y": scratch("y_heads", (B, NC, P, TT, C)),
    }
    d |= {
        "x1": scratch("x1_rows", (B * NC, P, TT * C)),
        "disp": scratch("dispatched", (E * CAP, C)),
        "eo": scratch("expert_out", (E * CAP, C)),
    }
    with ExitStack() as ctx:
        keep = Scope(nc, ctx, "keep")
        keep_on_chip = (keep.sb("gather_idx", [P, B * NC, 2 * TT], U32), keep.sb("kept", [P, B * NC, 2 * TT]),
                        keep.sb("top_vals", [P, B * NC, 2 * TT]))
        project_heads(nc, a, d)
        attend(nc, a, d)
        with ExitStack() as expert_ctx:
            early = ExpertOperands(nc, expert_ctx, a)
            mix_and_route(nc, a, d, keep_on_chip, early)
            experts(nc, a, d, early)
        combine(nc, a, d, keep_on_chip, out)


def kernel(**inputs):
    import concourse.bacc as bacc
    from concourse.bass_utils import run_bass_kernel_spmd

    nc = bacc.Bacc("TRN2", target_bir_lowering=False, num_devices=1)
    arrays = {**laid_out({k: np.asarray(v) for k, v in inputs.items()}), **const_arrays()}
    arrays = {f"in_{n}": np.ascontiguousarray(v) for n, v in arrays.items()}
    a = {n[3:]: nc.dram_tensor(n, v.shape, mybir.dt.from_np(v.dtype), kind="ExternalInput").ap()
         for n, v in arrays.items()}
    out = nc.dram_tensor("out_0", (B, T, C), F32, kind="ExternalOutput").ap()
    program(nc, a, out)
    r = run_bass_kernel_spmd(nc, [arrays], core_ids=[0])
    return r.results[0]["out_0"]
```
